# Optimizing a Trainium2 kernel written in Bass

```python
import numpy as np
import jax
import jax.numpy as jnp

def _softmax(x, axis=-1):
    return jax.nn.softmax(x, axis=axis)

def _gelu(x):
    return jax.nn.gelu(x, approximate=True)

def _silu(x):
    return jax.nn.silu(x)

def _sigmoid(x):
    return jax.nn.sigmoid(x)

def _layernorm(x, axis=-1, eps=1e-05):
    m = jnp.mean(x, axis=axis, keepdims=True)
    v = jnp.var(x, axis=axis, keepdims=True)
    return (x - m) / jnp.sqrt(v + eps)

def _scatter_add(tgt, idx, src, axis=0):
    return tgt.at[idx].add(src)

def _segment_sum(src, seg, n):
    return jax.ops.segment_sum(src, seg, n)
kernel_name = 'mk_hybrid_d2_jaxref_r8_e7ee7b'

def setup_inputs(seed: int=0):
    np.random.seed(seed)
    _w = jnp.asarray

    def _L0_attn_a_setup():
        import jax, jax.numpy as jnp
        import numpy as np
        B, S, D = (2, 256, 512)
        NH, NKV = (32, 8)
        HD = D // NH
        NREP = NH // NKV
        SCALE = HD ** (-0.5)
        key = jax.random.key(seed)
        kx, kq, kk, kv, ko = jax.random.split(key, 5)
        s = 0.02
        return {'x': jax.random.normal(kx, (B, S, D), dtype=jnp.float32), 'wq': jax.random.normal(kq, (D, NH * HD), dtype=jnp.float32) * s, 'wk': jax.random.normal(kk, (D, NKV * HD), dtype=jnp.float32) * s, 'wv': jax.random.normal(kv, (D, NKV * HD), dtype=jnp.float32) * s, 'wo': jax.random.normal(ko, (NH * HD, D), dtype=jnp.float32) * s}
    _L0_attn_a_in = _L0_attn_a_setup()

    def _L0_attn_b_setup():
        import jax, jax.numpy as jnp
        import numpy as np
        H = 512
        D_IN = 1024
        N = 16
        K = 4
        R = 32
        EPS = 1e-06

        def rms_forward(x, eps=EPS):
            xf = x.astype(jnp.float32)
            var = jnp.mean(xf * xf, axis=-1, keepdims=True)
            return (xf * jax.lax.rsqrt(var + eps)).astype(x.dtype)
        key = jax.random.key(seed)
        ks = jax.random.split(key, 10)
        s = 0.02
        hidden_states = jax.random.normal(ks[0], (2, 128, H), dtype=jnp.float32)
        W_in = jax.random.normal(ks[1], (2 * D_IN, H), dtype=jnp.float32) * s
        conv_w = jax.random.normal(ks[2], (D_IN, K), dtype=jnp.float32) * 0.2
        conv_b = jax.random.normal(ks[3], (D_IN,), dtype=jnp.float32) * 0.02
        W_x = jax.random.normal(ks[4], (R + 2 * N, D_IN), dtype=jnp.float32) * s
        W_dt = jax.random.normal(ks[5], (D_IN, R), dtype=jnp.float32) * s
        b_dt = jax.random.normal(ks[6], (D_IN,), dtype=jnp.float32) * 0.02
        A_log = jnp.log(jnp.broadcast_to(jnp.arange(1, N + 1, dtype=jnp.float32)[None, :], (D_IN, N)))
        D = jnp.ones((D_IN,), dtype=jnp.float32)
        W_out = jax.random.normal(ks[7], (H, D_IN), dtype=jnp.float32) * s
        return {'hidden_states': hidden_states, 'W_in': W_in, 'conv_w': conv_w, 'conv_b': conv_b, 'W_x': W_x, 'W_dt': W_dt, 'b_dt': b_dt, 'A_log': A_log, 'D': D, 'W_out': W_out}
    _L0_attn_b_in = _L0_attn_b_setup()

    def _L0_ffn_setup():
        import jax, jax.numpy as jnp
        import numpy as np
        BATCH, TOK, DIM, OUT = (4, 256, 512, 512)
        E, R, TOP_K = (8, 16, 2)
        SCALING = 16.0 / R
        key = jax.random.key(seed)
        ks = jax.random.split(key, 6)
        return {'x': jax.random.normal(ks[0], (BATCH, TOK, DIM), dtype=jnp.float32), 'W_base': jax.random.normal(ks[1], (OUT, DIM), dtype=jnp.float32) / np.sqrt(DIM), 'b_base': jax.random.normal(ks[2], (OUT,), dtype=jnp.float32) * 0.01, 'W_gate': jax.random.normal(ks[3], (E, DIM), dtype=jnp.float32) * 0.01, 'A': jax.random.normal(ks[4], (E, R, DIM), dtype=jnp.float32) / np.sqrt(DIM), 'B': jax.random.normal(ks[5], (OUT, OUT // OUT * R * 0 + R), dtype=jnp.float32)[None].repeat(E, 0) * 0.0 + jax.random.normal(ks[5], (E, OUT, R), dtype=jnp.float32) * 0.02}
    _L0_ffn_in = _L0_ffn_setup()

    def _L1_attn_a_setup():
        import jax, jax.numpy as jnp
        import numpy as np
        DIM = 512
        N_HEADS = 32
        HEAD_DIM = DIM // N_HEADS
        key = jax.random.key(seed)
        k0, k1, k2, k3, k4 = jax.random.split(key, 5)
        B, T = (2, 256)
        x = jax.random.normal(k0, (B, T, DIM), dtype=jnp.float32)
        s = 1.0 / np.sqrt(DIM)
        wq = jax.random.normal(k1, (DIM, DIM), dtype=jnp.float32) * s
        wk = jax.random.normal(k2, (DIM, HEAD_DIM), dtype=jnp.float32) * s
        wv = jax.random.normal(k3, (DIM, HEAD_DIM), dtype=jnp.float32) * s
        wo = jax.random.normal(k4, (DIM, DIM), dtype=jnp.float32) * s
        return {'x': x, 'wq': wq, 'wk': wk, 'wv': wv, 'wo': wo}
    _L1_attn_a_in = _L1_attn_a_setup()

    def _L1_attn_b_setup():
        import jax, jax.numpy as jnp
        import numpy as np
        HIDDEN = 512
        NUM_HEADS = 32
        HEAD_DIM = HIDDEN // NUM_HEADS

        def _fp8_roundtrip(x):
            return x.astype(jnp.float8_e4m3fn).astype(jnp.float32)
        key = jax.random.key(seed)
        ks = jax.random.split(key, 10)
        B, S = (2, 512)
        hidden_states = jax.random.normal(ks[0], (B, S, HIDDEN), dtype=jnp.float32)
        scale = 0.02

        def lin(kw, kb):
            w = jax.random.normal(kw, (HIDDEN, HIDDEN), dtype=jnp.float32) * scale
            b = jax.random.normal(kb, (HIDDEN,), dtype=jnp.float32) * scale
            return (w, b)
        wq, bq = lin(ks[1], ks[2])
        wk, bk = lin(ks[3], ks[4])
        wv, bv = lin(ks[5], ks[6])
        wl, bl = lin(ks[7], ks[8])
        wq, bq = (_fp8_roundtrip(wq), _fp8_roundtrip(bq))
        wk, bk = (_fp8_roundtrip(wk), _fp8_roundtrip(bk))
        wv, bv = (_fp8_roundtrip(wv), _fp8_roundtrip(bv))
        return {'hidden_states': hidden_states, 'wq': wq, 'bq': bq, 'wk': wk, 'bk': bk, 'wv': wv, 'bv': bv, 'wl': wl, 'bl': bl}
    _L1_attn_b_in = _L1_attn_b_setup()

    def _L1_ffn_setup():
        import jax, jax.numpy as jnp
        import numpy as np
        BITS = 4
        GROUP_SIZE = 128
        IN_FEATURES = 512
        OUT_FEATURES = 512
        MAXQ = 2 ** BITS - 1
        PACK = 32 // BITS

        def _dequantize(qweight, qzeros, scales):
            shifts = jnp.arange(0, 32, BITS, dtype=jnp.int32)
            zeros = qzeros[:, :, None] >> shifts[None, None, :] & MAXQ
            zeros = zeros.reshape(scales.shape).astype(scales.dtype)
            w = qweight[:, None, :] >> shifts[None, :, None] & MAXQ
            w = w.reshape(-1, qweight.shape[-1]).astype(scales.dtype)
            scales_full = jnp.repeat(scales, GROUP_SIZE, axis=0)
            zeros_full = jnp.repeat(zeros, GROUP_SIZE, axis=0)
            return scales_full * (w - zeros_full)
        key = jax.random.key(seed)
        k = jax.random.split(key, 5)
        x = jax.random.normal(k[0], (8, 256, IN_FEATURES), dtype=jnp.float32)
        qweight = jax.random.randint(k[1], (IN_FEATURES // PACK, OUT_FEATURES), 0, 2 ** 31 - 1, dtype=jnp.int32)
        n_groups = IN_FEATURES // GROUP_SIZE
        qzeros = jax.random.randint(k[2], (n_groups, OUT_FEATURES // PACK), 0, 2 ** 31 - 1, dtype=jnp.int32)
        scales = jax.random.uniform(k[3], (n_groups, OUT_FEATURES), dtype=jnp.float32) * 0.01 + 0.001
        bias = jax.random.normal(k[4], (OUT_FEATURES,), dtype=jnp.float32) * 0.01
        return {'x': x, 'qweight': qweight, 'qzeros': qzeros, 'scales': scales, 'bias': bias}
    _L1_ffn_in = _L1_ffn_setup()
    _d = {'L0_attn_a_x': _L0_attn_a_in['x'], 'L0_attn_a_wq': _L0_attn_a_in['wq'], 'L0_attn_a_wk': _L0_attn_a_in['wk'], 'L0_attn_a_wv': _L0_attn_a_in['wv'], 'L0_attn_a_wo': _L0_attn_a_in['wo'], 'L0_attn_b_W_in': _L0_attn_b_in['W_in'], 'L0_attn_b_conv_w': _L0_attn_b_in['conv_w'], 'L0_attn_b_conv_b': _L0_attn_b_in['conv_b'], 'L0_attn_b_W_x': _L0_attn_b_in['W_x'], 'L0_attn_b_W_dt': _L0_attn_b_in['W_dt'], 'L0_attn_b_b_dt': _L0_attn_b_in['b_dt'], 'L0_attn_b_A_log': _L0_attn_b_in['A_log'], 'L0_attn_b_D': _L0_attn_b_in['D'], 'L0_attn_b_W_out': _L0_attn_b_in['W_out'], 'L0_ffn_W_base': _L0_ffn_in['W_base'], 'L0_ffn_b_base': _L0_ffn_in['b_base'], 'L0_ffn_W_gate': _L0_ffn_in['W_gate'], 'L0_ffn_A': _L0_ffn_in['A'], 'L0_ffn_B': _L0_ffn_in['B'], 'L1_attn_a_wq': _L1_attn_a_in['wq'], 'L1_attn_a_wk': _L1_attn_a_in['wk'], 'L1_attn_a_wv': _L1_attn_a_in['wv'], 'L1_attn_a_wo': _L1_attn_a_in['wo'], 'L1_attn_b_wq': _L1_attn_b_in['wq'], 'L1_attn_b_bq': _L1_attn_b_in['bq'], 'L1_attn_b_wk': _L1_attn_b_in['wk'], 'L1_attn_b_bk': _L1_attn_b_in['bk'], 'L1_attn_b_wv': _L1_attn_b_in['wv'], 'L1_attn_b_bv': _L1_attn_b_in['bv'], 'L1_attn_b_wl': _L1_attn_b_in['wl'], 'L1_attn_b_bl': _L1_attn_b_in['bl'], 'L1_ffn_qweight': _L1_ffn_in['qweight'], 'L1_ffn_qzeros': _L1_ffn_in['qzeros'], 'L1_ffn_scales': _L1_ffn_in['scales'], 'L1_ffn_bias': _L1_ffn_in['bias']}
    _x0 = _d['L0_attn_a_x']
    _d['L0_attn_a_x'] = jax.random.normal(jax.random.fold_in(jax.random.key(seed), 1), (2, 512, 512), dtype=_x0.dtype)
    del _x0
    return _d

def reference(L0_attn_a_x, L0_attn_a_wq, L0_attn_a_wk, L0_attn_a_wv, L0_attn_a_wo, L0_attn_b_W_in, L0_attn_b_conv_w, L0_attn_b_conv_b, L0_attn_b_W_x, L0_attn_b_W_dt, L0_attn_b_b_dt, L0_attn_b_A_log, L0_attn_b_D, L0_attn_b_W_out, L0_ffn_W_base, L0_ffn_b_base, L0_ffn_W_gate, L0_ffn_A, L0_ffn_B, L1_attn_a_wq, L1_attn_a_wk, L1_attn_a_wv, L1_attn_a_wo, L1_attn_b_wq, L1_attn_b_bq, L1_attn_b_wk, L1_attn_b_bk, L1_attn_b_wv, L1_attn_b_bv, L1_attn_b_wl, L1_attn_b_bl, L1_ffn_qweight, L1_ffn_qzeros, L1_ffn_scales, L1_ffn_bias):

    def _L0_attn_a_ref(x, wq, wk, wv, wo):
        import jax, jax.numpy as jnp
        import numpy as np
        B, S, D = (2, 256, 512)
        NH, NKV = (32, 8)
        HD = D // NH
        NREP = NH // NKV
        SCALE = HD ** (-0.5)
        b, s, _ = x.shape
        q = (x @ wq).reshape(b, s, NH, HD)
        k = (x @ wk).reshape(b, s, NKV, HD)
        v = (x @ wv).reshape(b, s, NKV, HD)
        k = jnp.repeat(k, NREP, axis=2)
        v = jnp.repeat(v, NREP, axis=2)
        scores = jnp.einsum('bihd,bjhd->bhij', q, k) * SCALE
        causal = jnp.tril(jnp.ones((s, s), dtype=bool))
        scores = jnp.where(causal, scores, jnp.finfo(scores.dtype).min)
        attn = jax.nn.softmax(scores, axis=-1)
        out = jnp.einsum('bhij,bjhd->bihd', attn, v)
        out = out.reshape(b, s, NH * HD)
        return out @ wo

    def _L0_attn_b_ref(hidden_states, W_in, conv_w, conv_b, W_x, W_dt, b_dt, A_log, D, W_out):
        import jax, jax.numpy as jnp
        import numpy as np
        H = 512
        D_IN = 1024
        N = 16
        K = 4
        R = 32
        EPS = 1e-06

        def rms_forward(x, eps=EPS):
            xf = x.astype(jnp.float32)
            var = jnp.mean(xf * xf, axis=-1, keepdims=True)
            return (xf * jax.lax.rsqrt(var + eps)).astype(x.dtype)
        b, L, _ = hidden_states.shape
        proj = hidden_states @ W_in.T
        x, gate = (proj[..., :D_IN], proj[..., D_IN:])
        xpad = jnp.pad(x, ((0, 0), (K - 1, 0), (0, 0)))
        xc = conv_b
        for j in range(K):
            xc = xc + conv_w[:, j] * xpad[:, j:j + L, :]
        x = jax.nn.silu(xc)
        ssm = x @ W_x.T
        ts, Bm, Cm = (ssm[..., :R], ssm[..., R:R + N], ssm[..., R + N:])
        ts = rms_forward(ts)
        Bm = rms_forward(Bm)
        Cm = rms_forward(Cm)
        dt = jax.nn.softplus(ts @ W_dt.T + b_dt)
        A = -jnp.exp(A_log.astype(jnp.float32))

        def step(state, inp):
            dt_t, B_t, C_t, u_t = inp
            dA = jnp.exp(dt_t[..., None] * A)
            state = state * dA + (dt_t * u_t)[..., None] * B_t[:, None, :]
            y = jnp.einsum('bdn,bn->bd', state, C_t)
            return (state, y)
        init = jnp.zeros((b, D_IN, N), dtype=jnp.float32)
        xs = (dt.transpose(1, 0, 2), Bm.transpose(1, 0, 2), Cm.transpose(1, 0, 2), x.transpose(1, 0, 2))
        _, ys = jax.lax.scan(step, init, xs)
        y = ys.transpose(1, 0, 2) + x * D
        y = y * jax.nn.silu(gate)
        return y @ W_out.T

    def _L0_ffn_ref(x, W_base, b_base, W_gate, A, B):
        import jax, jax.numpy as jnp
        import numpy as np
        BATCH, TOK, DIM, OUT = (4, 256, 512, 512)
        E, R, TOP_K = (8, 16, 2)
        SCALING = 16.0 / R
        result = jnp.einsum('bnd,od->bno', x, W_base) + b_base
        logits = jnp.einsum('bnd,ed->bne', x, W_gate)
        probs = jax.nn.softmax(logits.astype(jnp.float32), axis=-1)
        top_p, top_i = jax.lax.top_k(probs, TOP_K)
        top_p = top_p / jnp.sum(top_p, axis=-1, keepdims=True)
        top_p = top_p.astype(x.dtype)
        route_w = jnp.sum(jax.nn.one_hot(top_i, E, dtype=x.dtype) * top_p[..., None], axis=-2)
        h = jnp.einsum('bnd,erd->bner', x, A)
        hw = h * route_w[..., None]
        delta = jnp.einsum('bner,eor->bno', hw, B)
        return result + delta * SCALING

    def _L1_attn_a_ref(x, wq, wk, wv, wo):
        import jax, jax.numpy as jnp
        import numpy as np
        DIM = 512
        N_HEADS = 32
        HEAD_DIM = DIM // N_HEADS
        B, T, C = x.shape
        q = (x @ wq).reshape(B, T, N_HEADS, HEAD_DIM)
        k = x @ wk
        v = x @ wv
        scale = 1.0 / jnp.sqrt(jnp.asarray(HEAD_DIM, dtype=x.dtype))
        scores = jnp.einsum('bqhd,bkd->bhqk', q, k) * scale
        causal = jnp.tril(jnp.ones((T, T), dtype=bool))
        scores = jnp.where(causal[None, None], scores, -jnp.inf)
        probs = jax.nn.softmax(scores.astype(jnp.float32), axis=-1).astype(x.dtype)
        out = jnp.einsum('bhqk,bkd->bqhd', probs, v).reshape(B, T, C)
        return out @ wo

    def _L1_attn_b_ref(hidden_states, wq, bq, wk, bk, wv, bv, wl, bl):
        import jax, jax.numpy as jnp
        import numpy as np
        HIDDEN = 512
        NUM_HEADS = 32
        HEAD_DIM = HIDDEN // NUM_HEADS

        def _fp8_roundtrip(x):
            return x.astype(jnp.float8_e4m3fn).astype(jnp.float32)
        B, S, E = hidden_states.shape
        H, D = (NUM_HEADS, HEAD_DIM)
        q = (hidden_states @ wq.T + bq).reshape(B, S, H, D)
        k = (hidden_states @ wk.T + bk).reshape(B, S, H, D)
        v = (hidden_states @ wv.T + bv).reshape(B, S, H, D)
        latent = hidden_states @ wl.T + bl
        scores = jnp.einsum('bshd,bstd->bsht', q, k) / np.sqrt(D).astype(np.float32)
        probs = jax.nn.softmax(scores, axis=-1)
        context = jnp.einsum('bsht,bstd->bshd', probs, v).reshape(B, S, E)
        return context

    def _L1_ffn_ref(x, qweight, qzeros, scales, bias):
        import jax, jax.numpy as jnp
        import numpy as np
        BITS = 4
        GROUP_SIZE = 128
        IN_FEATURES = 512
        OUT_FEATURES = 512
        MAXQ = 2 ** BITS - 1
        PACK = 32 // BITS

        def _dequantize(qweight, qzeros, scales):
            shifts = jnp.arange(0, 32, BITS, dtype=jnp.int32)
            zeros = qzeros[:, :, None] >> shifts[None, None, :] & MAXQ
            zeros = zeros.reshape(scales.shape).astype(scales.dtype)
            w = qweight[:, None, :] >> shifts[None, :, None] & MAXQ
            w = w.reshape(-1, qweight.shape[-1]).astype(scales.dtype)
            scales_full = jnp.repeat(scales, GROUP_SIZE, axis=0)
            zeros_full = jnp.repeat(zeros, GROUP_SIZE, axis=0)
            return scales_full * (w - zeros_full)
        out_shape = x.shape[:-1] + (OUT_FEATURES,)
        x2d = x.reshape(-1, x.shape[-1])
        W = _dequantize(qweight, qzeros, scales)
        out = jnp.matmul(x2d, W) + bias
        return out.reshape(out_shape)
    x = L0_attn_a_x
    x = x + _L0_attn_a_ref(_layernorm(x, axis=-1), L0_attn_a_wq, L0_attn_a_wk, L0_attn_a_wv, L0_attn_a_wo)
    x = x + _L0_ffn_ref(_layernorm(x, axis=-1), L0_ffn_W_base, L0_ffn_b_base, L0_ffn_W_gate, L0_ffn_A, L0_ffn_B)
    x = x + _L0_attn_b_ref(_layernorm(x, axis=-1), L0_attn_b_W_in, L0_attn_b_conv_w, L0_attn_b_conv_b, L0_attn_b_W_x, L0_attn_b_W_dt, L0_attn_b_b_dt, L0_attn_b_A_log, L0_attn_b_D, L0_attn_b_W_out)
    x = x + _L0_ffn_ref(_layernorm(x, axis=-1), L0_ffn_W_base, L0_ffn_b_base, L0_ffn_W_gate, L0_ffn_A, L0_ffn_B)
    x = x + _L1_attn_a_ref(_layernorm(x, axis=-1), L1_attn_a_wq, L1_attn_a_wk, L1_attn_a_wv, L1_attn_a_wo)
    x = x + _L1_ffn_ref(_layernorm(x, axis=-1), L1_ffn_qweight, L1_ffn_qzeros, L1_ffn_scales, L1_ffn_bias)
    x = x + _L1_attn_b_ref(_layernorm(x, axis=-1), L1_attn_b_wq, L1_attn_b_bq, L1_attn_b_wk, L1_attn_b_bk, L1_attn_b_wv, L1_attn_b_bv, L1_attn_b_wl, L1_attn_b_bl)
    x = x + _L1_ffn_ref(_layernorm(x, axis=-1), L1_ffn_qweight, L1_ffn_qzeros, L1_ffn_scales, L1_ffn_bias)
    return x

_drawn_inputs = setup_inputs


def setup_inputs(seed=0):
    import zlib

    import numpy as np

    out = dict(_drawn_inputs(seed))
    spreads = {'L0_attn_b_D': (1.0, 0.6)}
    factors = {'L0_attn_a_wq': 8.0,
     'L0_attn_a_wk': 8.0,
     'L0_attn_b_conv_b': 8.0,
     'L0_attn_b_W_dt': 8.0,
     'L0_attn_b_b_dt': 64.0,
     'L0_attn_b_A_log': 64.0,
     'L0_ffn_b_base': 5.201,
     'L1_attn_b_wq': 8.0,
     'L1_attn_b_bq': 22.504,
     'L1_attn_b_wk': 8.0,
     'L1_attn_b_bk': 22.221,
     'L1_attn_b_bv': 8.0,
     'L1_ffn_bias': 8.0}
    for name, (base, spread) in spreads.items():
        noise = np.random.default_rng([zlib.crc32(name.encode()), seed]).standard_normal(out[name].shape)
        drawn = base * np.exp(spread * noise) if base else spread * noise
        out[name] = jnp.asarray(drawn.astype(out[name].dtype))
    for name, factor in factors.items():
        out[name] = (out[name] * factor).astype(out[name].dtype)
    return out
```

```python
import concourse.bass as bass
from concourse import mybir
from contextlib import ExitStack

F32 = mybir.dt.float32
BF16 = mybir.dt.bfloat16
I32 = mybir.dt.int32
ALU = mybir.AluOpType
ACT = mybir.ActivationFunctionType
AX = mybir.AxisListType

P = 128
BATCH, SEQ, DIM = 2, 512, 512
TOK = BATCH * SEQ
NT = TOK // P
NTB = NT // BATCH
KC = DIM // P
HEADS, HD = 32, 16
HPC = P // HD
D_IN, NSTATE, DT_RANK, CONV = 1024, 16, 32, 4
DTILES = D_IN // P
EXPERTS, LORA = 8, 16
ER = EXPERTS * LORA
FCAT = ER + EXPERTS
NEG = -1.0e30
SCALE = HD ** -0.5
LN_EPS, RMS_EPS = 1e-5, 1e-6


def hybrid_kernel(nc, x, a_wq, a_wk, a_wv, a_wo, m_win, m_convw, m_convb, m_wx, m_wdt, m_bdt, m_alog, m_d,
                  m_wout, f_wbase, f_cat, f_bias, f_bt, q_wq, q_wk, q_wv, q_wo, h_wq, h_wk, h_wv, h_bias,
                  g_qw, g_qz, g_sc, g_bias, out):
    ctx = ExitStack()
    with ctx:
        def sb(name, shape, dt=F32):
            return ctx.enter_context(nc.sbuf_tensor(name, shape, dt))

        def sem(name):
            return ctx.enter_context(nc.semaphore(name))

        X = sb("X", [P, NT, DIM])
        XT = sb("XT", [P, KC, TOK])
        Wg = sb("Wg", [P, KC, DIM])
        Wf = sb("Wf", [P, KC, DIM])
        Wcat = sb("Wcat", [P, KC, FCAT])
        Wbt = sb("Wbt", [P, DIM])
        bias_f = sb("bias_f", [P, DIM])
        bias_g = sb("bias_g", [P, DIM])
        ident = sb("ident", [P, P])
        identb = sb("identb", [P, P], BF16)
        mask_qk = sb("mask_qk", [P, P], BF16)
        mask_kq = sb("mask_kq", [P, P], BF16)
        bn = sb("bn", [P, NT, 6])
        mv = sb("mv", [P, NT, 2])
        rstd = sb("rstd", [P, NT, 1])
        minus_half = sb("minus_half", [P, NTB * 4])
        rank8 = sb("rank8", [P, EXPERTS])
        ARENA = 37888
        arena = sb("arena", [P, ARENA])

        def at(off, n, dt=F32):
            v = arena[:, off:off + n]
            return v if dt == F32 else v.bitcast(dt)

        XN = at(5120, 4096).rearrange("p (t c) -> p t c", t=NT)

        PS = ctx.enter_context(nc.psum_tensor("PS", [P, 8, 512], F32))

        ATTN_A, FFN_0, MAMBA, FFN_1, ATTN_M, QUANT_0, ATTN_H, QUANT_1 = range(8)

        x_loaded = [sem(f"x_loaded{b}") for b in range(BATCH)]
        ln_stat = sem("ln_stat")
        ln_rstd = sem("ln_rstd")
        xn_ready = sem("xn_ready")
        tr_done = sem("tr_done")
        xt_ready = sem("xt_ready")
        out_ps = sem("out_ps")
        x_done = sem("x_done")
        x_bias = sem("x_bias")
        dve_own, pool_own, act_own = sem("dve_own"), sem("pool_own"), sem("act_own")
        consts = sem("consts")
        w_ffn, w_quant, wg_ready = sem("w_ffn"), sem("w_quant"), sem("wg_ready")
        stored = sem("stored")

        LINEAR = {FFN_0: 0, FFN_1: 1, QUANT_0: 2, QUANT_1: 3}

        class Own:

            def __init__(self, eng, s):
                self.eng, self.s, self.n = eng, s, 0

            def done(self, ins):
                self.n += 1
                ins.then_inc(self.s, 1)
                self.eng.wait_ge(self.s, self.n)

        def ln_stats(dve, own, s, t):
            if s == 0:
                dve.wait_ge(x_loaded[t // NTB], 16)
            own.done(nc.vector.bn_stats(bn[:, t, :], X[:, t, :]))
            nc.vector.bn_aggr(mv[:, t, :], bn[:, t, :]).then_inc(ln_stat, 1)

        def ln_rstds(pool, own, s):
            for t in range(NT):
                pool.wait_ge(ln_stat, NT * s + t + 1)
                own.done(nc.gpsimd.tensor_scalar(rstd[:, t, :], mv[:, t, 1:2], LN_EPS, None, ALU.add))
                nc.gpsimd.tensor_tensor(rstd[:, t, :], rstd[:, t, :], minus_half[:, 0:1], ALU.pow).then_inc(ln_rstd, 1)

        def ln_apply(dve, s, t):
            dve.wait_ge(ln_rstd, NT * s + t + 1)
            nc.vector.tensor_scalar(XN[:, t, :], X[:, t, :], mv[:, t, 0:1], rstd[:, t, :],
                                    ALU.subtract, ALU.mult).then_inc(xn_ready, 1)

        def layer_norm(dve, own, s):
            for t in range(NT):
                ln_stats(dve, own, s, t)
                if t >= 1:
                    ln_apply(dve, s, t - 1)
            ln_apply(dve, s, NT - 1)

        def transposes(pe, s):
            if s == 0:
                pe.wait_ge(consts, CONSTS)
            for t in range(NT):
                pe.wait_ge(xn_ready, NT * s + t + 1)
                if t >= 2:
                    pe.wait_ge(xt_ready, NT * s + t - 1)
                for k in range(KC):
                    last = nc.tensor.transpose(PS[:, 6 + t % 2, k * P:k * P + P], XN[:, t, k * P:k * P + P], ident[:, :])
                last.then_inc(tr_done, 1)

        def xt_copies(act, s):
            for t in range(NT):
                act.wait_ge(tr_done, NT * s + t + 1)
                nc.scalar.copy(XT[:, :, t * P:t * P + P],
                               PS[:, 6 + t % 2, :].rearrange("p (k n) -> p k n", k=KC)).then_inc(xt_ready, 1)

        def add_bias(pool, s, bias, loaded, n):
            pool.wait_ge(loaded, n)
            for t in range(NT):
                pool.wait_ge(xn_ready, NT * s + t + 1)
                nc.gpsimd.tensor_tensor(X[:, t, :], X[:, t, :], bias[:, :], ALU.add).then_inc(x_bias, 1)

        KV = {ATTN_A: 8, ATTN_M: 1}
        DMA = 16
        att_names = ["prj_ps", "hi", "rest", "mid", "lo", "v_ps", "v_sb", "fill", "ring", "nm3", "st", "exp",
                     "pv", "o_sb", "norm"]
        am = {s: {n: sem(f"{n}{s}") for n in att_names} for s in KV}
        for s in KV:
            am[s].update(w=sem(f"at_w{s}"), ones=sem(f"ones{s}"), spl_out=[sem(f"spl_out{s}{i}") for i in range(2)],
                         back=[sem(f"back{s}{b}") for b in range(BATCH)], mt_in=[sem(f"mt_in{s}{i}") for i in range(2)],
                         o_in=[sem(f"o_in{s}{i}") for i in range(2)])
        split_q = {s: nc.dram_tensor(f"split_q{s}", [3, DIM, TOK], BF16, kind="Internal").ap() for s in KV}
        split_k = {s: nc.dram_tensor(f"split_k{s}", [3, KV[s] * HD, TOK], BF16, kind="Internal").ap() for s in KV}
        a_wo_sb = at(0, 2048).rearrange("p (k n) -> p k n", k=KC)
        a_wq_sb = at(2048, 2048).rearrange("p (k n) -> p k n", k=KC)
        a_wk_sb = at(4096, 512).rearrange("p (k n) -> p k n", k=KC)
        a_wv_sb = at(4608, 512).rearrange("p (k n) -> p k n", k=KC)
        o_raw = at(35840, 2048).rearrange("p (r n) -> p r n", r=4)
        den = at(2048, 1024).rearrange("p (r n) -> p r n", r=2)
        mt = at(3072, 512).bitcast(BF16).rearrange("p (r n) -> p r n", r=2)
        nmf = sb("nmf", [P, 4, 16])
        nmr = sb("nmr", [P, 4, 16])
        nm3 = sb("nm3", [P, 4, 3, 16], BF16)
        Q6 = at(5120, 16384).bitcast(BF16).rearrange("p (h n) -> p h n", h=HEADS)
        K6 = at(21504, 4096).bitcast(BF16).rearrange("p (g n) -> p g n", g=8)
        V = at(25600, 2048).rearrange("p (t g d) -> p t g d", t=NT, g=8)
        PT = at(27648, 4096).rearrange("p (r h n) -> p r h n", r=2, h=4)
        spl = at(27648, 1536).bitcast(BF16).rearrange("p (r k n) -> p r k n", r=2, k=3)
        rest = at(29184, 1024).rearrange("p (r n) -> p r n", r=2)
        OT = at(31744, 4096).rearrange("p (m n) -> p m n", m=KC)
        GH = 16
        GROUPS = BATCH * HEADS // GH
        FILLS = [(qt, h, n) for h4 in range(0, GH, 4) for qt, n in ((0, 4), (1, 2), (2, 1), (3, 1))
                 for h in range(h4, h4 + 4, n)]
        PROJ = [("k", 0, 0), ("k", 0, 1)] + [("q", m, b) for b in range(BATCH) for m in range(KC)]
        BACK = {ATTN_A: [6 + 6 * KC, 6 * KC], ATTN_M: [6 + 6 * KC, 6 * KC]}

        def attention_steps():
            steps = [("proj", i) for i in range(2 + KC)] + [("v", 0)]
            late = [("proj", 2 + KC + i) for i in range(KC)]
            for f in range(len(FILLS)):
                if f % 11 == 0:
                    steps.append(late.pop(0))
                steps.append(("fill", 0, f))
            steps.append(("nmt", 0))
            outs0 = [("out", t) for t in range(NTB)]
            per = GH // 4 * 8
            for g in range(GROUPS):
                f = 0
                for u in range(per):
                    steps.append(("st", g * per + u))
                    if u % 2 and g * per + u >= 3:
                        steps.append(("pv", (g * per + u - 3) // 2))
                        if (g * per + u - 3) // 2 % 8 == 1 and (g * per + u - 3) // 16 >= 1:
                            steps.append(("norm", (g * per + u - 3) // 16 - 1))
                    while g + 1 < GROUPS and f < len(FILLS) and f < 1.7 * (u + 1):
                        steps.append(("fill", g + 1, f))
                        f += 1
                    if g + 1 < GROUPS and u == 27:
                        steps.append(("nmt", g + 1))
                    if g == 2 and u % 4 == 0 and u >= 8 and outs0:
                        steps.append(outs0.pop(0))
            last = GROUPS * per // 2 - 1
            steps += [("pv", last), ("norm", last // 8)] + [("out", NTB + t) for t in range(NTB)]
            return steps

        STEPS = attention_steps()
        RING = [x for x in STEPS if x[0] in ("fill", "nmt", "out")]

        def ring_of(step):
            return RING.index(step)

        def attention_sp(sp, s):
            m, kv = am[s], KV[s]

            def send_back(i):
                kind, mm, b = PROJ[i]
                sp.wait_ge(m["spl_out"][i % 2], DMA * (i // 2 + 1))
                if kind == "k" and b == 0:
                    return
                if kind == "k":
                    src = split_k[s].rearrange("k (g d) n -> k d g n", d=HD)
                    for row, k in ((0, 0), (16, 1), (32, 2), (48, 0), (64, 1), (80, 0)):
                        sp.dma_start(K6[row:row + HD, 0:kv, :], src[k]).then_inc(m["back"][0], DMA)
                    return
                if i == 2:
                    sp.wait_ge(xt_ready, NT * s + NT)
                src = split_q[s][:, mm * P:mm * P + P, b * SEQ:b * SEQ + SEQ].rearrange("k (h d) n -> k d h n", d=HD)
                for row, k in ((0, 0), (16, 0), (32, 0), (48, 1), (64, 1), (80, 2)):
                    sp.dma_start(Q6[row:row + HD, HPC * mm:HPC * mm + HPC, b * SEQ:b * SEQ + SEQ],
                                 src[k]).then_inc(m["back"][b], DMA)

            for step in STEPS:
                if step[0] == "proj":
                    i = step[1]
                    kind, mm, b = PROJ[i]
                    rows = kv * HD if kind == "k" else P
                    dst = split_k[s] if kind == "k" else split_q[s][:, mm * P:mm * P + P, :]
                    sp.wait_ge(m["lo"], i + 1)
                    sp.dma_start(dst[:, :, b * SEQ:b * SEQ + SEQ].rearrange("k p n -> p k n"),
                                 spl[0:rows, i % 2, :, :]).then_inc(m["spl_out"][i % 2], DMA)
                    if i >= 1 and i != 2 + KC:
                        send_back(i - 1)
                    if i in (1 + KC, 1 + 2 * KC):
                        send_back(i)
                elif step[0] == "nmt":
                    g = step[1]
                    b, h0 = g * GH // HEADS, g * GH % HEADS
                    sp.wait_ge(m["ring"], ring_of(step) + 1)
                    for k in range(3):
                        sp.dma_start(Q6[96 + k:97 + k, h0:h0 + GH, b * SEQ:b * SEQ + SEQ],
                                     mt[GH * k:GH * k + GH, g % 2, :]).then_inc(m["mt_in"][g % 2], DMA)
                elif step[0] == "pv" and step[1] % 4 == 3:
                    i = step[1] // 4
                    b, hq = i // 8, i % 8
                    c = i // 2
                    sp.wait_ge(m["o_sb"], i + 1)
                    if c >= 2:
                        sp.wait_ge(m["norm"], c - 1)
                    for j in range(4):
                        r = hq % 2 * 64 + HD * j
                        sp.dma_start(OT[r:r + HD, hq // 2, b * SEQ:b * SEQ + SEQ],
                                     o_raw[32 * j:32 * j + HD, i % 4, :]).then_inc(m["o_in"][c % 2], DMA)
                        sp.dma_start(den[r:r + HD, c % 2, :],
                                     o_raw[32 * j + HD:32 * j + 2 * HD, i % 4, :]).then_inc(m["o_in"][c % 2], DMA)

        def attention_pe(pe, s):
            m, kv = am[s], KV[s]
            group = HEADS // kv
            pe.wait_ge(m["w"], 4 * DMA)
            pe.wait_ge(xt_ready, NT * s + NT)
            for step in STEPS:
                if step[0] == "proj":
                    i = step[1]
                    kind, mm, b = PROJ[i]
                    w = a_wk_sb[:, :, 0:kv * HD] if kind == "k" else a_wq_sb[:, :, mm * P:mm * P + P]
                    if i >= 4:
                        pe.wait_ge(m["rest"], i - 3)
                    for k in range(KC):
                        last = nc.tensor.matmul(PS[0:w.shape[2], 2 + i % 4, :], w[:, k, :], XT[:, k, b * SEQ:b * SEQ + SEQ],
                                                start=k == 0, stop=k == KC - 1)
                    last.then_inc(m["prj_ps"], 1)
                elif step[0] == "v":
                    for t in range(NT):
                        for k in range(KC):
                            last = nc.tensor.matmul(PS[:, 6 + t // 4, t % 4 * kv * HD:(t % 4 + 1) * kv * HD],
                                                    XT[:, k, t * P:t * P + P], a_wv_sb[:, k, 0:kv * HD],
                                                    start=k == 0, stop=k == KC - 1)
                        if t % 4 == 3:
                            last.then_inc(m["v_ps"], 1)
                elif step[0] == "fill":
                    g, f = step[1:]
                    b, h0 = g * GH // HEADS, g * GH % HEADS
                    a = ring_of(step)
                    if f == 0 and g in (0, GROUPS // 2):
                        pe.wait_ge(m["back"][b], DMA * BACK[s][b])
                    if a >= 2:
                        pe.wait_ge(m["ring"], a - 1)
                    qt, h, n = FILLS[f]
                    w = (qt + 1) * P
                    for e in range(n):
                        hh = h0 + h + e
                        o = PS[:, a % 2, e * w:e * w + w]
                        q0 = b * SEQ + qt * P
                        nc.tensor.matmul(o, Q6[0:96, hh, q0:q0 + P], K6[0:96, hh // group, b * SEQ:b * SEQ + w],
                                         start=True, stop=False)
                        last = nc.tensor.matmul(o[:, qt * P:w], identb[:, :], mask_qk[:, :], start=False, stop=True)
                    last.then_inc(m["fill"], 1)
                elif step[0] == "nmt":
                    g = step[1]
                    a = ring_of(step)
                    pe.wait_ge(m["ring"], a - 1)
                    pe.wait_ge(m["nm3"], g + 1)
                    o = PS[:, a % 2, :].bitcast(BF16)
                    for qt in range(4):
                        last = nc.tensor.transpose(o[0:48, qt * P:qt * P + P],
                                                   nm3[:, qt, :, :].rearrange("p k h -> p (k h)"), identb[:, :])
                    last.then_inc(m["fill"], 1)
                elif step[0] == "st":
                    u = step[1]
                    i, kt, pair = u // 8, u // 2 % 4, u % 2
                    b, hq = i // 8, i % 8
                    g = i // (GH // 4)
                    if u % (GH * 2) == 0:
                        pe.wait_ge(m["mt_in"][g % 2], DMA * 3 * (g // 2 + 1))
                    if u >= 2:
                        pe.wait_ge(m["exp"], u - 1)
                    k0, w = b * SEQ + kt * P, SEQ - kt * P
                    for e in range(2):
                        hh = 4 * hq + 2 * pair + e
                        o = PS[:, 2 + u % 2 * 2 + e, 0:w]
                        nc.tensor.matmul(o, K6[0:99, hh // group, k0:k0 + P], Q6[0:99, hh, k0:(b + 1) * SEQ],
                                         start=True, stop=False)
                        last = nc.tensor.matmul(o[:, 0:P], identb[:, :], mask_kq[:, :], start=False, stop=True)
                    last.then_inc(m["st"], 1)
                elif step[0] == "pv":
                    v = step[1]
                    i, kt = v // 4, v % 4
                    b, hq = i // 8, i % 8
                    pe.wait_ge(m["exp"], 2 * v + 2)
                    if v == 0:
                        pe.wait_ge(m["v_sb"], 2)
                        pe.wait_ge(m["ones"], 2)
                    if kt == 0 and i >= 2:
                        pe.wait_ge(m["o_sb"], i - 1)
                    w = SEQ - kt * P
                    for j in range(4):
                        hh = 4 * hq + j
                        last = nc.tensor.matmul(PS[32 * j:32 * j + 32, 6 + i % 2, kt * P:SEQ],
                                                V[:, b * NTB + kt, hh // group, :], PT[:, v % 2, j, 0:w],
                                                start=kt == 0, stop=kt == 3, tile_position=(0, 32 * j))
                    last.then_inc(m["pv"], 1)
                elif step[0] == "out":
                    t = step[1]
                    a = ring_of(step)
                    pe.wait_ge(m["ring"], a - 1)
                    pe.wait_ge(m["norm"], KC * (t // NTB + 1))
                    for k in range(KC):
                        last = nc.tensor.matmul(PS[:, a % 2, :], OT[:, k, t * P:t * P + P], a_wo_sb[:, k, :],
                                                start=k == 0, stop=k == KC - 1)
                    last.then_inc(m["fill"], 1)

        def attention_act(act, s):
            m, kv = am[s], KV[s]
            for step in STEPS:
                if step[0] == "proj":
                    i = step[1]
                    rows = kv * HD if PROJ[i][0] == "k" else P
                    act.wait_ge(m["prj_ps"], i + 1)
                    if i >= 2:
                        act.wait_ge(m["spl_out"][i % 2], DMA * (i // 2))
                    nc.scalar.copy(spl[0:rows, i % 2, 0, :], PS[0:rows, 2 + i % 4, :]).then_inc(m["hi"], 1)
                elif step[0] == "v":
                    for n in range(2):
                        act.wait_ge(m["v_ps"], n + 1)
                        src = PS[:, 6 + n, 0:4 * kv * HD].rearrange("p (t g d) -> p t g d", t=4, g=kv)
                        for t in range(4):
                            last = nc.scalar.copy(V[:, 4 * n + t, 0:kv, 0:HD], src[:, t, :, :])
                        last.then_inc(m["v_sb"], 1)
                elif step[0] == "st":
                    u = step[1]
                    kt, pair, v = u // 2 % 4, u % 2, u // 2
                    w = SEQ - kt * P
                    act.wait_ge(m["st"], u + 1)
                    if u == 0:
                        act.wait_ge(m["spl_out"][0], DMA * (len(PROJ) // 2))
                        act.wait_ge(m["spl_out"][1], DMA * (len(PROJ) // 2))
                    if v >= 2:
                        act.wait_ge(m["pv"], v - 1)
                    nc.scalar.activation(PT[:, v % 2, 2 * pair:2 * pair + 2, 0:w], PS[:, 2 + u % 2 * 2:4 + u % 2 * 2, 0:w],
                                         ACT.Exp, scale=SCALE).then_inc(m["exp"], 1)

        def attention_dve(dve, own, s):
            m, kv = am[s], KV[s]
            for step in STEPS:
                if step[0] == "proj":
                    i = step[1]
                    rows = kv * HD if PROJ[i][0] == "k" else P
                    dve.wait_ge(m["hi"], i + 1)
                    if i >= 2:
                        dve.wait_ge(m["lo"], i - 1)
                    nc.vector.tensor_tensor(rest[0:rows, i % 2, :], PS[0:rows, 2 + i % 4, :], spl[0:rows, i % 2, 0, :],
                                            ALU.subtract).then_inc(m["rest"], 1)
                elif step[0] == "fill":
                    g, f = step[1:]
                    a = ring_of(step)
                    qt, h, n = FILLS[f]
                    dve.wait_ge(m["fill"], a + 1)
                    red = nc.vector.tensor_reduce(nmf[:, qt, h:h + n],
                                                  PS[:, a % 2, 0:n * (qt + 1) * P].rearrange("p (h n) -> p h n", h=n),
                                                  AX.X, ALU.max, negate=True)
                    red.then_inc(m["ring"], 1)
                    if f == len(FILLS) - 1:
                        dve.wait_ge(m["ring"], a + 1)
                        if g >= 1:
                            dve.wait_ge(m["fill"], ring_of(("nmt", g - 1)) + 1)
                        own.done(nc.vector.tensor_copy(nm3[:, :, 0, :], nmf[:, :, :]))
                        own.done(nc.vector.tensor_tensor(nmr[:, :, :], nmf[:, :, :], nm3[:, :, 0, :], ALU.subtract))
                        own.done(nc.vector.tensor_copy(nm3[:, :, 1, :], nmr[:, :, :]))
                        nc.vector.tensor_tensor(nm3[:, :, 2, :], nmr[:, :, :], nm3[:, :, 1, :],
                                                ALU.subtract).then_inc(m["nm3"], 1)
                        dve.wait_ge(m["nm3"], g + 1)
                elif step[0] == "nmt":
                    g = step[1]
                    a = ring_of(step)
                    dve.wait_ge(m["fill"], a + 1)
                    if g == 0:
                        dve.wait_ge(m["rest"], len(PROJ))
                        dve.wait_ge(m["prj_ps"], len(PROJ))
                    if g >= 2:
                        dve.wait_ge(m["mt_in"][g % 2], DMA * 3 * (g // 2))
                    nc.vector.tensor_copy(mt[0:48, g % 2, :],
                                          PS[:, a % 2, :].bitcast(BF16)[0:48, 0:SEQ]).then_inc(m["ring"], 1)
                elif step[0] == "pv" and step[1] % 4 == 3:
                    i = step[1] // 4
                    dve.wait_ge(m["pv"], step[1] + 1)
                    nc.vector.tensor_copy(o_raw[:, i % 4, :], PS[:, 6 + i % 2, :]).then_inc(m["o_sb"], 1)
                elif step[0] == "norm":
                    c = step[1]
                    b, mm = c // KC, c % KC
                    dve.wait_ge(m["o_in"][c % 2], DMA * 16 * (c // 2 + 1))
                    own.done(nc.vector.reciprocal(den[:, c % 2, :], den[:, c % 2, :]))
                    o = OT[:, mm, b * SEQ:b * SEQ + SEQ]
                    nc.vector.tensor_tensor(o, o, den[:, c % 2, :], ALU.mult).then_inc(m["norm"], 1)
                elif step[0] == "out":
                    t = step[1]
                    a = ring_of(step)
                    dve.wait_ge(m["fill"], a + 1)
                    nc.vector.tensor_tensor(X[:, t, :], X[:, t, :], PS[:, a % 2, :], ALU.add).then_inc(m["ring"], 1)
                    dve.wait_ge(m["ring"], a + 1)

        def attention_pool(pool, s):
            m, kv = am[s], KV[s]
            if s != ATTN_A:
                pool.wait_ge(xn_ready, NT * s + NT)
            nc.gpsimd.memset(V[:, :, 0:kv, HD:2 * HD], 1.0).then_inc(m["ones"], 1)
            pool.wait_ge(m["ones"], 1)
            nc.gpsimd.memset(K6[96:99, 0:kv, :], 1.0).then_inc(m["ones"], 1)
            pool.wait_ge(m["ones"], 2)
            for i, (kind, mm, b) in enumerate(PROJ):
                rows = kv * HD if kind == "k" else P
                pool.wait_ge(m["rest"], i + 1)
                nc.gpsimd.tensor_copy(spl[0:rows, i % 2, 1, :], rest[0:rows, i % 2, :]).then_inc(m["mid"], 1)
                pool.wait_ge(m["mid"], i + 1)
                nc.gpsimd.tensor_tensor(spl[0:rows, i % 2, 2, :], rest[0:rows, i % 2, :], spl[0:rows, i % 2, 1, :],
                                        ALU.subtract).then_inc(m["lo"], 1)

        ffn_names = ["h_ps", "h_sb", "hw", "hwt_ps", "hwt_sb", "logit", "exp"]
        fm = {s: {n: sem(f"{n}{s}") for n in ffn_names} for s in (FFN_0, FFN_1)}
        Hcat = at(27648, NT * FCAT).rearrange("p (t n) -> p t n", t=NT)
        HW = at(28736, NT * ER).rearrange("p (t n) -> p t n", t=NT)
        HWT = at(29760, NT * P).rearrange("p (t n) -> p t n", t=NT)
        rt = [at(30784 + 64 * i, 64).rearrange("p (t e) -> p t e", t=NT) for i in range(8)]
        r1 = [at(31296 + 8 * i, 8) for i in range(6)]

        def ffn_pe(pe, s):
            m = fm[s]
            pe.wait_ge(w_ffn, 4 * DMA)
            for t in range(NT):
                pe.wait_ge(xt_ready, NT * s + t + 1)
                if t >= 2:
                    pe.wait_ge(m["h_sb"], t - 1)
                for k in range(KC):
                    last = nc.tensor.matmul(PS[:, t % 2, 0:FCAT], XT[:, k, t * P:t * P + P], Wcat[:, k, :],
                                            start=k == 0, stop=k == KC - 1)
                last.then_inc(m["h_ps"], 1)

            def base(t):
                if t >= 3:
                    pe.wait_ge(x_done, NT * LINEAR[s] + t - 2)
                for k in range(KC):
                    nc.tensor.matmul(PS[:, 2 + t % 3, :], XT[:, k, t * P:t * P + P], Wf[:, k, :], start=k == 0, stop=False)

            base(0)
            base(1)
            for t in range(NT):
                pe.wait_ge(m["hw"], t + 1)
                if t == 0:
                    pe.wait_ge(m["h_sb"], NT)
                if t >= 2:
                    pe.wait_ge(m["hwt_sb"], t - 1)
                nc.tensor.transpose(PS[:, t % 2, 0:P], HW[:, t, :], ident[:, :]).then_inc(m["hwt_ps"], 1)
                if t + 2 < NT:
                    base(t + 2)
                pe.wait_ge(m["hwt_sb"], t + 1)
                nc.tensor.matmul(PS[:, 2 + t % 3, :], HWT[:, t, :], Wbt[:, :], start=False, stop=True).then_inc(out_ps, 1)

        def ffn_act(act, s):
            m = fm[s]
            for t in range(NT):
                act.wait_ge(m["h_ps"], t + 1)
                nc.scalar.copy(Hcat[:, t, :], PS[:, t % 2, 0:FCAT]).then_inc(m["h_sb"], 1)
            act.wait_ge(m["logit"], 1)
            nc.scalar.activation(rt[1], rt[0], ACT.Exp).then_inc(m["exp"], 1)
            for t in range(NT):
                act.wait_ge(m["hwt_ps"], t + 1)
                nc.scalar.copy(HWT[:, t, :], PS[:, t % 2, 0:P]).then_inc(m["hwt_sb"], 1)

        def ffn_dve(dve, own, s):
            m = fm[s]
            bc = lambda v: v.unsqueeze(2).broadcast_to([P, NT, EXPERTS])
            dve.wait_ge(m["h_sb"], NT)
            logit, e, p, c1, oh1, p2, c2, oh2 = rt
            mx, sm, m1, k1, m2, k2 = r1
            TT, TR, TS = nc.vector.tensor_tensor, nc.vector.tensor_reduce, nc.vector.tensor_scalar
            rank = rank8[:, :].unsqueeze(1).broadcast_to([P, NT, EXPERTS])
            own.done(TR(mx, Hcat[:, :, ER:FCAT], AX.X, ALU.max))
            TT(logit, Hcat[:, :, ER:FCAT], bc(mx), ALU.subtract).then_inc(m["logit"], 1)
            dve.wait_ge(m["exp"], 1)
            own.done(TR(sm, e, AX.X, ALU.add))
            own.done(nc.vector.reciprocal(sm, sm))
            own.done(TT(p, e, bc(sm), ALU.mult))
            own.done(TR(m1, p, AX.X, ALU.max))
            own.done(TT(c1, p, bc(m1), ALU.is_equal))
            own.done(TT(c1, c1, rank, ALU.mult))
            own.done(TR(k1, c1, AX.X, ALU.max))
            own.done(TT(oh1, c1, bc(k1), ALU.is_equal))
            own.done(nc.vector.scalar_tensor_tensor(p2, oh1, -2.0, p, ALU.mult, ALU.add))
            own.done(TR(m2, p2, AX.X, ALU.max))
            own.done(TT(c2, p2, bc(m2), ALU.is_equal))
            own.done(TT(c2, c2, rank, ALU.mult))
            own.done(TR(k2, c2, AX.X, ALU.max))
            own.done(TT(oh2, c2, bc(k2), ALU.is_equal))
            own.done(TT(sm, m1, m2, ALU.add))
            own.done(nc.vector.reciprocal(sm, sm))
            own.done(TT(m1, m1, sm, ALU.mult))
            own.done(TT(m2, m2, sm, ALU.mult))
            own.done(TT(oh1, oh1, bc(m1), ALU.mult))
            own.done(TT(oh2, oh2, bc(m2), ALU.mult))
            own.done(TT(oh1, oh1, oh2, ALU.add))
            for t in range(NT):
                nc.vector.tensor_tensor(HW[:, t, :].rearrange("p (e r) -> p e r", e=EXPERTS),
                                        Hcat[:, t, 0:ER].rearrange("p (e r) -> p e r", e=EXPERTS),
                                        oh1[:, t, :].unsqueeze(2).broadcast_to([P, EXPERTS, LORA]),
                                        ALU.mult).then_inc(m["hw"], 1)

        def add_outputs(dve, own, s, banks, nxt):
            for t in range(NT):
                dve.wait_ge(out_ps, NT * LINEAR[s] + t + 1)
                dve.wait_ge(x_bias, NT * LINEAR[s] + t + 1)
                nc.vector.tensor_tensor(X[:, t, :], X[:, t, :], PS[:, banks[t % len(banks)], :], ALU.add).then_inc(x_done, 1)
                dve.wait_ge(x_done, NT * LINEAR[s] + t + 1)
                if nxt is not None:
                    ln_stats(dve, own, nxt, t)
                    if t >= 1:
                        ln_apply(dve, nxt, t - 1)
            if nxt is not None:
                ln_apply(dve, nxt, NT - 1)

        qz_sb = at(9216, 256).bitcast(I32).rearrange("p (g c) -> p g c", g=4)
        zeros = at(9472, 2048).bitcast(I32).rearrange("p (g n) -> p g n", g=4)
        qw_sb = at(11520, 2048).bitcast(I32).rearrange("p (g n) -> p g n", g=4)
        sc_sb = at(13568, 2048).rearrange("p (g n) -> p g n", g=4)
        shift = sb("shift", [P, 1], I32)
        part = sb("part", [P, 1], I32)

        def quant_loads(sp):
            src = g_qw.rearrange("(g q) n -> q g n", g=4)
            for q in range(16):
                sp.dma_start(qw_sb[8 * q:8 * q + 8, :, :], src[q, :, :].partition_broadcast(8)).then_inc(w_quant, DMA)
            sp.dma_start(qz_sb, g_qz.partition_broadcast(P)).then_inc(w_quant, DMA)
            sp.dma_start(sc_sb, g_sc.partition_broadcast(P)).then_inc(w_quant, DMA)

        def dequantise(dve, own):
            dve.wait_ge(consts, CONSTS)
            own.done(nc.vector.tensor_scalar(shift[:, :], part[:, :], 7, 2, ALU.bitwise_and, ALU.logical_shift_left))
            dve.wait_ge(w_quant, 19 * DMA)
            own.done(nc.vector.tensor_scalar(qw_sb, qw_sb, shift[:, 0:1], 15, ALU.arith_shift_right, ALU.bitwise_and))
            z8 = zeros.rearrange("p g (c s) -> p g c s", s=8)
            for j in range(8):
                own.done(nc.vector.tensor_scalar(z8[:, :, :, j], qz_sb, 4 * j, 15, ALU.arith_shift_right, ALU.bitwise_and))
            own.done(nc.vector.tensor_tensor(Wg[:, :, :], qw_sb, zeros, ALU.subtract))
            nc.vector.tensor_tensor(Wg[:, :, :], Wg[:, :, :], sc_sb, ALU.mult).then_inc(wg_ready, 1)

        def quant_pe(pe, s):
            pe.wait_ge(wg_ready, 1)
            for t in range(NT):
                pe.wait_ge(xt_ready, NT * s + t + 1)
                if t >= 4:
                    pe.wait_ge(x_done, NT * LINEAR[s] + t - 3)
                for k in range(KC):
                    last = nc.tensor.matmul(PS[:, t % 4, :], XT[:, k, t * P:t * P + P], Wg[:, k, :],
                                            start=k == 0, stop=k == KC - 1)
                last.then_inc(out_ps, 1)

        ms_names = ["par", "wout", "prj_ps", "prj_free", "th", "xs", "ss_ps", "ss_sb", "ms", "rs", "ssn", "sst_ps", "sst",
                    "bc_out", "ex", "w1", "ln", "dt", "dA", "scn", "u", "hc", "y", "tz", "yg", "par2", "aexp", "amin"]
        mm_ = {n: sem(f"m_{n}") for n in ms_names}
        win_in = [sem(f"win_in{i}") for i in range(3)]
        bc_in = [sem(f"bc_in{i}") for i in range(4)]
        Wout = at(0, 4096).rearrange("p (k n) -> p k n", k=DTILES)
        Wx = at(4096, 512).rearrange("p (k n) -> p k n", k=DTILES)
        par = at(4608, 32 + 3 * 8 + 128)
        convw = par[:, 0:32].rearrange("p (i j) -> p i j", i=DTILES)
        convb, bdt, Dp = par[:, 32:40], par[:, 40:48], par[:, 48:56]
        Aneg = par[:, 56:184].rearrange("p (i n) -> p i n", i=DTILES)
        win = at(5120, 1536).rearrange("p (r k n) -> p r k n", r=3, k=KC)
        Wdt = at(6656, 1024)
        dtu = at(7680, 1024).rearrange("p (r n) -> p r n", r=2)
        tz = at(8704, 512)
        xs = at(9216, 4096).rearrange("p (i n) -> p i n", i=DTILES)
        dt_ = at(13312, 4096).rearrange("p (i n) -> p i n", i=DTILES)
        Bbc = at(17408, 8192).rearrange("p (n t) -> p n t", n=NSTATE)
        Cbc = at(25600, 8192).rearrange("p (n t) -> p n t", n=NSTATE)
        U = 4
        ub = at(33792, 4096).rearrange("p (r n t) -> p r n t", r=U, n=2)
        tmp = at(33792, 4096).rearrange("p (r k n) -> p r k n", r=2, k=4)
        ss_sb = at(4800, 256).rearrange("p (t n) -> p t n", t=NTB)
        sq_sb = at(7680, 256).rearrange("p (t n) -> p t n", t=NTB)
        gs = sb("gs", [P, NTB, 4])
        ssT = at(8704, 512)[0:64, :]
        bc_dram = nc.dram_tensor("bc_dram", [BATCH, 2 * NSTATE, SEQ], F32, kind="Internal").ap()
        PER = 3 * DTILES + NTB
        NCH = NSTATE // 2

        def mamba_sp(sp):
            m = mm_
            sp.wait_ge(out_ps, NT * LINEAR[FFN_0] + NT)
            sp.dma_start(convw, m_convw.rearrange("(i p) j -> p i j", p=P)).then_inc(m["par"], DMA)
            for dst, v in ((convb, m_convb), (bdt, m_bdt), (Dp, m_d)):
                sp.dma_start(dst, v.rearrange("(i p) -> p i", p=P), allow_slow_non_contiguous=True).then_inc(m["par"], DMA)
            sp.dma_start(Aneg, m_alog.rearrange("(i p) n -> p i n", p=P)).then_inc(m["par"], DMA)
            sp.dma_start(Wx, m_wx.rearrange("(k p) n -> p k n", p=P)).then_inc(m["par"], DMA)
            sp.dma_start(Wout, m_wout.rearrange("(k p) n -> p k n", p=P)).then_inc(m["par"], DMA)
            sp.wait_ge(tr_done, NT * MAMBA + NT)
            sp.dma_start(Wdt[0:DT_RANK, :], m_wdt).then_inc(m["par2"], DMA)

            def load_win(n):
                b, j = n // 16, n % 16
                if n >= 3:
                    R = (n - 3) // 16 * PER + (n - 3) % 16 + (DTILES if (n - 3) % 16 >= DTILES else 0)
                    sp.wait_ge(m["prj_ps"], R + 1)
                sp.dma_start(win[:, n % 3, :, :],
                             m_win[:, j * P:j * P + P].rearrange("(k p) n -> p k n", p=P)).then_inc(win_in[n % 3], DMA)

            for b in range(BATCH):
                for j in range(DTILES + 3 if b == 0 else DTILES):
                    load_win(16 * b + j + (3 if b else 0))
                sp.wait_ge(m["sst"], b + 1)
                sp.dma_start(bc_dram[b, :, :], ssT[DT_RANK:64, :]).then_inc(m["bc_out"], DMA)
                sp.wait_ge(m["bc_out"], DMA * (b + 1))
                if b >= 1:
                    sp.wait_ge(m["hc"], NCH * DTILES * b)
                for q in range(4):
                    for k, dst in ((0, Bbc), (1, Cbc)):
                        sp.dma_start(dst[:, 4 * q:4 * q + 4, :],
                                     bc_dram[b, NSTATE * k + 4 * q:NSTATE * k + 4 * q + 4, :].partition_broadcast(P)
                                     ).then_inc(bc_in[q], DMA)
                for j in range(DTILES + 3, 2 * DTILES + 3):
                    if 16 * b + j < 32:
                        load_win(16 * b + j)

        def mamba_pe(pe):
            m = mm_
            pe.wait_ge(xt_ready, NT * MAMBA + NT)
            n = [0]

            def project(b, R):
                pe.wait_ge(win_in[n[0] % 3], DMA * (n[0] // 3 + 1))
                if R >= 2:
                    pe.wait_ge(m["prj_free"], R - 1)
                for k in range(KC):
                    last = nc.tensor.matmul(PS[:, 6 + R % 2, :], win[:, n[0] % 3, k, :], XT[:, k, b * SEQ:b * SEQ + SEQ],
                                            start=k == 0, stop=k == KC - 1)
                last.then_inc(m["prj_ps"], 1)
                n[0] += 1

            for b in range(BATCH):
                R0 = b * PER
                for i in range(DTILES):
                    project(b, R0 + i)
                pe.wait_ge(m["par"], 7 * DMA)
                pe.wait_ge(m["xs"], DTILES * (b + 1))
                if b:
                    pe.wait_ge(m["yg"], DTILES * b)
                for t in range(NTB):
                    for i in range(DTILES):
                        last = nc.tensor.matmul(PS[:, 4, 64 * t:64 * t + 64], xs[:, i, t * P:t * P + P], Wx[:, i, :],
                                                start=i == 0, stop=i == DTILES - 1)
                last.then_inc(m["ss_ps"], 1)
                pe.wait_ge(m["ssn"], b + 1)
                for t in range(NTB):
                    last = nc.tensor.transpose(PS[0:64, 5, t * P:t * P + P], ss_sb[:, t, :], ident[:, :])
                last.then_inc(m["sst_ps"], 1)
                pe.wait_ge(m["sst"], b + 1)
                pe.wait_ge(m["par2"], DMA)
                for i in range(DTILES):
                    R = R0 + DTILES + i
                    pe.wait_ge(m["prj_free"], R - 1)
                    nc.tensor.matmul(PS[:, 6 + R % 2, :], Wdt[0:DT_RANK, i * P:i * P + P], ssT[0:DT_RANK, :],
                                     start=True, stop=True).then_inc(m["prj_ps"], 1)
                for i in range(DTILES):
                    k = b * DTILES + i
                    project(b, R0 + 2 * DTILES + i)
                    if k >= 2:
                        pe.wait_ge(m["yg"], k - 1)
                    for c in range(NCH):
                        q = k * NCH + c
                        pe.wait_ge(m["hc"], q + 1)
                        for e in range(2):
                            last = nc.tensor.matmul(PS[:, 4 + k % 2, :], ident[:, :], ub[:, q % U, e, :],
                                                    start=c == 0 and e == 0, stop=c == NCH - 1 and e == 1)
                        last.then_inc(m["y"], 1)
                pe.wait_ge(m["yg"], DTILES * (b + 1))
                for t in range(NTB):
                    R = R0 + 3 * DTILES + t
                    pe.wait_ge(m["prj_free"], R - 1)
                    for i in range(DTILES):
                        last = nc.tensor.matmul(PS[:, 6 + R % 2, :], xs[:, i, t * P:t * P + P], Wout[:, i, :],
                                                start=i == 0, stop=i == DTILES - 1)
                    last.then_inc(m["prj_ps"], 1)

        def mamba_act(act, own):
            m = mm_
            act.wait_ge(m["amin"], 1)
            nc.scalar.activation(Aneg, Aneg, ACT.Exp).then_inc(m["aexp"], 1)
            for b in range(BATCH):
                R0 = b * PER
                for i in range(DTILES):
                    act.wait_ge(m["prj_free"], R0 + i + 1)
                    if i >= 2:
                        act.wait_ge(m["xs"], b * DTILES + i - 1)
                    nc.scalar.activation(tmp[:, i % 2, 0, :], xs[:, i, :], ACT.Tanh).then_inc(m["th"], 1)
                act.wait_ge(m["ss_ps"], b + 1)
                nc.scalar.copy(ss_sb[:, :, :], PS[:, 4, 0:256].rearrange("p (t n) -> p t n", t=NTB)).then_inc(m["ss_sb"], 1)
                act.wait_ge(m["sst_ps"], b + 1)
                nc.scalar.copy(ssT[:, :], PS[0:64, 5, :]).then_inc(m["sst"], 1)
                for i in range(DTILES + 1):
                    k = b * DTILES + i
                    if i < DTILES:
                        R = R0 + DTILES + i
                        act.wait_ge(m["prj_ps"], R + 1)
                        if i >= 2:
                            act.wait_ge(m["dt"], k - 1)
                        T = tmp[:, i % 2, 0, :]
                        own.done(nc.scalar.activation(T, PS[:, 6 + R % 2, :], ACT.Abs, bias=bdt[:, i:i + 1]))
                        nc.scalar.activation(dt_[:, i, :], PS[:, 6 + R % 2, :], ACT.Relu,
                                             bias=bdt[:, i:i + 1]).then_inc(m["prj_free"], 1)
                        nc.scalar.activation(T, T, ACT.Exp, scale=-1.0).then_inc(m["ex"], 1)
                    if i >= 1:
                        act.wait_ge(m["w1"], k - 1 + 2)
                        nc.scalar.activation(tmp[:, (i - 1) % 2, 2, :], tmp[:, (i - 1) % 2, 1, :], ACT.Ln).then_inc(m["ln"], 1)
                act.wait_ge(m["dt"], DTILES * (b + 1))
                act.wait_ge(m["bc_out"], DMA * (b + 1))
                for i in range(DTILES):
                    k = b * DTILES + i
                    for c in range(NCH):
                        q = k * NCH + c
                        if q >= 2:
                            act.wait_ge(m["scn"], q - 1)
                        for e in range(2):
                            last = nc.scalar.activation(PS[:, q % 2 * 2 + e, 1:SEQ], dt_[:, i, 1:SEQ], ACT.Exp,
                                                        scale=Aneg[:, i, 2 * c + e:2 * c + e + 1])
                        last.then_inc(m["dA"], 1)
                        if c == 2:
                            R = R0 + 2 * DTILES + i
                            act.wait_ge(m["prj_ps"], R + 1)
                            if k:
                                act.wait_ge(m["yg"], k)
                            nc.scalar.activation(tz, PS[:, 6 + R % 2, :], ACT.Tanh, scale=0.5).then_inc(m["tz"], 1)

        def mamba_pool(pool, own):
            m = mm_
            for b in range(BATCH):
                pool.wait_ge(m["ms"], b + 1)
                own.done(nc.gpsimd.tensor_scalar(gs[:, :, :], gs[:, :, :], RMS_EPS, None, ALU.add))
                nc.gpsimd.tensor_tensor(gs[:, :, :], gs[:, :, :], minus_half[:, :].rearrange("p (t k) -> p t k", t=NTB),
                                        ALU.pow).then_inc(m["rs"], 1)
                for i in range(DTILES):
                    k = b * DTILES + i
                    pool.wait_ge(m["dt"], DTILES * (b + 1))
                    own.done(nc.gpsimd.tensor_tensor(dtu[:, k % 2, :], dt_[:, i, :], xs[:, i, :], ALU.mult))
                    for c in range(NCH):
                        q = k * NCH + c
                        if i == 0 and c % 2 == 0:
                            pool.wait_ge(bc_in[c // 2], 2 * DMA * (b + 1))
                        if q >= U:
                            pool.wait_ge(m["y"], q - U + 1)
                        nc.gpsimd.tensor_tensor(ub[:, q % U, :, :], dtu[:, k % 2, :].unsqueeze(1).broadcast_to([P, 2, SEQ]),
                                                Bbc[:, 2 * c:2 * c + 2, :], ALU.mult).then_inc(m["u"], 1)

        def mamba_dve(dve, own):
            m = mm_
            TT, TS, STT = nc.vector.tensor_tensor, nc.vector.tensor_scalar, nc.vector.scalar_tensor_tensor
            dve.wait_ge(m["par"], 7 * DMA)
            TS(Aneg, Aneg, 86.0, None, ALU.min).then_inc(m["amin"], 1)
            dve.wait_ge(m["aexp"], 1)
            own.done(TS(Aneg, Aneg, -1.0, None, ALU.mult))
            own.done(TS(par[:, 0:40], par[:, 0:40], 0.5, None, ALU.mult))
            dve.wait_ge(xt_ready, NT * MAMBA + NT)
            nc.vector.memset(PS[:, 0:4, 0:1], 0.0).then_inc(m["w1"], 1)

            def silu(b, i):
                dve.wait_ge(m["th"], b * DTILES + i + 1)
                STT(xs[:, i, :], tmp[:, i % 2, 0, :], 1.0, xs[:, i, :], ALU.add, ALU.mult).then_inc(m["xs"], 1)

            for b in range(BATCH):
                R0 = b * PER
                for i in range(DTILES):
                    R = R0 + i
                    dve.wait_ge(m["prj_ps"], R + 1)
                    ps = PS[:, 6 + R % 2, :]
                    own.done(TS(xs[:, i, :], ps, convw[:, i, 3:4], convb[:, i:i + 1], ALU.mult, ALU.add))
                    for j in (2, 1):
                        own.done(STT(xs[:, i, 3 - j:SEQ], ps[:, 0:SEQ - 3 + j], convw[:, i, j:j + 1], xs[:, i, 3 - j:SEQ],
                                     ALU.mult, ALU.add))
                    STT(xs[:, i, 3:SEQ], ps[:, 0:SEQ - 3], convw[:, i, 0:1], xs[:, i, 3:SEQ],
                        ALU.mult, ALU.add).then_inc(m["prj_free"], 1)
                    if i:
                        silu(b, i - 1)
                silu(b, DTILES - 1)
                dve.wait_ge(m["ss_sb"], b + 1)
                own.done(TT(sq_sb[:, :, :], ss_sb[:, :, :], ss_sb[:, :, :], ALU.mult))
                own.done(nc.vector.tensor_reduce(gs[:, :, :], sq_sb[:, :, :].rearrange("p t (k n) -> p t k n", k=4), AX.X, ALU.add))
                own.done(TT(gs[:, :, 0], gs[:, :, 0], gs[:, :, 1], ALU.add))
                own.done(TS(gs[:, :, 0], gs[:, :, 0], 0.5, None, ALU.mult))
                own.done(nc.vector.tensor_copy(gs[:, :, 1], gs[:, :, 0]))
                TS(gs[:, :, :], gs[:, :, :], 1.0 / NSTATE, None, ALU.mult).then_inc(m["ms"], 1)
                dve.wait_ge(m["rs"], b + 1)
                TT(ss_sb[:, :, :].rearrange("p t (k n) -> p t k n", k=4), ss_sb[:, :, :].rearrange("p t (k n) -> p t k n", k=4),
                   gs[:, :, :].unsqueeze(3).broadcast_to([P, NTB, 4, 16]), ALU.mult).then_inc(m["ssn"], 1)
                for i in range(DTILES + 1):
                    k = b * DTILES + i
                    if i < DTILES:
                        dve.wait_ge(m["ex"], k + 1)
                        e, w = tmp[:, i % 2, 0, :], tmp[:, i % 2, 1, :]
                        TS(w, e, 1.0, None, ALU.add).then_inc(m["w1"], 1)
                    if i >= 1:
                        e, w, l, d = [tmp[:, (i - 1) % 2, x, :] for x in range(4)]
                        dve.wait_ge(m["ln"], k)
                        own.done(TS(d, w, 1.0, None, ALU.subtract))
                        own.done(STT(w, d, 0.0, d, ALU.is_equal, ALU.add))
                        own.done(STT(l, d, 0.0, l, ALU.is_equal, ALU.add))
                        own.done(TT(l, l, e, ALU.mult))
                        own.done(nc.vector.reciprocal(w, w))
                        own.done(TT(l, l, w, ALU.mult))
                        TT(dt_[:, i - 1, :], dt_[:, i - 1, :], l, ALU.add).then_inc(m["dt"], 1)
                for i in range(DTILES):
                    k = b * DTILES + i
                    for c in range(NCH + 1):
                        q = k * NCH + c
                        if c < NCH:
                            v = ub[:, q % U, :, :].rearrange("p n t -> p (n t)")
                            dve.wait_ge(m["dA"], q + 1)
                            dve.wait_ge(m["u"], q + 1)
                            nc.vector.tensor_tensor_scan(v, PS[:, q % 2 * 2:q % 2 * 2 + 2, :].rearrange("p n t -> p (n t)"), v,
                                                         0.0, ALU.mult, ALU.add).then_inc(m["scn"], 1)
                        if c >= 1:
                            dve.wait_ge(m["scn"], q)
                            TT(ub[:, (q - 1) % U, :, :], ub[:, (q - 1) % U, :, :], Cbc[:, 2 * c - 2:2 * c, :],
                               ALU.mult).then_inc(m["hc"], 1)
                    R = R0 + 2 * DTILES + i
                    dve.wait_ge(m["tz"], k + 1)
                    STT(tz, tz, 1.0, PS[:, 6 + R % 2, :], ALU.add, ALU.mult).then_inc(m["prj_free"], 1)
                    dve.wait_ge(m["y"], NCH * (k + 1))
                    dve.wait_ge(m["prj_free"], R + 1)
                    own.done(STT(xs[:, i, :], xs[:, i, :], Dp[:, i:i + 1], PS[:, 4 + k % 2, :], ALU.mult, ALU.add))
                    STT(xs[:, i, :], xs[:, i, :], 0.5, tz, ALU.mult, ALU.mult).then_inc(m["yg"], 1)
                for t in range(NTB):
                    R = R0 + 3 * DTILES + t
                    dve.wait_ge(m["prj_ps"], R + 1)
                    TT(X[:, b * NTB + t, :], X[:, b * NTB + t, :], PS[:, 6 + R % 2, :], ALU.add).then_inc(m["prj_free"], 1)
                    dve.wait_ge(m["prj_free"], R + 1)

        hs_names = ["w", "pad", "prj_ps", "prj_free", "vt", "s_ps", "s_free", "sub", "ex", "rs", "p", "pt", "o_ps", "ct", "ct_ps", "res"]
        hm = {n: sem(f"h_{n}") for n in hs_names}
        HALF = P
        WPAD = DIM + HD
        hw = [at(31552 + KC * WPAD * i, KC * WPAD).rearrange("p (k n) -> p k n", k=KC) for i in range(3)]
        hb = sb("hb", [P, 3, HEADS])
        VG = at(5120, 4096).rearrange("p (t d) -> p t d", t=HALF)
        QKV = [at(9216 + 4096 * i, 4096).rearrange("p (h t) -> p h t", h=HEADS) for i in range(3)]
        CT = QKV[0].rearrange("p h t -> p (h t)").rearrange("p (t h) -> p t h", t=HALF)
        PR = at(21504, 4096).rearrange("p (t g) -> p t g", t=HALF)
        PRT = at(25600, 4096).rearrange("p (t g) -> p t g", t=HALF)
        hmax = at(29696, HALF)
        hsum = at(29696 + HALF, HALF)
        BT = 512 // HEADS
        NB = HALF // BT

        def heads_sp(sp):
            m = hm
            sp.wait_ge(am[ATTN_M]["ring"], len(RING))
            for i, w in enumerate((h_wq, h_wk, h_wv)):
                sp.dma_start(hw[i][:, :, 0:DIM], w.rearrange("(k p) n -> p k n", p=P)).then_inc(m["w"], DMA)
            sp.wait_ge(m["pad"], 1)
            for r in range(4):
                sp.dma_start(hb[32 * r:32 * r + HD, :, :], h_bias).then_inc(m["w"], DMA)

        def heads_pool(pool, own):
            m = hm
            nc.gpsimd.memset(hb[:, :, :], 0.0).then_inc(m["pad"], 1)
            pool.wait_ge(am[ATTN_M]["ring"], len(RING))
            for i in range(3):
                own.done(nc.gpsimd.memset(hw[i][:, :, DIM:WPAD], 0.0))
            nc.gpsimd.memset(hmax[:, 0:1], 0.0).then_inc(m["pad"], 1)
            for e in range(2 * NB):
                pool.wait_ge(m["rs"], e + 1)
                sl = slice(e % NB * BT, e % NB * BT + BT)
                nc.gpsimd.tensor_tensor(PR[:, sl, :], PR[:, sl, :], hsum[:, sl].unsqueeze(2).broadcast_to([P, BT, HEADS]),
                                        ALU.mult).then_inc(m["p"], 1)

        def heads_pe(pe):
            m = hm
            pe.wait_ge(m["w"], 7 * DMA)
            pe.wait_ge(m["pad"], 2)
            pe.wait_ge(xt_ready, NT * ATTN_H + NT)
            for hf in range(2):
                for n in range(24):
                    u = hf * 24 + n
                    if u >= 4:
                        pe.wait_ge(m["prj_free"], u - 3)
                    if n < 4 and hf:
                        pe.wait_ge(m["res"], 8 * hf)
                    for h in range(4 * (n % 8), 4 * (n % 8) + 4):
                        for k in range(KC):
                            for r in range(4):
                                t0 = r * 2 * HALF + hf * HALF
                                last = nc.tensor.matmul(PS[32 * r:32 * r + 32, u % 4, h % 4 * P:h % 4 * P + P],
                                                        hw[n // 8][:, k, HD * h:HD * h + 32], XT[:, k, t0:t0 + HALF],
                                                        start=k == 0, stop=k == KC - 1, tile_position=(0, 32 * r))
                    last.then_inc(m["prj_ps"], 1)
                for e in range(NB):
                    ee = hf * NB + e
                    if e == 0:
                        pe.wait_ge(m["prj_free"], 24 * (hf + 1))
                    if ee >= 4:
                        pe.wait_ge(m["sub"], ee - 3)
                    for t in range(BT * e, BT * e + BT):
                        for r in range(4):
                            o = t % BT * HEADS
                            last = nc.tensor.matmul(PS[32 * r:32 * r + 32, 4 + e % 4, o:o + HEADS],
                                                    QKV[0][32 * r:32 * r + HD, :, t], QKV[1][32 * r:32 * r + HD, :, t],
                                                    start=True, stop=True, tile_position=(32 * r, 32 * r))
                    last.then_inc(m["s_ps"], 1)
                pe.wait_ge(m["vt"], 4 * (hf + 1))
                for e in range(NB):
                    ee = hf * NB + e
                    pe.wait_ge(m["pt"], ee + 1)
                    if ee >= 4 and e >= 4:
                        pe.wait_ge(m["ct"], ee - 3)
                    for t in range(BT * e, BT * e + BT):
                        for r in range(4):
                            o = t % BT * HEADS
                            last = nc.tensor.matmul(PS[32 * r:32 * r + 32, e % 4, o:o + HEADS],
                                                    VG[32 * r:32 * r + 32, t, :], PRT[32 * r:32 * r + 32, t, :],
                                                    start=True, stop=True, tile_position=(32 * r, 32 * r))
                    last.then_inc(m["o_ps"], 1)
                pe.wait_ge(m["ct"], NB * (hf + 1))
                for n in range(8):
                    if n >= 4:
                        pe.wait_ge(m["res"], hf * 8 + n - 3)
                    for h in range(4 * n, 4 * n + 4):
                        last = nc.tensor.transpose(PS[:, n % 4, h % 4 * P:h % 4 * P + P], CT[:, :, h], ident[:, :])
                    last.then_inc(m["ct_ps"], 1)

        def heads_act(act):
            m = hm
            for hf in range(2):
                for e in range(NB):
                    ee = hf * NB + e
                    act.wait_ge(m["sub"], ee + 1)
                    sl = slice(e * BT, e * BT + BT)
                    nc.scalar.activation(PR[:, sl, :], PR[:, sl, :], ACT.Exp, scale=SCALE).then_inc(m["ex"], 1)
                for e in range(NB):
                    ee = hf * NB + e
                    act.wait_ge(m["o_ps"], ee + 1)
                    nc.scalar.copy(CT[:, e * BT:e * BT + BT, :], PS[:, e % 4, :].rearrange("p (t h) -> p t h", t=BT)
                                   ).then_inc(m["ct"], 1)

        def heads_dve(dve, own):
            m = hm
            TT, TR = nc.vector.tensor_tensor, nc.vector.tensor_reduce
            dve.wait_ge(m["w"], 7 * DMA)
            dve.wait_ge(xt_ready, NT * ATTN_H + NT)
            for hf in range(2):
                for n in range(24):
                    u = hf * 24 + n
                    dve.wait_ge(m["prj_ps"], u + 1)
                    h0 = n % 8 * 4
                    TT(QKV[n // 8][:, h0:h0 + 4, :], PS[:, u % 4, :].rearrange("p (h t) -> p h t", h=4),
                       hb[:, n // 8, h0:h0 + 4].unsqueeze(2).broadcast_to([P, 4, HALF]), ALU.add).then_inc(m["prj_free"], 1)
                dve.wait_ge(m["prj_free"], 24 * (hf + 1))
                for c in range(4):
                    sl = slice(32 * c, 32 * c + 32)
                    nc.vector.transpose(VG[:, sl, :], QKV[2][:, :, sl].rearrange("p h t -> p t h")).then_inc(m["vt"], 1)
                for e in range(NB + 1):
                    ee = hf * NB + e
                    if e < NB:
                        sl = slice(e * BT, e * BT + BT)
                        ps = PS[:, 4 + e % 4, :].rearrange("p (t g) -> p t g", t=BT)
                        dve.wait_ge(m["s_ps"], ee + 1)
                        own.done(TR(hmax[:, sl], ps, AX.X, ALU.max, negate=True))
                        TT(PR[:, sl, :], ps, hmax[:, sl].unsqueeze(2).broadcast_to([P, BT, HEADS]), ALU.add).then_inc(m["sub"], 1)
                    if e >= 1:
                        sl = slice((e - 1) * BT, e * BT)
                        dve.wait_ge(m["ex"], ee)
                        own.done(TR(hsum[:, sl], PR[:, sl, :], AX.X, ALU.add))
                        nc.vector.reciprocal(hsum[:, sl], hsum[:, sl]).then_inc(m["rs"], 1)
                for e in range(NB):
                    sl = slice(e * BT, e * BT + BT)
                    dve.wait_ge(m["p"], hf * NB + e + 1)
                    nc.vector.transpose(PRT[:, sl, :], PR[:, sl, :]).then_inc(m["pt"], 1)
                for n in range(8):
                    dve.wait_ge(m["ct_ps"], hf * 8 + n + 1)
                    src = PS[:, n % 4, :].rearrange("p (h r d) -> p h r d", h=4, r=4)
                    for r in range(4):
                        dst = X[:, 2 * r + hf, 64 * n:64 * n + 64].rearrange("p (h d) -> p h d", h=4)
                        last = TT(dst, dst, src[:, :, r, 0:HD], ALU.add)
                    last.then_inc(m["res"], 1)
            dve.wait_ge(m["res"], 16)

        CONSTS = 6
        block = ctx.enter_context(nc.Block())

        def attention_weights(sp, s, wq, wk, wv, wo):
            kw = wk.shape[1]
            for dst, w in ((a_wk_sb[:, :, 0:kw], wk), (a_wq_sb, wq), (a_wv_sb[:, :, 0:kw], wv), (a_wo_sb, wo)):
                sp.dma_start(dst, w.rearrange("(k p) n -> p k n", p=P)).then_inc(am[s]["w"], DMA)

        DONE = {1: (am[ATTN_A]["ring"], len(RING)), 2: (x_done, NT * LINEAR[FFN_0] + NT), 3: (mm_["prj_free"], 2 * PER),
                4: (x_done, NT * LINEAR[FFN_1] + NT), 5: (am[ATTN_M]["ring"], len(RING)), 6: (x_done, NT * LINEAR[QUANT_0] + NT), 7: (hm["res"], 16),
                8: (x_done, NT * LINEAR[QUANT_1] + NT)}

        @block.sync
        def _(sp):
            for b in range(BATCH):
                sp.dma_start(X[:, NTB * b:NTB * b + NTB, :],
                             x[b, :, :].rearrange("(t p) c -> p t c", p=P)).then_inc(x_loaded[b], DMA)
            attention_weights(sp, ATTN_A, a_wq, a_wk, a_wv, a_wo)
            for dst, w in ((Wf[:, :, :], f_wbase), (Wcat[:, :, :], f_cat)):
                sp.dma_start(dst, w.rearrange("(k p) n -> p k n", p=P)).then_inc(w_ffn, DMA)
            sp.dma_start(Wbt[:, :], f_bt).then_inc(w_ffn, DMA)
            sp.dma_start(bias_f[:, :], f_bias.partition_broadcast(P)).then_inc(w_ffn, DMA)
            sp.dma_start(bias_g[:, :], g_bias.partition_broadcast(P)).then_inc(w_quant, DMA)
            attention_sp(sp, ATTN_A)
            sp.wait_ge(am[ATTN_A]["exp"], 128)
            quant_loads(sp)
            mamba_sp(sp)
            sp.wait_ge(*DONE[3])
            attention_weights(sp, ATTN_M, q_wq, q_wk, q_wv, q_wo)
            attention_sp(sp, ATTN_M)
            heads_sp(sp)
            sp.wait_ge(*DONE[8])
            sp.dma_start(out[:, :, :].rearrange("b (t p) c -> p (b t) c", p=P), X[:, :, :]).then_inc(stored, DMA)
            sp.wait_ge(stored, DMA)

        @block.gpsimd
        def _(pool):
            own = Own(pool, pool_own)
            own.done(nc.gpsimd.memset(ident[:, :], 0.0))
            nc.gpsimd.affine_select(out=ident[:, :], in_=ident[:, :], compare_op=ALU.not_equal, fill=1.0, base=0,
                                    pattern=[[-1, P]], channel_multiplier=1).then_inc(consts, 1)
            own.done(nc.gpsimd.memset(identb[:, :], 0.0))
            nc.gpsimd.affine_select(out=identb[:, :], in_=identb[:, :], compare_op=ALU.not_equal, fill=1.0, base=0,
                                    pattern=[[-1, P]], channel_multiplier=1).then_inc(consts, 1)
            own.done(nc.gpsimd.memset(mask_qk[:, :], 0.0))
            nc.gpsimd.affine_select(out=mask_qk[:, :], in_=mask_qk[:, :], compare_op=ALU.is_ge, fill=NEG, base=0,
                                    pattern=[[-1, P]], channel_multiplier=1).then_inc(consts, 1)
            own.done(nc.gpsimd.memset(mask_kq[:, :], 0.0))
            nc.gpsimd.affine_select(out=mask_kq[:, :], in_=mask_kq[:, :], compare_op=ALU.is_ge, fill=NEG, base=0,
                                    pattern=[[1, P]], channel_multiplier=-1).then_inc(consts, 1)
            own.done(nc.gpsimd.memset(minus_half[:, :], -0.5))
            nc.gpsimd.iota(part[:, :], [[0, 1]], base=0, channel_multiplier=1).then_inc(consts, 1)
            for e in range(EXPERTS):
                own.done(nc.gpsimd.memset(rank8[:, e:e + 1], float(EXPERTS - e)))
            nc.gpsimd.memset(rank8[:, 0:1], float(EXPERTS)).then_inc(consts, 1)
            pool.wait_ge(consts, 6)
            ln_rstds(pool, own, ATTN_A)
            attention_pool(pool, ATTN_A)
            for s, bias, w, n in ((FFN_0, bias_f, w_ffn, 4 * DMA),):
                ln_rstds(pool, own, s)
                add_bias(pool, s, bias, w, n)
            ln_rstds(pool, own, MAMBA)
            mamba_pool(pool, own)
            ln_rstds(pool, own, FFN_1)
            add_bias(pool, FFN_1, bias_f, w_ffn, 4 * DMA)
            ln_rstds(pool, own, ATTN_M)
            attention_pool(pool, ATTN_M)
            ln_rstds(pool, own, QUANT_0)
            add_bias(pool, QUANT_0, bias_g, w_quant, 19 * DMA)
            ln_rstds(pool, own, ATTN_H)
            heads_pool(pool, own)
            ln_rstds(pool, own, QUANT_1)
            add_bias(pool, QUANT_1, bias_g, w_quant, 19 * DMA)

        @block.scalar
        def _(act):
            own = Own(act, act_own)
            xt_copies(act, ATTN_A)
            attention_act(act, ATTN_A)
            xt_copies(act, FFN_0)
            ffn_act(act, FFN_0)
            xt_copies(act, MAMBA)
            mamba_act(act, own)
            xt_copies(act, FFN_1)
            ffn_act(act, FFN_1)
            xt_copies(act, ATTN_M)
            attention_act(act, ATTN_M)
            xt_copies(act, QUANT_0)
            xt_copies(act, ATTN_H)
            heads_act(act)
            xt_copies(act, QUANT_1)

        @block.vector
        def _(dve):
            own = Own(dve, dve_own)
            layer_norm(dve, own, ATTN_A)
            attention_dve(dve, own, ATTN_A)
            layer_norm(dve, own, FFN_0)
            dequantise(dve, own)
            ffn_dve(dve, own, FFN_0)
            add_outputs(dve, own, FFN_0, (2, 3, 4), MAMBA)
            mamba_dve(dve, own)
            layer_norm(dve, own, FFN_1)
            ffn_dve(dve, own, FFN_1)
            add_outputs(dve, own, FFN_1, (2, 3, 4), ATTN_M)
            attention_dve(dve, own, ATTN_M)
            layer_norm(dve, own, QUANT_0)
            add_outputs(dve, own, QUANT_0, (0, 1, 2, 3), ATTN_H)
            heads_dve(dve, own)
            layer_norm(dve, own, QUANT_1)
            add_outputs(dve, own, QUANT_1, (0, 1, 2, 3), None)

        @block.tensor
        def _(pe):
            transposes(pe, ATTN_A)
            attention_pe(pe, ATTN_A)
            transposes(pe, FFN_0)
            ffn_pe(pe, FFN_0)
            transposes(pe, MAMBA)
            mamba_pe(pe)
            transposes(pe, FFN_1)
            ffn_pe(pe, FFN_1)
            transposes(pe, ATTN_M)
            attention_pe(pe, ATTN_M)
            transposes(pe, QUANT_0)
            quant_pe(pe, QUANT_0)
            transposes(pe, ATTN_H)
            heads_pe(pe)
            transposes(pe, QUANT_1)
            quant_pe(pe, QUANT_1)


def _laid_out(i):
    import numpy as np
    c = np.ascontiguousarray
    w = {k: np.asarray(v) for k, v in i.items()}
    head_cols = lambda b: c(b.reshape(HEADS, HD).T)
    return {
        "x": w["L0_attn_a_x"],
        "a_wq": w["L0_attn_a_wq"], "a_wk": w["L0_attn_a_wk"], "a_wv": w["L0_attn_a_wv"], "a_wo": w["L0_attn_a_wo"],
        "m_win": c(w["L0_attn_b_W_in"].T), "m_convw": w["L0_attn_b_conv_w"], "m_convb": w["L0_attn_b_conv_b"],
        "m_wx": c(w["L0_attn_b_W_x"].T), "m_wdt": c(w["L0_attn_b_W_dt"].T), "m_bdt": w["L0_attn_b_b_dt"],
        "m_alog": w["L0_attn_b_A_log"], "m_d": w["L0_attn_b_D"], "m_wout": c(w["L0_attn_b_W_out"].T),
        "f_wbase": c(w["L0_ffn_W_base"].T),
        "f_cat": c(np.concatenate([w["L0_ffn_A"].reshape(ER, DIM), w["L0_ffn_W_gate"]], 0).T),
        "f_bias": w["L0_ffn_b_base"], "f_bt": c(w["L0_ffn_B"].transpose(0, 2, 1).reshape(ER, DIM)),
        "q_wq": w["L1_attn_a_wq"], "q_wk": w["L1_attn_a_wk"], "q_wv": w["L1_attn_a_wv"], "q_wo": w["L1_attn_a_wo"],
        "h_wq": c(w["L1_attn_b_wq"].T), "h_wk": c(w["L1_attn_b_wk"].T), "h_wv": c(w["L1_attn_b_wv"].T),
        "h_bias": c(np.stack([head_cols(w["L1_attn_b_bq"]), head_cols(w["L1_attn_b_bk"]), head_cols(w["L1_attn_b_bv"])], 1)),
        "g_qw": w["L1_ffn_qweight"], "g_qz": w["L1_ffn_qzeros"], "g_sc": w["L1_ffn_scales"], "g_bias": w["L1_ffn_bias"],
    }


def kernel(**inputs):
    import numpy as _np
    import concourse.bacc as _bacc
    from concourse import mybir as _mybir
    from concourse.bass_utils import run_bass_kernel_spmd as _run

    nc = _bacc.Bacc("TRN2", target_bir_lowering=False, num_devices=1)
    arrays = {f"in_{k}": _np.ascontiguousarray(v) for k, v in _laid_out(inputs).items()}
    args = [nc.dram_tensor(k, a.shape, _mybir.dt.from_np(a.dtype), kind="ExternalInput").ap() for k, a in arrays.items()]
    args.append(nc.dram_tensor("out_x", (BATCH, SEQ, DIM), _mybir.dt.float32, kind="ExternalOutput").ap())
    hybrid_kernel(nc, *args)
    r = _run(nc, [arrays], core_ids=[0])
    return r.results[0]["out_x"]
```

```python
import concourse.bass as bass
from concourse import mybir
from contextlib import ExitStack

F32 = mybir.dt.float32
BF16 = mybir.dt.bfloat16
I32 = mybir.dt.int32
ALU = mybir.AluOpType
ACT = mybir.ActivationFunctionType
AX = mybir.AxisListType

P = 128
BATCH, SEQ, DIM = 2, 512, 512
TOK = BATCH * SEQ
NT = TOK // P
NTB = NT // BATCH
KC = DIM // P
HEADS, HD = 32, 16
HPC = P // HD
D_IN, NSTATE, DT_RANK, CONV = 1024, 16, 32, 4
DTILES = D_IN // P
EXPERTS, LORA = 8, 16
ER = EXPERTS * LORA
FCAT = ER + EXPERTS
NEG = -1.0e30
SCALE = HD ** -0.5
LN_EPS, RMS_EPS = 1e-5, 1e-6


def hybrid_kernel(nc, x, a_wq, a_wk, a_wv, a_wo, m_win, m_convw, m_convb, m_wx, m_wdt, m_bdt, m_alog, m_d,
                  m_wout, f_wbase, f_cat, f_bias, f_bt, q_wq, q_wk, q_wv, q_wo, h_wq, h_wk, h_wv, h_bias,
                  g_qw, g_qz, g_sc, g_bias, out):
    ctx = ExitStack()
    with ctx:
        def sb(name, shape, dt=F32):
            return ctx.enter_context(nc.sbuf_tensor(name, shape, dt))

        def sem(name):
            return ctx.enter_context(nc.semaphore(name))

        X = sb("X", [P, NT, DIM])
        XT = sb("XT", [P, KC, TOK])
        Wg = sb("Wg", [P, KC, DIM])
        Wf = sb("Wf", [P, KC, DIM])
        Wcat = sb("Wcat", [P, KC, FCAT])
        Wbt = sb("Wbt", [P, DIM])
        bias_f = sb("bias_f", [P, DIM])
        bias_g = sb("bias_g", [P, DIM])
        ident = sb("ident", [P, P])
        identb = sb("identb", [P, P], BF16)
        mask_qk = sb("mask_qk", [P, P], BF16)
        mask_kq = sb("mask_kq", [P, P], BF16)
        bn = sb("bn", [P, NT, 6])
        mv = sb("mv", [P, NT, 2])
        rstd = sb("rstd", [P, NT, 1])
        minus_half = sb("minus_half", [P, NTB * 4])
        rank8 = sb("rank8", [P, EXPERTS])
        ARENA = 37888
        arena = sb("arena", [P, ARENA])

        def at(off, n, dt=F32):
            v = arena[:, off:off + n]
            return v if dt == F32 else v.bitcast(dt)

        XN = at(5120, 4096).rearrange("p (t c) -> p t c", t=NT)

        PS = ctx.enter_context(nc.psum_tensor("PS", [P, 8, 512], F32))

        ATTN_A, FFN_0, MAMBA, FFN_1, ATTN_M, QUANT_0, ATTN_H, QUANT_1 = range(8)

        x_loaded = [sem(f"x_loaded{b}") for b in range(BATCH)]
        ln_stat = sem("ln_stat")
        ln_rstd = sem("ln_rstd")
        xn_ready = sem("xn_ready")
        tr_done = sem("tr_done")
        xt_ready = sem("xt_ready")
        out_ps = sem("out_ps")
        x_done = sem("x_done")
        x_bias = sem("x_bias")
        dve_own, pool_own, act_own = sem("dve_own"), sem("pool_own"), sem("act_own")
        consts = sem("consts")
        w_ffn, w_quant, wg_ready = sem("w_ffn"), sem("w_quant"), sem("wg_ready")
        stored = sem("stored")

        LINEAR = {FFN_0: 0, FFN_1: 1, QUANT_0: 2, QUANT_1: 3}

        class Own:

            def __init__(self, eng, s):
                self.eng, self.s, self.n = eng, s, 0

            def done(self, ins):
                self.n += 1
                ins.then_inc(self.s, 1)
                self.eng.wait_ge(self.s, self.n)

        def ln_stats(dve, own, s, t):
            if s == 0:
                dve.wait_ge(x_loaded[t // NTB], 16)
            own.done(nc.vector.bn_stats(bn[:, t, :], X[:, t, :]))
            nc.vector.bn_aggr(mv[:, t, :], bn[:, t, :]).then_inc(ln_stat, 1)

        def ln_rstds(pool, own, s):
            for t in range(NT):
                pool.wait_ge(ln_stat, NT * s + t + 1)
                own.done(nc.gpsimd.tensor_scalar(rstd[:, t, :], mv[:, t, 1:2], LN_EPS, None, ALU.add))
                nc.gpsimd.tensor_tensor(rstd[:, t, :], rstd[:, t, :], minus_half[:, 0:1], ALU.pow).then_inc(ln_rstd, 1)

        def ln_apply(dve, s, t):
            dve.wait_ge(ln_rstd, NT * s + t + 1)
            nc.vector.tensor_scalar(XN[:, t, :], X[:, t, :], mv[:, t, 0:1], rstd[:, t, :],
                                    ALU.subtract, ALU.mult).then_inc(xn_ready, 1)

        def layer_norm(dve, own, s):
            for t in range(NT):
                ln_stats(dve, own, s, t)
                if t >= 1:
                    ln_apply(dve, s, t - 1)
            ln_apply(dve, s, NT - 1)

        def transposes(pe, s):
            if s == 0:
                pe.wait_ge(consts, CONSTS)
            for t in range(NT):
                pe.wait_ge(xn_ready, NT * s + t + 1)
                if t >= 2:
                    pe.wait_ge(xt_ready, NT * s + t - 1)
                for k in range(KC):
                    last = nc.tensor.transpose(PS[:, 6 + t % 2, k * P:k * P + P], XN[:, t, k * P:k * P + P], ident[:, :])
                last.then_inc(tr_done, 1)

        def xt_copies(act, s):
            for t in range(NT):
                act.wait_ge(tr_done, NT * s + t + 1)
                nc.scalar.copy(XT[:, :, t * P:t * P + P],
                               PS[:, 6 + t % 2, :].rearrange("p (k n) -> p k n", k=KC)).then_inc(xt_ready, 1)

        def add_bias(pool, s, bias, loaded, n):
            pool.wait_ge(loaded, n)
            for t in range(NT):
                pool.wait_ge(xn_ready, NT * s + t + 1)
                nc.gpsimd.tensor_tensor(X[:, t, :], X[:, t, :], bias[:, :], ALU.add).then_inc(x_bias, 1)

        KV = {ATTN_A: 8, ATTN_M: 1}
        DMA = 16
        att_names = ["prj_ps", "hi", "rest", "mid", "lo", "v_ps", "v_sb", "fill", "ring", "nm3", "st", "exp",
                     "pv", "o_sb", "rden", "norm"]
        am = {s: {n: sem(f"{n}{s}") for n in att_names} for s in KV}
        for s in KV:
            am[s].update(w=sem(f"at_w{s}"), ones=sem(f"ones{s}"), spl_out=[sem(f"spl_out{s}{i}") for i in range(2)],
                         back=[sem(f"back{s}{b}") for b in range(BATCH)], mt_in=[sem(f"mt_in{s}{i}") for i in range(2)],
                         o_in=[sem(f"o_in{s}{i}") for i in range(2)])
        split_q = {s: nc.dram_tensor(f"split_q{s}", [3, DIM, TOK], BF16, kind="Internal").ap() for s in KV}
        split_k = {s: nc.dram_tensor(f"split_k{s}", [3, KV[s] * HD, TOK], BF16, kind="Internal").ap() for s in KV}
        a_wo_sb = at(0, 2048).rearrange("p (k n) -> p k n", k=KC)
        a_wq_sb = at(2048, 2048).rearrange("p (k n) -> p k n", k=KC)
        a_wk_sb = at(4096, 512).rearrange("p (k n) -> p k n", k=KC)
        a_wv_sb = at(4608, 512).rearrange("p (k n) -> p k n", k=KC)
        o_raw = at(35840, 2048).rearrange("p (r n) -> p r n", r=4)
        den = at(2048, 1024).rearrange("p (r n) -> p r n", r=2)
        mt = at(3072, 512).bitcast(BF16).rearrange("p (r n) -> p r n", r=2)
        nmf = sb("nmf", [P, 4, 16])
        nmr = sb("nmr", [P, 4, 16])
        nm3 = sb("nm3", [P, 4, 3, 16], BF16)
        Q6 = at(5120, 16384).bitcast(BF16).rearrange("p (h n) -> p h n", h=HEADS)
        K6 = at(21504, 4096).bitcast(BF16).rearrange("p (g n) -> p g n", g=8)
        V = at(25600, 2048).rearrange("p (t g d) -> p t g d", t=NT, g=8)
        PT = at(27648, 4096).rearrange("p (r h n) -> p r h n", r=2, h=4)
        spl = at(27648, 1536).bitcast(BF16).rearrange("p (r k n) -> p r k n", r=2, k=3)
        rest = at(29184, 1024).rearrange("p (r n) -> p r n", r=2)
        OT = at(31744, 4096).rearrange("p (m n) -> p m n", m=KC)
        GH = 16
        GROUPS = BATCH * HEADS // GH
        FILLS = [(qt, h, n) for h4 in range(0, GH, 4) for qt, n in ((0, 4), (1, 2), (2, 1), (3, 1))
                 for h in range(h4, h4 + 4, n)]
        PROJ = [("k", 0, 0), ("k", 0, 1)] + [("q", m, b) for b in range(BATCH) for m in range(KC)]
        BACK = {ATTN_A: [6 + 6 * KC, 6 * KC], ATTN_M: [6 + 6 * KC, 6 * KC]}

        def attention_steps():
            steps = [("proj", i) for i in range(2 + KC)] + [("v", 0)]
            late = [("proj", 2 + KC + i) for i in range(KC)]
            for f in range(len(FILLS)):
                if f % 11 == 0:
                    steps.append(late.pop(0))
                steps.append(("fill", 0, f))
            steps.append(("nmt", 0))
            outs0 = [("out", t) for t in range(NTB)]
            per = GH // 4 * 8
            for g in range(GROUPS):
                f = 0
                for u in range(per):
                    steps.append(("st", g * per + u))
                    if u % 2 and g * per + u >= 3:
                        steps.append(("pv", (g * per + u - 3) // 2))
                        if (g * per + u - 3) // 2 % 8 == 1 and (g * per + u - 3) // 16 >= 1:
                            steps.append(("norm", (g * per + u - 3) // 16 - 1))
                    while g + 1 < GROUPS and f < len(FILLS) and f < 2.2 * (u + 1):
                        steps.append(("fill", g + 1, f))
                        f += 1
                    if g + 1 < GROUPS and u == 22:
                        steps.append(("nmt", g + 1))
                    if g == 2 and u % 4 == 0 and u >= 8 and outs0:
                        steps.append(outs0.pop(0))
            last = GROUPS * per // 2 - 1
            steps += [("pv", last), ("norm", last // 8)] + [("out", NTB + t) for t in range(NTB)]
            return steps

        STEPS = attention_steps()
        RING = [x for x in STEPS if x[0] in ("fill", "nmt", "out")]

        ABANKS = (0, 1, 6)
        NA = len(ABANKS)
        OB = 7

        def ring_of(step):
            return RING.index(step)

        def attention_sp(sp, s):
            m, kv = am[s], KV[s]

            def send_back(i):
                kind, mm, b = PROJ[i]
                sp.wait_ge(m["spl_out"][i % 2], DMA * (i // 2 + 1))
                if kind == "k" and b == 0:
                    return
                if kind == "k":
                    src = split_k[s].rearrange("k (g d) n -> k d g n", d=HD)
                    for row, k in ((0, 0), (16, 1), (32, 2), (48, 0), (64, 1), (80, 0)):
                        sp.dma_start(K6[row:row + HD, 0:kv, :], src[k]).then_inc(m["back"][0], DMA)
                    return
                if i == 2:
                    sp.wait_ge(xt_ready, NT * s + NT)
                src = split_q[s][:, mm * P:mm * P + P, b * SEQ:b * SEQ + SEQ].rearrange("k (h d) n -> k d h n", d=HD)
                for row, k in ((0, 0), (16, 0), (32, 0), (48, 1), (64, 1), (80, 2)):
                    sp.dma_start(Q6[row:row + HD, HPC * mm:HPC * mm + HPC, b * SEQ:b * SEQ + SEQ],
                                 src[k]).then_inc(m["back"][b], DMA)

            for step in STEPS:
                if step[0] == "proj":
                    i = step[1]
                    kind, mm, b = PROJ[i]
                    rows = kv * HD if kind == "k" else P
                    dst = split_k[s] if kind == "k" else split_q[s][:, mm * P:mm * P + P, :]
                    sp.wait_ge(m["lo"], i + 1)
                    sp.dma_start(dst[:, :, b * SEQ:b * SEQ + SEQ].rearrange("k p n -> p k n"),
                                 spl[0:rows, i % 2, :, :]).then_inc(m["spl_out"][i % 2], DMA)
                    if i >= 1 and i != 2 + KC:
                        send_back(i - 1)
                    if i in (1 + KC, 1 + 2 * KC):
                        send_back(i)
                elif step[0] == "pv" and step[1] % 4 == 3:
                    i = step[1] // 4
                    b, hq = i // 8, i % 8
                    c = i // 2
                    sp.wait_ge(m["o_sb"], i + 1)
                    if c >= 2:
                        sp.wait_ge(m["norm"], c - 1)
                    for j in range(4):
                        r = hq % 2 * 64 + HD * j
                        sp.dma_start(OT[r:r + HD, hq // 2, b * SEQ:b * SEQ + SEQ],
                                     o_raw[32 * j:32 * j + HD, i % 4, :]).then_inc(m["o_in"][c % 2], DMA)
                        sp.dma_start(den[r:r + HD, c % 2, :],
                                     o_raw[32 * j + HD:32 * j + 2 * HD, i % 4, :]).then_inc(m["o_in"][c % 2], DMA)

        def attention_pe(pe, s):
            m, kv = am[s], KV[s]
            group = HEADS // kv
            pe.wait_ge(m["w"], 4 * DMA)
            pe.wait_ge(xt_ready, NT * s + NT)
            for step in STEPS:
                if step[0] == "proj":
                    i = step[1]
                    kind, mm, b = PROJ[i]
                    w = a_wk_sb[:, :, 0:kv * HD] if kind == "k" else a_wq_sb[:, :, mm * P:mm * P + P]
                    if i >= 4:
                        pe.wait_ge(m["rest"], i - 3)
                    for k in range(KC):
                        last = nc.tensor.matmul(PS[0:w.shape[2], 2 + i % 4, :], w[:, k, :], XT[:, k, b * SEQ:b * SEQ + SEQ],
                                                start=k == 0, stop=k == KC - 1)
                    last.then_inc(m["prj_ps"], 1)
                elif step[0] == "v":
                    for t in range(NT):
                        for k in range(KC):
                            last = nc.tensor.matmul(PS[:, 6 + t // 4, t % 4 * kv * HD:(t % 4 + 1) * kv * HD],
                                                    XT[:, k, t * P:t * P + P], a_wv_sb[:, k, 0:kv * HD],
                                                    start=k == 0, stop=k == KC - 1)
                        if t % 4 == 3:
                            last.then_inc(m["v_ps"], 1)
                elif step[0] == "fill":
                    g, f = step[1:]
                    b, h0 = g * GH // HEADS, g * GH % HEADS
                    a = ring_of(step)
                    if a == 0:
                        pe.wait_ge(m["v_sb"], 2)
                    if f == 0 and g in (0, GROUPS // 2):
                        pe.wait_ge(m["back"][b], DMA * BACK[s][b])
                    if a >= NA:
                        pe.wait_ge(m["ring"], a - NA + 1)
                    qt, h, n = FILLS[f]
                    w = (qt + 1) * P
                    for e in range(n):
                        hh = h0 + h + e
                        o = PS[:, ABANKS[a % NA], e * w:e * w + w]
                        q0 = b * SEQ + qt * P
                        nc.tensor.matmul(o, Q6[0:96, hh, q0:q0 + P], K6[0:96, hh // group, b * SEQ:b * SEQ + w],
                                         start=True, stop=False)
                        last = nc.tensor.matmul(o[:, qt * P:w], identb[:, :], mask_qk[:, :], start=False, stop=True)
                    last.then_inc(m["fill"], 1)
                elif step[0] == "nmt":
                    g = step[1]
                    a = ring_of(step)
                    pe.wait_ge(m["ring"], a - NA + 1)
                    pe.wait_ge(m["nm3"], g + 1)
                    o = PS[:, ABANKS[a % NA], :].bitcast(BF16)
                    for qt in range(4):
                        last = nc.tensor.transpose(o[0:48, qt * P:qt * P + P],
                                                   nm3[:, qt, :, :].rearrange("p k h -> p (k h)"), identb[:, :])
                    last.then_inc(m["fill"], 1)
                elif step[0] == "st":
                    u = step[1]
                    i, kt, pair = u // 8, u // 2 % 4, u % 2
                    b, hq = i // 8, i % 8
                    g = i // (GH // 4)
                    if u % (GH * 2) == 0:
                        pe.wait_ge(m["mt_in"][g % 2], DMA * 3 * (g // 2 + 1))
                    if u >= 2:
                        pe.wait_ge(m["exp"], u - 1)
                    k0, w = b * SEQ + kt * P, SEQ - kt * P
                    for e in range(2):
                        hh = 4 * hq + 2 * pair + e
                        o = PS[:, 2 + u % 2 * 2 + e, 0:w]
                        nc.tensor.matmul(o, K6[0:99, hh // group, k0:k0 + P], Q6[0:99, hh, k0:(b + 1) * SEQ],
                                         start=True, stop=False)
                        last = nc.tensor.matmul(o[:, 0:P], identb[:, :], mask_kq[:, :], start=False, stop=True)
                    last.then_inc(m["st"], 1)
                elif step[0] == "pv":
                    v = step[1]
                    i, kt = v // 4, v % 4
                    b, hq = i // 8, i % 8
                    pe.wait_ge(m["exp"], 2 * v + 2)
                    if v == 0:
                        pe.wait_ge(m["v_sb"], 2)
                        pe.wait_ge(m["ones"], 2)
                    if kt == 0 and i >= 1:
                        pe.wait_ge(m["o_sb"], i)
                    w = SEQ - kt * P
                    for j in range(4):
                        hh = 4 * hq + j
                        last = nc.tensor.matmul(PS[32 * j:32 * j + 32, OB, kt * P:SEQ],
                                                V[:, b * NTB + kt, hh // group, :], PT[:, v % 2, j, 0:w],
                                                start=kt == 0, stop=kt == 3, tile_position=(0, 32 * j))
                    last.then_inc(m["pv"], 1)
                elif step[0] == "out":
                    t = step[1]
                    a = ring_of(step)
                    pe.wait_ge(m["ring"], a - NA + 1)
                    pe.wait_ge(m["norm"], KC * (t // NTB + 1))
                    for k in range(KC):
                        last = nc.tensor.matmul(PS[:, ABANKS[a % NA], :], OT[:, k, t * P:t * P + P], a_wo_sb[:, k, :],
                                                start=k == 0, stop=k == KC - 1)
                    last.then_inc(m["fill"], 1)

        def attention_act(act, s):
            m, kv = am[s], KV[s]
            for step in STEPS:
                if step[0] == "proj":
                    i = step[1]
                    rows = kv * HD if PROJ[i][0] == "k" else P
                    act.wait_ge(m["prj_ps"], i + 1)
                    if i >= 2:
                        act.wait_ge(m["spl_out"][i % 2], DMA * (i // 2))
                    nc.scalar.copy(spl[0:rows, i % 2, 0, :], PS[0:rows, 2 + i % 4, :]).then_inc(m["hi"], 1)
                elif step[0] == "v":
                    for n in range(2):
                        act.wait_ge(m["v_ps"], n + 1)
                        src = PS[:, 6 + n, 0:4 * kv * HD].rearrange("p (t g d) -> p t g d", t=4, g=kv)
                        for t in range(4):
                            last = nc.scalar.copy(V[:, 4 * n + t, 0:kv, 0:HD], src[:, t, :, :])
                        last.then_inc(m["v_sb"], 1)
                elif step[0] == "st":
                    u = step[1]
                    kt, pair, v = u // 2 % 4, u % 2, u // 2
                    w = SEQ - kt * P
                    act.wait_ge(m["st"], u + 1)
                    if u == 0:
                        act.wait_ge(m["spl_out"][0], DMA * (len(PROJ) // 2))
                        act.wait_ge(m["spl_out"][1], DMA * (len(PROJ) // 2))
                    if v >= 2:
                        act.wait_ge(m["pv"], v - 1)
                    nc.scalar.activation(PT[:, v % 2, 2 * pair:2 * pair + 2, 0:w], PS[:, 2 + u % 2 * 2:4 + u % 2 * 2, 0:w],
                                         ACT.Exp, scale=SCALE).then_inc(m["exp"], 1)

        def attention_dve(dve, own, s):
            m, kv = am[s], KV[s]
            for step in STEPS:
                if step[0] == "proj":
                    i = step[1]
                    rows = kv * HD if PROJ[i][0] == "k" else P
                    dve.wait_ge(m["hi"], i + 1)
                    if i >= 2:
                        dve.wait_ge(m["lo"], i - 1)
                    nc.vector.tensor_tensor(rest[0:rows, i % 2, :], PS[0:rows, 2 + i % 4, :], spl[0:rows, i % 2, 0, :],
                                            ALU.subtract).then_inc(m["rest"], 1)
                elif step[0] == "fill":
                    g, f = step[1:]
                    a = ring_of(step)
                    qt, h, n = FILLS[f]
                    dve.wait_ge(m["fill"], a + 1)
                    red = nc.vector.tensor_reduce(nmf[:, qt, h:h + n],
                                                  PS[:, ABANKS[a % NA], 0:n * (qt + 1) * P].rearrange("p (h n) -> p h n", h=n),
                                                  AX.X, ALU.max, negate=True)
                    red.then_inc(m["ring"], 1)
                    if f == len(FILLS) - 1:
                        dve.wait_ge(m["ring"], a + 1)
                        if g >= 1:
                            dve.wait_ge(m["fill"], ring_of(("nmt", g - 1)) + 1)
                        own.done(nc.vector.tensor_copy(nm3[:, :, 0, :], nmf[:, :, :]))
                        own.done(nc.vector.tensor_tensor(nmr[:, :, :], nmf[:, :, :], nm3[:, :, 0, :], ALU.subtract))
                        own.done(nc.vector.tensor_copy(nm3[:, :, 1, :], nmr[:, :, :]))
                        nc.vector.tensor_tensor(nm3[:, :, 2, :], nmr[:, :, :], nm3[:, :, 1, :],
                                                ALU.subtract).then_inc(m["nm3"], 1)
                        dve.wait_ge(m["nm3"], g + 1)
                elif step[0] == "nmt":
                    g = step[1]
                    a = ring_of(step)
                    dve.wait_ge(m["fill"], a + 1)
                    if g == 0:
                        dve.wait_ge(m["rest"], len(PROJ))
                        dve.wait_ge(m["prj_ps"], len(PROJ))
                    if g >= 2:
                        dve.wait_ge(m["mt_in"][g % 2], DMA * 3 * (g // 2))
                    nc.vector.tensor_copy(mt[0:48, g % 2, :],
                                          PS[:, ABANKS[a % NA], :].bitcast(BF16)[0:48, 0:SEQ]).then_inc(m["ring"], 1)
                elif step[0] == "pv" and step[1] % 4 == 3:
                    i = step[1] // 4
                    dve.wait_ge(m["pv"], step[1] + 1)
                    if i >= 4:
                        dve.wait_ge(m["norm"], i // 2 - 1)
                    nc.vector.tensor_copy(o_raw[:, i % 4, :], PS[:, OB, :]).then_inc(m["o_sb"], 1)
                elif step[0] == "norm":
                    c = step[1]
                    dve.wait_ge(m["o_in"][c % 2], DMA * 16 * (c // 2 + 1))
                    nc.vector.reciprocal(den[:, c % 2, :], den[:, c % 2, :]).then_inc(m["rden"], 1)
                elif step[0] == "out":
                    t = step[1]
                    a = ring_of(step)
                    dve.wait_ge(m["fill"], a + 1)
                    nc.vector.tensor_tensor(X[:, t, :], X[:, t, :], PS[:, ABANKS[a % NA], :], ALU.add).then_inc(m["ring"], 1)
                    dve.wait_ge(m["ring"], a + 1)

        def attention_pool(pool, own, s):
            m, kv = am[s], KV[s]
            if s != ATTN_A:
                pool.wait_ge(xn_ready, NT * s + NT)
            nc.gpsimd.memset(V[:, :, 0:kv, HD:2 * HD], 1.0).then_inc(m["ones"], 1)
            pool.wait_ge(m["ones"], 1)
            nc.gpsimd.memset(K6[96:99, 0:kv, :], 1.0).then_inc(m["ones"], 1)
            pool.wait_ge(m["ones"], 2)
            for step in STEPS:
                if step[0] == "proj":
                    i = step[1]
                    rows = kv * HD if PROJ[i][0] == "k" else P
                    pool.wait_ge(m["rest"], i + 1)
                    nc.gpsimd.tensor_copy(spl[0:rows, i % 2, 1, :], rest[0:rows, i % 2, :]).then_inc(m["mid"], 1)
                    pool.wait_ge(m["mid"], i + 1)
                    nc.gpsimd.tensor_tensor(spl[0:rows, i % 2, 2, :], rest[0:rows, i % 2, :], spl[0:rows, i % 2, 1, :],
                                            ALU.subtract).then_inc(m["lo"], 1)
                elif step[0] == "nmt":
                    g = step[1]
                    b, h0 = g * GH // HEADS, g * GH % HEADS
                    pool.wait_ge(m["ring"], ring_of(step) + 1)
                    for k in range(3):
                        pool.dma_start(Q6[96 + k:97 + k, h0:h0 + GH, b * SEQ:b * SEQ + SEQ],
                                     mt[GH * k:GH * k + GH, g % 2, :]).then_inc(m["mt_in"][g % 2], DMA)
                elif step[0] == "norm":
                    c = step[1]
                    b, mm = c // KC, c % KC
                    pool.wait_ge(m["rden"], c + 1)
                    o = OT[:, mm, b * SEQ:b * SEQ + SEQ]
                    nc.gpsimd.tensor_tensor(o, o, den[:, c % 2, :], ALU.mult).then_inc(m["norm"], 1)

        ffn_names = ["h_ps", "h_sb", "hw", "hwt_ps", "hwt_sb", "logit", "exp"]
        fm = {s: {n: sem(f"{n}{s}") for n in ffn_names} for s in (FFN_0, FFN_1)}
        Hcat = at(27648, NT * FCAT).rearrange("p (t n) -> p t n", t=NT)
        HW = at(28736, NT * ER).rearrange("p (t n) -> p t n", t=NT)
        HWT = at(29760, NT * P).rearrange("p (t n) -> p t n", t=NT)
        rt = [at(30784 + 64 * i, 64).rearrange("p (t e) -> p t e", t=NT) for i in range(8)]
        r1 = [at(31296 + 8 * i, 8) for i in range(6)]

        def ffn_pe(pe, s):
            m = fm[s]
            pe.wait_ge(w_ffn, 4 * DMA)
            for t in range(NT):
                pe.wait_ge(xt_ready, NT * s + t + 1)
                if t >= 2:
                    pe.wait_ge(m["h_sb"], t - 1)
                for k in range(KC):
                    last = nc.tensor.matmul(PS[:, t % 2, 0:FCAT], XT[:, k, t * P:t * P + P], Wcat[:, k, :],
                                            start=k == 0, stop=k == KC - 1)
                last.then_inc(m["h_ps"], 1)

            def base(t):
                if t >= 3:
                    pe.wait_ge(x_done, NT * LINEAR[s] + t - 2)
                for k in range(KC):
                    nc.tensor.matmul(PS[:, 2 + t % 3, :], XT[:, k, t * P:t * P + P], Wf[:, k, :], start=k == 0, stop=False)

            base(0)
            base(1)
            for t in range(NT):
                pe.wait_ge(m["hw"], t + 1)
                if t == 0:
                    pe.wait_ge(m["h_sb"], NT)
                if t >= 2:
                    pe.wait_ge(m["hwt_sb"], t - 1)
                nc.tensor.transpose(PS[:, t % 2, 0:P], HW[:, t, :], ident[:, :]).then_inc(m["hwt_ps"], 1)
                if t + 2 < NT:
                    base(t + 2)
                pe.wait_ge(m["hwt_sb"], t + 1)
                nc.tensor.matmul(PS[:, 2 + t % 3, :], HWT[:, t, :], Wbt[:, :], start=False, stop=True).then_inc(out_ps, 1)

        def ffn_act(act, s):
            m = fm[s]
            for t in range(NT):
                act.wait_ge(m["h_ps"], t + 1)
                nc.scalar.copy(Hcat[:, t, :], PS[:, t % 2, 0:FCAT]).then_inc(m["h_sb"], 1)
            act.wait_ge(m["logit"], 1)
            nc.scalar.activation(rt[1], rt[0], ACT.Exp).then_inc(m["exp"], 1)
            for t in range(NT):
                act.wait_ge(m["hwt_ps"], t + 1)
                nc.scalar.copy(HWT[:, t, :], PS[:, t % 2, 0:P]).then_inc(m["hwt_sb"], 1)

        def ffn_dve(dve, own, s):
            m = fm[s]
            bc = lambda v: v.unsqueeze(2).broadcast_to([P, NT, EXPERTS])
            dve.wait_ge(m["h_sb"], NT)
            logit, e, p, c1, oh1, p2, c2, oh2 = rt
            mx, sm, m1, k1, m2, k2 = r1
            TT, TR, TS = nc.vector.tensor_tensor, nc.vector.tensor_reduce, nc.vector.tensor_scalar
            rank = rank8[:, :].unsqueeze(1).broadcast_to([P, NT, EXPERTS])
            own.done(TR(mx, Hcat[:, :, ER:FCAT], AX.X, ALU.max))
            TT(logit, Hcat[:, :, ER:FCAT], bc(mx), ALU.subtract).then_inc(m["logit"], 1)
            dve.wait_ge(m["exp"], 1)
            own.done(TR(sm, e, AX.X, ALU.add))
            own.done(nc.vector.reciprocal(sm, sm))
            own.done(TT(p, e, bc(sm), ALU.mult))
            own.done(TR(m1, p, AX.X, ALU.max))
            own.done(TT(c1, p, bc(m1), ALU.is_equal))
            own.done(TT(c1, c1, rank, ALU.mult))
            own.done(TR(k1, c1, AX.X, ALU.max))
            own.done(TT(oh1, c1, bc(k1), ALU.is_equal))
            own.done(nc.vector.scalar_tensor_tensor(p2, oh1, -2.0, p, ALU.mult, ALU.add))
            own.done(TR(m2, p2, AX.X, ALU.max))
            own.done(TT(c2, p2, bc(m2), ALU.is_equal))
            own.done(TT(c2, c2, rank, ALU.mult))
            own.done(TR(k2, c2, AX.X, ALU.max))
            own.done(TT(oh2, c2, bc(k2), ALU.is_equal))
            own.done(TT(sm, m1, m2, ALU.add))
            own.done(nc.vector.reciprocal(sm, sm))
            own.done(TT(m1, m1, sm, ALU.mult))
            own.done(TT(m2, m2, sm, ALU.mult))
            own.done(TT(oh1, oh1, bc(m1), ALU.mult))
            own.done(TT(oh2, oh2, bc(m2), ALU.mult))
            own.done(TT(oh1, oh1, oh2, ALU.add))
            for t in range(NT):
                nc.vector.tensor_tensor(HW[:, t, :].rearrange("p (e r) -> p e r", e=EXPERTS),
                                        Hcat[:, t, 0:ER].rearrange("p (e r) -> p e r", e=EXPERTS),
                                        oh1[:, t, :].unsqueeze(2).broadcast_to([P, EXPERTS, LORA]),
                                        ALU.mult).then_inc(m["hw"], 1)

        def add_outputs(dve, own, s, banks, nxt):
            for t in range(NT):
                dve.wait_ge(out_ps, NT * LINEAR[s] + t + 1)
                dve.wait_ge(x_bias, NT * LINEAR[s] + t + 1)
                nc.vector.tensor_tensor(X[:, t, :], X[:, t, :], PS[:, banks[t % len(banks)], :], ALU.add).then_inc(x_done, 1)
                dve.wait_ge(x_done, NT * LINEAR[s] + t + 1)
                if nxt is not None:
                    ln_stats(dve, own, nxt, t)
                    if t >= 1:
                        ln_apply(dve, nxt, t - 1)
            if nxt is not None:
                ln_apply(dve, nxt, NT - 1)

        qz_sb = at(9216, 256).bitcast(I32).rearrange("p (g c) -> p g c", g=4)
        zeros = at(9472, 2048).bitcast(I32).rearrange("p (g n) -> p g n", g=4)
        qw_sb = at(11520, 2048).bitcast(I32).rearrange("p (g n) -> p g n", g=4)
        sc_sb = at(13568, 2048).rearrange("p (g n) -> p g n", g=4)
        shift = sb("shift", [P, 1], I32)
        part = sb("part", [P, 1], I32)

        def quant_loads(sp):
            src = g_qw.rearrange("(g q) n -> q g n", g=4)
            for q in range(16):
                sp.dma_start(qw_sb[8 * q:8 * q + 8, :, :], src[q, :, :].partition_broadcast(8)).then_inc(w_quant, DMA)
            sp.dma_start(qz_sb, g_qz.partition_broadcast(P)).then_inc(w_quant, DMA)
            sp.dma_start(sc_sb, g_sc.partition_broadcast(P)).then_inc(w_quant, DMA)

        def dequantise(dve, own):
            dve.wait_ge(consts, CONSTS)
            own.done(nc.vector.tensor_scalar(shift[:, :], part[:, :], 7, 2, ALU.bitwise_and, ALU.logical_shift_left))
            dve.wait_ge(w_quant, 19 * DMA)
            own.done(nc.vector.tensor_scalar(qw_sb, qw_sb, shift[:, 0:1], 15, ALU.arith_shift_right, ALU.bitwise_and))
            z8 = zeros.rearrange("p g (c s) -> p g c s", s=8)
            for j in range(8):
                own.done(nc.vector.tensor_scalar(z8[:, :, :, j], qz_sb, 4 * j, 15, ALU.arith_shift_right, ALU.bitwise_and))
            own.done(nc.vector.tensor_tensor(Wg[:, :, :], qw_sb, zeros, ALU.subtract))
            nc.vector.tensor_tensor(Wg[:, :, :], Wg[:, :, :], sc_sb, ALU.mult).then_inc(wg_ready, 1)

        def quant_pe(pe, s):
            pe.wait_ge(wg_ready, 1)
            for t in range(NT):
                pe.wait_ge(xt_ready, NT * s + t + 1)
                if t >= 4:
                    pe.wait_ge(x_done, NT * LINEAR[s] + t - 3)
                for k in range(KC):
                    last = nc.tensor.matmul(PS[:, t % 4, :], XT[:, k, t * P:t * P + P], Wg[:, k, :],
                                            start=k == 0, stop=k == KC - 1)
                last.then_inc(out_ps, 1)

        ms_names = ["par", "wout", "prj_ps", "prj_free", "th", "xs", "ss_ps", "ss_sb", "ms", "rs", "ssn", "sst_ps", "sst",
                    "bc_out", "ex", "w1", "ln", "dt", "dA", "scn", "u", "hc", "y", "tz", "yg", "par2", "aexp", "amin", "r"]
        mm_ = {n: sem(f"m_{n}") for n in ms_names}
        win_in = [sem(f"win_in{i}") for i in range(3)]
        bc_in = [sem(f"bc_in{i}") for i in range(4)]
        Wout = at(0, 4096).rearrange("p (k n) -> p k n", k=DTILES)
        Wx = at(4096, 512).rearrange("p (k n) -> p k n", k=DTILES)
        par = at(4608, 32 + 3 * 8 + 128)
        convw = par[:, 0:32].rearrange("p (i j) -> p i j", i=DTILES)
        convb, bdt, Dp = par[:, 32:40], par[:, 40:48], par[:, 48:56]
        Aneg = par[:, 56:184].rearrange("p (i n) -> p i n", i=DTILES)
        win = at(5120, 1536).rearrange("p (r k n) -> p r k n", r=3, k=KC)
        Wdt = at(6656, 1024)
        dtu = at(7680, 1024).rearrange("p (r n) -> p r n", r=2)
        tz = at(8704, 512)
        xs = at(9216, 4096).rearrange("p (i n) -> p i n", i=DTILES)
        dt_ = at(13312, 4096).rearrange("p (i n) -> p i n", i=DTILES)
        Bbc = at(17408, 8192).rearrange("p (n t) -> p n t", n=NSTATE)
        Cbc = at(25600, 8192).rearrange("p (n t) -> p n t", n=NSTATE)
        U = 4
        ub = at(33792, 4096).rearrange("p (r n t) -> p r n t", r=U, n=2)
        tmp = at(33792, 4096).rearrange("p (r k n) -> p r k n", r=2, k=4)
        ss_sb = at(4800, 256).rearrange("p (t n) -> p t n", t=NTB)
        sq_sb = at(7680, 256).rearrange("p (t n) -> p t n", t=NTB)
        gs = sb("gs", [P, NTB, 4])
        ssT = at(8704, 512)[0:64, :]
        bc_dram = nc.dram_tensor("bc_dram", [BATCH, 2 * NSTATE, SEQ], F32, kind="Internal").ap()
        PER = 3 * DTILES + NTB
        NCH = NSTATE // 2

        def mamba_sp(sp):
            m = mm_
            sp.wait_ge(out_ps, NT * LINEAR[FFN_0] + NT)
            sp.dma_start(convw, m_convw.rearrange("(i p) j -> p i j", p=P)).then_inc(m["par"], DMA)
            for dst, v in ((convb, m_convb), (bdt, m_bdt), (Dp, m_d)):
                sp.dma_start(dst, v.rearrange("(i p) -> p i", p=P), allow_slow_non_contiguous=True).then_inc(m["par"], DMA)
            sp.dma_start(Aneg, m_alog.rearrange("(i p) n -> p i n", p=P)).then_inc(m["par"], DMA)
            sp.dma_start(Wx, m_wx.rearrange("(k p) n -> p k n", p=P)).then_inc(m["par"], DMA)
            sp.dma_start(Wout, m_wout.rearrange("(k p) n -> p k n", p=P)).then_inc(m["par"], DMA)
            sp.wait_ge(tr_done, NT * MAMBA + NT)
            sp.dma_start(Wdt[0:DT_RANK, :], m_wdt).then_inc(m["par2"], DMA)

            def load_win(n):
                b, j = n // 16, n % 16
                if n >= 3:
                    R = (n - 3) // 16 * PER + (n - 3) % 16 + (DTILES if (n - 3) % 16 >= DTILES else 0)
                    sp.wait_ge(m["prj_ps"], R + 1)
                sp.dma_start(win[:, n % 3, :, :],
                             m_win[:, j * P:j * P + P].rearrange("(k p) n -> p k n", p=P)).then_inc(win_in[n % 3], DMA)

            for b in range(BATCH):
                for j in range(DTILES + 3 if b == 0 else DTILES):
                    load_win(16 * b + j + (3 if b else 0))
                sp.wait_ge(m["sst"], b + 1)
                sp.dma_start(bc_dram[b, :, :], ssT[DT_RANK:64, :]).then_inc(m["bc_out"], DMA)
                sp.wait_ge(m["bc_out"], DMA * (b + 1))
                if b >= 1:
                    sp.wait_ge(m["hc"], NCH * DTILES * b)
                for q in range(4):
                    for k, dst in ((0, Bbc), (1, Cbc)):
                        sp.dma_start(dst[:, 4 * q:4 * q + 4, :],
                                     bc_dram[b, NSTATE * k + 4 * q:NSTATE * k + 4 * q + 4, :].partition_broadcast(P)
                                     ).then_inc(bc_in[q], DMA)
                for j in range(DTILES + 3, 2 * DTILES + 3):
                    if 16 * b + j < 32:
                        load_win(16 * b + j)

        def mamba_pe(pe):
            m = mm_
            pe.wait_ge(xt_ready, NT * MAMBA + NT)
            n = [0]

            def project(b, R):
                pe.wait_ge(win_in[n[0] % 3], DMA * (n[0] // 3 + 1))
                if R >= 2:
                    pe.wait_ge(m["prj_free"], R - 1)
                for k in range(KC):
                    last = nc.tensor.matmul(PS[:, 6 + R % 2, :], win[:, n[0] % 3, k, :], XT[:, k, b * SEQ:b * SEQ + SEQ],
                                            start=k == 0, stop=k == KC - 1)
                last.then_inc(m["prj_ps"], 1)
                n[0] += 1

            for b in range(BATCH):
                R0 = b * PER
                for i in range(DTILES):
                    project(b, R0 + i)
                pe.wait_ge(m["par"], 7 * DMA)
                pe.wait_ge(m["xs"], DTILES * (b + 1))
                if b:
                    pe.wait_ge(m["yg"], DTILES * b)
                for t in range(NTB):
                    for i in range(DTILES):
                        last = nc.tensor.matmul(PS[:, 4, 64 * t:64 * t + 64], xs[:, i, t * P:t * P + P], Wx[:, i, :],
                                                start=i == 0, stop=i == DTILES - 1)
                last.then_inc(m["ss_ps"], 1)
                pe.wait_ge(m["ssn"], b + 1)
                for t in range(NTB):
                    last = nc.tensor.transpose(PS[0:64, 5, t * P:t * P + P], ss_sb[:, t, :], ident[:, :])
                last.then_inc(m["sst_ps"], 1)
                pe.wait_ge(m["sst"], b + 1)
                pe.wait_ge(m["par2"], DMA)
                for i in range(DTILES):
                    R = R0 + DTILES + i
                    pe.wait_ge(m["prj_free"], R - 1)
                    nc.tensor.matmul(PS[:, 6 + R % 2, :], Wdt[0:DT_RANK, i * P:i * P + P], ssT[0:DT_RANK, :],
                                     start=True, stop=True).then_inc(m["prj_ps"], 1)
                for i in range(DTILES):
                    k = b * DTILES + i
                    project(b, R0 + 2 * DTILES + i)
                    if k >= 2:
                        pe.wait_ge(m["yg"], k - 1)
                    for c in range(NCH):
                        q = k * NCH + c
                        pe.wait_ge(m["hc"], q + 1)
                        for e in range(2):
                            last = nc.tensor.matmul(PS[:, 4 + k % 2, :], ident[:, :], ub[:, q % U, e, :],
                                                    start=c == 0 and e == 0, stop=c == NCH - 1 and e == 1)
                        last.then_inc(m["y"], 1)
                pe.wait_ge(m["yg"], DTILES * (b + 1))
                for t in range(NTB):
                    R = R0 + 3 * DTILES + t
                    pe.wait_ge(m["prj_free"], R - 1)
                    for i in range(DTILES):
                        last = nc.tensor.matmul(PS[:, 6 + R % 2, :], xs[:, i, t * P:t * P + P], Wout[:, i, :],
                                                start=i == 0, stop=i == DTILES - 1)
                    last.then_inc(m["prj_ps"], 1)

        def mamba_act(act, own):
            m = mm_
            act.wait_ge(m["amin"], 1)
            nc.scalar.activation(Aneg, Aneg, ACT.Exp).then_inc(m["aexp"], 1)
            for b in range(BATCH):
                R0 = b * PER
                for i in range(DTILES):
                    act.wait_ge(m["prj_free"], R0 + i + 1)
                    if i >= 2:
                        act.wait_ge(m["xs"], b * DTILES + i - 1)
                    nc.scalar.activation(tmp[:, i % 2, 0, :], xs[:, i, :], ACT.Tanh).then_inc(m["th"], 1)
                act.wait_ge(m["ss_ps"], b + 1)
                nc.scalar.copy(ss_sb[:, :, :], PS[:, 4, 0:256].rearrange("p (t n) -> p t n", t=NTB)).then_inc(m["ss_sb"], 1)
                act.wait_ge(m["sst_ps"], b + 1)
                nc.scalar.copy(ssT[:, :], PS[0:64, 5, :]).then_inc(m["sst"], 1)
                for i in range(DTILES + 1):
                    k = b * DTILES + i
                    if i < DTILES:
                        R = R0 + DTILES + i
                        act.wait_ge(m["prj_ps"], R + 1)
                        if i >= 2:
                            act.wait_ge(m["dt"], k - 1)
                        T = tmp[:, i % 2, 0, :]
                        own.done(nc.scalar.activation(T, PS[:, 6 + R % 2, :], ACT.Abs, bias=bdt[:, i:i + 1]))
                        nc.scalar.activation(dt_[:, i, :], PS[:, 6 + R % 2, :], ACT.Relu,
                                             bias=bdt[:, i:i + 1]).then_inc(m["prj_free"], 1)
                        nc.scalar.activation(T, T, ACT.Exp, scale=-1.0).then_inc(m["ex"], 1)
                    if i >= 1:
                        act.wait_ge(m["w1"], k - 1 + 2)
                        nc.scalar.activation(tmp[:, (i - 1) % 2, 2, :], tmp[:, (i - 1) % 2, 1, :], ACT.Ln).then_inc(m["ln"], 1)
                act.wait_ge(m["dt"], DTILES * (b + 1))
                act.wait_ge(m["bc_out"], DMA * (b + 1))
                for i in range(DTILES):
                    k = b * DTILES + i
                    for c in range(NCH):
                        q = k * NCH + c
                        if q >= 2:
                            act.wait_ge(m["scn"], q - 1)
                        for e in range(2):
                            last = nc.scalar.activation(PS[:, q % 2 * 2 + e, 1:SEQ], dt_[:, i, 1:SEQ], ACT.Exp,
                                                        scale=Aneg[:, i, 2 * c + e:2 * c + e + 1])
                        last.then_inc(m["dA"], 1)
                        if c == 2:
                            R = R0 + 2 * DTILES + i
                            act.wait_ge(m["prj_ps"], R + 1)
                            if k:
                                act.wait_ge(m["yg"], k)
                            nc.scalar.activation(tz, PS[:, 6 + R % 2, :], ACT.Tanh, scale=0.5).then_inc(m["tz"], 1)

        def mamba_pool(pool, own):
            m = mm_
            for b in range(BATCH):
                pool.wait_ge(m["ms"], b + 1)
                own.done(nc.gpsimd.tensor_scalar(gs[:, :, :], gs[:, :, :], RMS_EPS, None, ALU.add))
                nc.gpsimd.tensor_tensor(gs[:, :, :], gs[:, :, :], minus_half[:, :].rearrange("p (t k) -> p t k", t=NTB),
                                        ALU.pow).then_inc(m["rs"], 1)
                for i in range(DTILES):
                    k = b * DTILES + i
                    pool.wait_ge(m["dt"], DTILES * (b + 1))
                    own.done(nc.gpsimd.tensor_tensor(dtu[:, k % 2, :], dt_[:, i, :], xs[:, i, :], ALU.mult))
                    for c in range(NCH):
                        q = k * NCH + c
                        if i == 0 and c % 2 == 0:
                            pool.wait_ge(bc_in[c // 2], 2 * DMA * (b + 1))
                        if q >= U:
                            pool.wait_ge(m["y"], q - U + 1)
                        nc.gpsimd.tensor_tensor(ub[:, q % U, :, :], dtu[:, k % 2, :].unsqueeze(1).broadcast_to([P, 2, SEQ]),
                                                Bbc[:, 2 * c:2 * c + 2, :], ALU.mult).then_inc(m["u"], 1)

        def mamba_dve(dve, own):
            m = mm_
            TT, TS, STT = nc.vector.tensor_tensor, nc.vector.tensor_scalar, nc.vector.scalar_tensor_tensor
            dve.wait_ge(m["par"], 7 * DMA)
            TS(Aneg, Aneg, 86.0, None, ALU.min).then_inc(m["amin"], 1)
            dve.wait_ge(m["aexp"], 1)
            own.done(TS(Aneg, Aneg, -1.0, None, ALU.mult))
            own.done(TS(par[:, 0:40], par[:, 0:40], 0.5, None, ALU.mult))
            dve.wait_ge(xt_ready, NT * MAMBA + NT)
            nc.vector.memset(PS[:, 0:4, 0:1], 0.0).then_inc(m["w1"], 1)

            def silu(b, i):
                dve.wait_ge(m["th"], b * DTILES + i + 1)
                STT(xs[:, i, :], tmp[:, i % 2, 0, :], 1.0, xs[:, i, :], ALU.add, ALU.mult).then_inc(m["xs"], 1)

            for b in range(BATCH):
                R0 = b * PER
                for i in range(DTILES):
                    R = R0 + i
                    dve.wait_ge(m["prj_ps"], R + 1)
                    ps = PS[:, 6 + R % 2, :]
                    own.done(TS(xs[:, i, :], ps, convw[:, i, 3:4], convb[:, i:i + 1], ALU.mult, ALU.add))
                    for j in (2, 1):
                        own.done(STT(xs[:, i, 3 - j:SEQ], ps[:, 0:SEQ - 3 + j], convw[:, i, j:j + 1], xs[:, i, 3 - j:SEQ],
                                     ALU.mult, ALU.add))
                    STT(xs[:, i, 3:SEQ], ps[:, 0:SEQ - 3], convw[:, i, 0:1], xs[:, i, 3:SEQ],
                        ALU.mult, ALU.add).then_inc(m["prj_free"], 1)
                    if i:
                        silu(b, i - 1)
                silu(b, DTILES - 1)
                dve.wait_ge(m["ss_sb"], b + 1)
                own.done(TT(sq_sb[:, :, :], ss_sb[:, :, :], ss_sb[:, :, :], ALU.mult))
                own.done(nc.vector.tensor_reduce(gs[:, :, :], sq_sb[:, :, :].rearrange("p t (k n) -> p t k n", k=4), AX.X, ALU.add))
                own.done(TT(gs[:, :, 0], gs[:, :, 0], gs[:, :, 1], ALU.add))
                own.done(TS(gs[:, :, 0], gs[:, :, 0], 0.5, None, ALU.mult))
                own.done(nc.vector.tensor_copy(gs[:, :, 1], gs[:, :, 0]))
                TS(gs[:, :, :], gs[:, :, :], 1.0 / NSTATE, None, ALU.mult).then_inc(m["ms"], 1)
                dve.wait_ge(m["rs"], b + 1)
                TT(ss_sb[:, :, :].rearrange("p t (k n) -> p t k n", k=4), ss_sb[:, :, :].rearrange("p t (k n) -> p t k n", k=4),
                   gs[:, :, :].unsqueeze(3).broadcast_to([P, NTB, 4, 16]), ALU.mult).then_inc(m["ssn"], 1)
                for i in range(DTILES + 1):
                    k = b * DTILES + i
                    if i < DTILES:
                        dve.wait_ge(m["ex"], k + 1)
                        e, w, _, r = [tmp[:, i % 2, x, :] for x in range(4)]
                        TS(w, e, 1.0, None, ALU.add).then_inc(m["w1"], 1)
                        dve.wait_ge(m["w1"], k + 2)
                        STT(r, w, 1.0, e, ALU.subtract, ALU.subtract).then_inc(m["r"], 1)
                    if i >= 1:
                        e, w, l, r = [tmp[:, (i - 1) % 2, x, :] for x in range(4)]
                        dve.wait_ge(m["ln"], k)
                        dve.wait_ge(m["r"], k)
                        own.done(TT(l, l, r, ALU.subtract))
                        TT(dt_[:, i - 1, :], dt_[:, i - 1, :], l, ALU.add).then_inc(m["dt"], 1)
                for i in range(DTILES):
                    k = b * DTILES + i
                    for c in range(NCH + 1):
                        q = k * NCH + c
                        if c < NCH:
                            v = ub[:, q % U, :, :].rearrange("p n t -> p (n t)")
                            dve.wait_ge(m["dA"], q + 1)
                            dve.wait_ge(m["u"], q + 1)
                            nc.vector.tensor_tensor_scan(v, PS[:, q % 2 * 2:q % 2 * 2 + 2, :].rearrange("p n t -> p (n t)"), v,
                                                         0.0, ALU.mult, ALU.add).then_inc(m["scn"], 1)
                        if c >= 1:
                            dve.wait_ge(m["scn"], q)
                            TT(ub[:, (q - 1) % U, :, :], ub[:, (q - 1) % U, :, :], Cbc[:, 2 * c - 2:2 * c, :],
                               ALU.mult).then_inc(m["hc"], 1)
                    R = R0 + 2 * DTILES + i
                    dve.wait_ge(m["tz"], k + 1)
                    STT(tz, tz, 1.0, PS[:, 6 + R % 2, :], ALU.add, ALU.mult).then_inc(m["prj_free"], 1)
                    dve.wait_ge(m["y"], NCH * (k + 1))
                    dve.wait_ge(m["prj_free"], R + 1)
                    own.done(STT(xs[:, i, :], xs[:, i, :], Dp[:, i:i + 1], PS[:, 4 + k % 2, :], ALU.mult, ALU.add))
                    STT(xs[:, i, :], xs[:, i, :], 0.5, tz, ALU.mult, ALU.mult).then_inc(m["yg"], 1)
                for t in range(NTB):
                    R = R0 + 3 * DTILES + t
                    dve.wait_ge(m["prj_ps"], R + 1)
                    TT(X[:, b * NTB + t, :], X[:, b * NTB + t, :], PS[:, 6 + R % 2, :], ALU.add).then_inc(m["prj_free"], 1)
                    dve.wait_ge(m["prj_free"], R + 1)

        hs_names = ["w", "zero", "prj_ps", "stg", "q_in", "k_in", "v_in", "vt", "s_ps", "sub", "ex", "rs", "p", "pt",
                    "o_ps", "ct", "ct_ps", "res"]
        hm = {n: sem(f"h_{n}") for n in hs_names}
        h_out = [sem(f"h_out{i}") for i in range(2)]
        HALF = P
        HM = 4096
        split_h = nc.dram_tensor("heads_qkv", [3, DIM, TOK], F32, kind="Internal").ap()
        QKV = [at(2 * HM * i, 2 * HM).rearrange("p (h t) -> p h t", h=HEADS) for i in range(3)]
        token_head = lambda off: at(off, HM).rearrange("p (t g) -> p t g", t=HALF)
        VG = [token_head(6 * HM), token_head(2 * HM)]
        PRT = [token_head(8 * HM), token_head(3 * HM)]
        PR = token_head(7 * HM)
        CT = [token_head(0), token_head(HM)]
        hwv, stg = at(6 * HM, 2048), at(6 * HM + 2048, 1024).rearrange("p (r n) -> p r n", r=2)
        hw = [w.rearrange("p (k n) -> p k n", k=KC) for w in (at(8 * HM, 2048), at(8 * HM + 2048, 2048), hwv)]
        hmax = at(9 * HM, HALF)
        hsum = at(9 * HM + HALF, HALF)
        hb = at(9 * HM + 2 * HALF, 3 * KC)
        BT = 512 // HEADS
        NB = HALF // BT
        HPROJ = [(i, b, mm) for i in range(3) for b in range(BATCH) for mm in range(KC)]
        NP = len(HPROJ)

        def heads_order():
            order = [("proj", i) for i in range(2 * NP // 3 + 3)]
            rest_ = [("proj", i) for i in range(2 * NP // 3 + 3, NP)]
            for e in range(NB):
                order.append(("s", e))
                if rest_:
                    order.append(rest_.pop(0))
            order += [("s", NB + e) for e in range(NB)] + [("pv", e) for e in range(NB)]
            for e in range(NB):
                order += [("pv", NB + e), ("ct", e)]
            return order + [("ct", NB + e) for e in range(NB)]

        def heads_sp(sp):
            m = hm
            sp.wait_ge(am[ATTN_M]["ring"], len(RING))
            for i, w in enumerate((h_wq, h_wk, h_wv)):
                sp.dma_start(hw[i], w.rearrange("(k p) n -> p k n", p=P)).then_inc(m["w"], DMA)
            sp.dma_start(hb, h_bias).then_inc(m["w"], DMA)
            for u, (i, b, mm) in enumerate(HPROJ):
                sp.wait_ge(m["stg"], u + 1)
                sp.dma_start(split_h[i, mm * P:mm * P + P, b * SEQ:b * SEQ + SEQ], stg[:, u % 2, :]).then_inc(h_out[u % 2], DMA)
                if mm < KC - 1:
                    continue
                for par in range(2):
                    sp.wait_ge(h_out[par], DMA * (u // 2 + 1))
                if i == 2:
                    sp.wait_ge(m["zero"], 1)
                elif i == 0:
                    sp.wait_ge(xt_ready, NT * ATTN_H + NT)
                for r in (2 * b, 2 * b + 1):
                    sp.dma_start(QKV[i][32 * r:32 * r + HD, :, :],
                                 split_h[i, :, r * 2 * HALF:(r + 1) * 2 * HALF].rearrange("(h d) t -> d h t", d=HD)
                                 ).then_inc(m[("q_in", "k_in", "v_in")[i]], DMA)

        def heads_pool(pool, own):
            m = hm
            pool.wait_ge(am[ATTN_M]["ring"], len(RING))
            nc.gpsimd.memset(QKV[2][:, :, :], 0.0).then_inc(m["zero"], 1)
            for e in range(2 * NB):
                pool.wait_ge(m["rs"], e + 1)
                sl = slice(e % NB * BT, e % NB * BT + BT)
                nc.gpsimd.tensor_tensor(PR[:, sl, :], PR[:, sl, :], hsum[:, sl].unsqueeze(2).broadcast_to([P, BT, HEADS]),
                                        ALU.mult).then_inc(m["p"], 1)

        def heads_pe(pe):
            m = hm
            pe.wait_ge(m["w"], 4 * DMA)
            for kind, u in heads_order():
                if kind == "proj":
                    i, b, mm = HPROJ[u]
                    pe.wait_ge(xt_ready, NT * ATTN_H + NTB * (b + 1))
                    if u >= 4:
                        pe.wait_ge(m["stg"], u - 3)
                    for k in range(KC):
                        last = nc.tensor.matmul(PS[:, u % 4, :], hw[i][:, k, mm * P:mm * P + P],
                                                XT[:, k, b * SEQ:b * SEQ + SEQ], start=k == 0, stop=k == KC - 1)
                    last.then_inc(m["prj_ps"], 1)
                elif kind == "s":
                    if u == 0:
                        pe.wait_ge(m["q_in"], 4 * DMA)
                        pe.wait_ge(m["k_in"], 4 * DMA)
                        pe.wait_ge(xt_ready, NT * ATTN_H + NT)
                    if u >= 4:
                        pe.wait_ge(m["sub"], u - 3)
                    for j in range(BT):
                        t = BT * u + j
                        for r in range(4):
                            last = nc.tensor.matmul(PS[32 * r:32 * r + 32, 4 + u % 4, j * HEADS:j * HEADS + HEADS],
                                                    QKV[0][32 * r:32 * r + HD, :, t], QKV[1][32 * r:32 * r + HD, :, t],
                                                    start=True, stop=True, tile_position=(32 * r, 32 * r))
                    last.then_inc(m["s_ps"], 1)
                elif kind == "pv":
                    hf, e = u // NB, u % NB
                    if u == 0:
                        pe.wait_ge(m["stg"], NP)
                    if e == 0:
                        pe.wait_ge(m["vt"], 4 * (hf + 1))
                    pe.wait_ge(m["pt"], u + 1)
                    if u >= 4:
                        pe.wait_ge(m["ct"], u - 3)
                    for j in range(BT):
                        t = BT * e + j
                        for r in range(4):
                            last = nc.tensor.matmul(PS[32 * r:32 * r + 32, u % 4, j * HEADS:j * HEADS + HEADS],
                                                    VG[hf][32 * r:32 * r + 32, t, :], PRT[hf][32 * r:32 * r + 32, t, :],
                                                    start=True, stop=True, tile_position=(32 * r, 32 * r))
                    last.then_inc(m["o_ps"], 1)
                else:
                    hf, n = u // NB, u % NB
                    if n == 0:
                        pe.wait_ge(m["ct"], NB * (hf + 1))
                    if u == 0:
                        pe.wait_ge(m["sub"], 2 * NB)
                    if u >= 4:
                        pe.wait_ge(m["res"], u - 3)
                    for h in range(4 * n, 4 * n + 4):
                        last = nc.tensor.transpose(PS[:, 4 + u % 4, h % 4 * P:h % 4 * P + P], CT[hf][:, :, h], ident[:, :])
                    last.then_inc(m["ct_ps"], 1)

        def heads_act(act):
            m = hm
            act.wait_ge(m["w"], 4 * DMA)
            for kind, u in heads_order():
                if kind == "proj":
                    i, b, mm = HPROJ[u]
                    act.wait_ge(m["prj_ps"], u + 1)
                    if u >= 2:
                        act.wait_ge(h_out[u % 2], DMA * (u // 2))
                    nc.scalar.activation(stg[:, u % 2, :], PS[:, u % 4, :], ACT.Identity,
                                         bias=hb[:, KC * i + mm:KC * i + mm + 1]).then_inc(m["stg"], 1)
                elif kind == "s":
                    act.wait_ge(m["sub"], u + 1)
                    sl = slice(u % NB * BT, u % NB * BT + BT)
                    nc.scalar.activation(PR[:, sl, :], PR[:, sl, :], ACT.Exp, scale=SCALE).then_inc(m["ex"], 1)
                elif kind == "pv":
                    act.wait_ge(m["o_ps"], u + 1)
                    if u == 0:
                        act.wait_ge(m["s_ps"], 2 * NB)
                    e = u % NB
                    nc.scalar.copy(CT[u // NB][:, e * BT:e * BT + BT, :], PS[:, u % 4, :].rearrange("p (t h) -> p t h", t=BT)
                                   ).then_inc(m["ct"], 1)

        def heads_dve(dve, own):
            m = hm
            TT, TR = nc.vector.tensor_tensor, nc.vector.tensor_reduce
            for hf in range(2):
                for e in range(NB + 1):
                    ee = hf * NB + e
                    if e < NB:
                        sl = slice(e * BT, e * BT + BT)
                        ps = PS[:, 4 + ee % 4, :].rearrange("p (t g) -> p t g", t=BT)
                        dve.wait_ge(m["s_ps"], ee + 1)
                        own.done(TR(hmax[:, sl], ps, AX.X, ALU.max, negate=True))
                        TT(PR[:, sl, :], ps, hmax[:, sl].unsqueeze(2).broadcast_to([P, BT, HEADS]), ALU.add).then_inc(m["sub"], 1)
                    if e >= 1:
                        sl = slice((e - 1) * BT, e * BT)
                        dve.wait_ge(m["ex"], ee)
                        own.done(TR(hsum[:, sl], PR[:, sl, :], AX.X, ALU.add))
                        nc.vector.reciprocal(hsum[:, sl], hsum[:, sl]).then_inc(m["rs"], 1)
                if hf == 0:
                    dve.wait_ge(m["prj_ps"], NP)
                    dve.wait_ge(h_out[0], DMA * NP // 2)
                    dve.wait_ge(h_out[1], DMA * NP // 2)
                    dve.wait_ge(m["v_in"], 4 * DMA)
                else:
                    dve.wait_ge(m["s_ps"], 2 * NB)
                for e in range(NB):
                    sl = slice(e * BT, e * BT + BT)
                    dve.wait_ge(m["p"], hf * NB + e + 1)
                    nc.vector.transpose(PRT[hf][:, sl, :], PR[:, sl, :]).then_inc(m["pt"], 1)
                    if e % 2:
                        sl, c = slice(e // 2 * 32, e // 2 * 32 + 32), hf * HALF + e // 2 * 32
                        nc.vector.transpose(VG[hf][:, sl, :],
                                            QKV[2][:, :, c:c + 32].rearrange("p h t -> p t h")).then_inc(m["vt"], 1)
                dve.wait_ge(m["pt"], NB * (hf + 1))
            for u in range(2 * NB):
                hf, n = u // NB, u % NB
                dve.wait_ge(m["ct_ps"], u + 1)
                src = PS[:, 4 + u % 4, :].rearrange("p (h r d) -> p h r d", h=4, r=4)
                for r in range(4):
                    dst = X[:, 2 * r + hf, 64 * n:64 * n + 64].rearrange("p (h d) -> p h d", h=4)
                    last = TT(dst, dst, src[:, :, r, 0:HD], ALU.add)
                last.then_inc(m["res"], 1)
            dve.wait_ge(m["res"], 2 * NB)

        CONSTS = 6
        block = ctx.enter_context(nc.Block())

        def attention_weights(sp, s, wq, wk, wv, wo):
            kw = wk.shape[1]
            for dst, w in ((a_wk_sb[:, :, 0:kw], wk), (a_wq_sb, wq), (a_wv_sb[:, :, 0:kw], wv), (a_wo_sb, wo)):
                sp.dma_start(dst, w.rearrange("(k p) n -> p k n", p=P)).then_inc(am[s]["w"], DMA)

        DONE = {1: (am[ATTN_A]["ring"], len(RING)), 2: (x_done, NT * LINEAR[FFN_0] + NT), 3: (mm_["prj_free"], 2 * PER),
                4: (x_done, NT * LINEAR[FFN_1] + NT), 5: (am[ATTN_M]["ring"], len(RING)), 6: (x_done, NT * LINEAR[QUANT_0] + NT), 7: (hm["res"], 16),
                8: (x_done, NT * LINEAR[QUANT_1] + NT)}

        @block.sync
        def _(sp):
            for b in range(BATCH):
                sp.dma_start(X[:, NTB * b:NTB * b + NTB, :],
                             x[b, :, :].rearrange("(t p) c -> p t c", p=P)).then_inc(x_loaded[b], DMA)
            attention_weights(sp, ATTN_A, a_wq, a_wk, a_wv, a_wo)
            for dst, w in ((Wf[:, :, :], f_wbase), (Wcat[:, :, :], f_cat)):
                sp.dma_start(dst, w.rearrange("(k p) n -> p k n", p=P)).then_inc(w_ffn, DMA)
            sp.dma_start(Wbt[:, :], f_bt).then_inc(w_ffn, DMA)
            sp.dma_start(bias_f[:, :], f_bias.partition_broadcast(P)).then_inc(w_ffn, DMA)
            sp.dma_start(bias_g[:, :], g_bias.partition_broadcast(P)).then_inc(w_quant, DMA)
            attention_sp(sp, ATTN_A)
            sp.wait_ge(am[ATTN_A]["exp"], 128)
            quant_loads(sp)
            mamba_sp(sp)
            sp.wait_ge(*DONE[3])
            attention_weights(sp, ATTN_M, q_wq, q_wk, q_wv, q_wo)
            attention_sp(sp, ATTN_M)
            heads_sp(sp)
            sp.wait_ge(*DONE[8])
            sp.dma_start(out[:, :, :].rearrange("b (t p) c -> p (b t) c", p=P), X[:, :, :]).then_inc(stored, DMA)
            sp.wait_ge(stored, DMA)

        @block.gpsimd
        def _(pool):
            own = Own(pool, pool_own)
            own.done(nc.gpsimd.memset(ident[:, :], 0.0))
            nc.gpsimd.affine_select(out=ident[:, :], in_=ident[:, :], compare_op=ALU.not_equal, fill=1.0, base=0,
                                    pattern=[[-1, P]], channel_multiplier=1).then_inc(consts, 1)
            own.done(nc.gpsimd.memset(identb[:, :], 0.0))
            nc.gpsimd.affine_select(out=identb[:, :], in_=identb[:, :], compare_op=ALU.not_equal, fill=1.0, base=0,
                                    pattern=[[-1, P]], channel_multiplier=1).then_inc(consts, 1)
            own.done(nc.gpsimd.memset(mask_qk[:, :], 0.0))
            nc.gpsimd.affine_select(out=mask_qk[:, :], in_=mask_qk[:, :], compare_op=ALU.is_ge, fill=NEG, base=0,
                                    pattern=[[-1, P]], channel_multiplier=1).then_inc(consts, 1)
            own.done(nc.gpsimd.memset(mask_kq[:, :], 0.0))
            nc.gpsimd.affine_select(out=mask_kq[:, :], in_=mask_kq[:, :], compare_op=ALU.is_ge, fill=NEG, base=0,
                                    pattern=[[1, P]], channel_multiplier=-1).then_inc(consts, 1)
            own.done(nc.gpsimd.memset(minus_half[:, :], -0.5))
            nc.gpsimd.iota(part[:, :], [[0, 1]], base=0, channel_multiplier=1).then_inc(consts, 1)
            for e in range(EXPERTS):
                own.done(nc.gpsimd.memset(rank8[:, e:e + 1], float(EXPERTS - e)))
            nc.gpsimd.memset(rank8[:, 0:1], float(EXPERTS)).then_inc(consts, 1)
            pool.wait_ge(consts, 6)
            ln_rstds(pool, own, ATTN_A)
            attention_pool(pool, own, ATTN_A)
            for s, bias, w, n in ((FFN_0, bias_f, w_ffn, 4 * DMA),):
                ln_rstds(pool, own, s)
                add_bias(pool, s, bias, w, n)
            ln_rstds(pool, own, MAMBA)
            mamba_pool(pool, own)
            ln_rstds(pool, own, FFN_1)
            add_bias(pool, FFN_1, bias_f, w_ffn, 4 * DMA)
            ln_rstds(pool, own, ATTN_M)
            attention_pool(pool, own, ATTN_M)
            ln_rstds(pool, own, QUANT_0)
            add_bias(pool, QUANT_0, bias_g, w_quant, 19 * DMA)
            ln_rstds(pool, own, ATTN_H)
            heads_pool(pool, own)
            ln_rstds(pool, own, QUANT_1)
            add_bias(pool, QUANT_1, bias_g, w_quant, 19 * DMA)

        @block.scalar
        def _(act):
            own = Own(act, act_own)
            xt_copies(act, ATTN_A)
            attention_act(act, ATTN_A)
            xt_copies(act, FFN_0)
            ffn_act(act, FFN_0)
            xt_copies(act, MAMBA)
            mamba_act(act, own)
            xt_copies(act, FFN_1)
            ffn_act(act, FFN_1)
            xt_copies(act, ATTN_M)
            attention_act(act, ATTN_M)
            xt_copies(act, QUANT_0)
            xt_copies(act, ATTN_H)
            heads_act(act)
            xt_copies(act, QUANT_1)

        @block.vector
        def _(dve):
            own = Own(dve, dve_own)
            layer_norm(dve, own, ATTN_A)
            attention_dve(dve, own, ATTN_A)
            layer_norm(dve, own, FFN_0)
            dequantise(dve, own)
            ffn_dve(dve, own, FFN_0)
            add_outputs(dve, own, FFN_0, (2, 3, 4), MAMBA)
            mamba_dve(dve, own)
            layer_norm(dve, own, FFN_1)
            ffn_dve(dve, own, FFN_1)
            add_outputs(dve, own, FFN_1, (2, 3, 4), ATTN_M)
            attention_dve(dve, own, ATTN_M)
            layer_norm(dve, own, QUANT_0)
            add_outputs(dve, own, QUANT_0, (0, 1, 2, 3), ATTN_H)
            heads_dve(dve, own)
            layer_norm(dve, own, QUANT_1)
            add_outputs(dve, own, QUANT_1, (0, 1, 2, 3), None)

        @block.tensor
        def _(pe):
            transposes(pe, ATTN_A)
            attention_pe(pe, ATTN_A)
            transposes(pe, FFN_0)
            ffn_pe(pe, FFN_0)
            transposes(pe, MAMBA)
            mamba_pe(pe)
            transposes(pe, FFN_1)
            ffn_pe(pe, FFN_1)
            transposes(pe, ATTN_M)
            attention_pe(pe, ATTN_M)
            transposes(pe, QUANT_0)
            quant_pe(pe, QUANT_0)
            transposes(pe, ATTN_H)
            heads_pe(pe)
            transposes(pe, QUANT_1)
            quant_pe(pe, QUANT_1)


def _laid_out(i):
    import numpy as np
    c = np.ascontiguousarray
    w = {k: np.asarray(v) for k, v in i.items()}
    head_cols = lambda b: b.reshape(KC, P).T
    return {
        "x": w["L0_attn_a_x"],
        "a_wq": w["L0_attn_a_wq"], "a_wk": w["L0_attn_a_wk"], "a_wv": w["L0_attn_a_wv"], "a_wo": w["L0_attn_a_wo"],
        "m_win": c(w["L0_attn_b_W_in"].T), "m_convw": w["L0_attn_b_conv_w"], "m_convb": w["L0_attn_b_conv_b"],
        "m_wx": c(w["L0_attn_b_W_x"].T), "m_wdt": c(w["L0_attn_b_W_dt"].T), "m_bdt": w["L0_attn_b_b_dt"],
        "m_alog": w["L0_attn_b_A_log"], "m_d": w["L0_attn_b_D"], "m_wout": c(w["L0_attn_b_W_out"].T),
        "f_wbase": c(w["L0_ffn_W_base"].T),
        "f_cat": c(np.concatenate([w["L0_ffn_A"].reshape(ER, DIM), w["L0_ffn_W_gate"]], 0).T),
        "f_bias": w["L0_ffn_b_base"], "f_bt": c(w["L0_ffn_B"].transpose(0, 2, 1).reshape(ER, DIM)),
        "q_wq": w["L1_attn_a_wq"], "q_wk": w["L1_attn_a_wk"], "q_wv": w["L1_attn_a_wv"], "q_wo": w["L1_attn_a_wo"],
        "h_wq": c(w["L1_attn_b_wq"].T), "h_wk": c(w["L1_attn_b_wk"].T), "h_wv": c(w["L1_attn_b_wv"].T),
        "h_bias": c(np.stack([head_cols(w["L1_attn_b_bq"]), head_cols(w["L1_attn_b_bk"]), head_cols(w["L1_attn_b_bv"])], 1).reshape(P, 3 * KC)),
        "g_qw": w["L1_ffn_qweight"], "g_qz": w["L1_ffn_qzeros"], "g_sc": w["L1_ffn_scales"], "g_bias": w["L1_ffn_bias"],
    }


def kernel(**inputs):
    import numpy as _np
    import concourse.bacc as _bacc
    from concourse import mybir as _mybir
    from concourse.bass_utils import run_bass_kernel_spmd as _run

    nc = _bacc.Bacc("TRN2", target_bir_lowering=False, num_devices=1)
    arrays = {f"in_{k}": _np.ascontiguousarray(v) for k, v in _laid_out(inputs).items()}
    args = [nc.dram_tensor(k, a.shape, _mybir.dt.from_np(a.dtype), kind="ExternalInput").ap() for k, a in arrays.items()]
    args.append(nc.dram_tensor("out_x", (BATCH, SEQ, DIM), _mybir.dt.float32, kind="ExternalOutput").ap())
    hybrid_kernel(nc, *args)
    r = _run(nc, [arrays], core_ids=[0])
    return r.results[0]["out_x"]
```

```python
import concourse.bass as bass
from concourse import mybir
from contextlib import ExitStack

F32 = mybir.dt.float32
BF16 = mybir.dt.bfloat16
I32 = mybir.dt.int32
ALU = mybir.AluOpType
ACT = mybir.ActivationFunctionType
AX = mybir.AxisListType

P = 128
BATCH, SEQ, DIM = 2, 512, 512
TOK = BATCH * SEQ
NT = TOK // P
NTB = NT // BATCH
KC = DIM // P
HEADS, HD = 32, 16
HPC = P // HD
D_IN, NSTATE, DT_RANK, CONV = 1024, 16, 32, 4
DTILES = D_IN // P
EXPERTS, LORA = 8, 16
ER = EXPERTS * LORA
FCAT = ER + EXPERTS
NEG = -1.0e30
SCALE = HD ** -0.5
LN_EPS, RMS_EPS = 1e-5, 1e-6


def hybrid_kernel(nc, x, a_wq, a_wk, a_wv, a_wo, m_win, m_convw, m_convb, m_wx, m_wdt, m_bdt, m_alog, m_d, m_group,
                  m_wout, f_wbase, f_cat, f_bias, f_bt, q_wq, q_wk, q_wv, q_wo, h_wq, h_wk, h_wv, h_bias,
                  g_qw, g_qz, g_sc, g_bias, out):
    ctx = ExitStack()
    with ctx:
        def sb(name, shape, dt=F32):
            return ctx.enter_context(nc.sbuf_tensor(name, shape, dt))

        def sem(name):
            return ctx.enter_context(nc.semaphore(name))

        X = sb("X", [P, NT, DIM])
        XT = sb("XT", [P, KC, TOK])
        Wg = sb("Wg", [P, KC, DIM])
        Wf = sb("Wf", [P, KC, DIM])
        Wcat = sb("Wcat", [P, KC, FCAT])
        Wbt = sb("Wbt", [P, DIM])
        bias_f = sb("bias_f", [P, DIM])
        bias_g = sb("bias_g", [P, DIM])
        ident = sb("ident", [P, P])
        identb = sb("identb", [P, P], BF16)
        mask_qk = sb("mask_qk", [P, P], BF16)
        mask_kq = sb("mask_kq", [P, P], BF16)
        bn = sb("bn", [P, NT, 6])
        mv = sb("mv", [P, NT, 2])
        rstd = sb("rstd", [P, NT, 1])
        minus_half = sb("minus_half", [P, NTB * 4])
        rank8 = sb("rank8", [P, EXPERTS])
        ARENA = 37888
        arena = sb("arena", [P, ARENA])

        def at(off, n, dt=F32):
            v = arena[:, off:off + n]
            return v if dt == F32 else v.bitcast(dt)

        XN = at(9216, 4096).rearrange("p (t c) -> p t c", t=NT)

        PS = ctx.enter_context(nc.psum_tensor("PS", [P, 8, 512], F32))

        ATTN_A, FFN_0, MAMBA, FFN_1, ATTN_M, QUANT_0, ATTN_H, QUANT_1 = range(8)

        x_loaded = [sem(f"x_loaded{i}") for i in range(NT // 2)]
        ln_stat = sem("ln_stat")
        ln_rstd = sem("ln_rstd")
        xn_ready = sem("xn_ready")
        tr_done = sem("tr_done")
        xt_ready = sem("xt_ready")
        out_ps = sem("out_ps")
        x_done = sem("x_done")
        x_bias = sem("x_bias")
        dve_own, pool_own, act_own = sem("dve_own"), sem("pool_own"), sem("act_own")
        consts = sem("consts")
        w_ffn, w_quant, wg_ready = sem("w_ffn"), sem("w_quant"), sem("wg_ready")
        stored = sem("stored")

        TR_BANK = {s: {FFN_1: 4, ATTN_H: 4, QUANT_1: 0}.get(s, 6) for s in range(8)}
        LINEAR = {FFN_0: 0, FFN_1: 1, QUANT_0: 2, QUANT_1: 3}

        class Own:

            def __init__(self, eng, s):
                self.eng, self.s, self.n = eng, s, 0

            def done(self, ins):
                self.n += 1
                ins.then_inc(self.s, 1)
                self.eng.wait_ge(self.s, self.n)

        def ln_stats(dve, own, s, t):
            if s == 0:
                dve.wait_ge(x_loaded[t // 2], 16)
            own.done(nc.vector.bn_stats(bn[:, t, :], X[:, t, :]))
            nc.vector.bn_aggr(mv[:, t, :], bn[:, t, :]).then_inc(ln_stat, 1)

        def ln_rstds(pool, own, s, tiles=range(NT)):
            for t in tiles:
                pool.wait_ge(ln_stat, NT * s + t + 1)
                own.done(nc.gpsimd.tensor_scalar(rstd[:, t, :], mv[:, t, 1:2], LN_EPS, None, ALU.add))
                nc.gpsimd.tensor_tensor(rstd[:, t, :], rstd[:, t, :], minus_half[:, 0:1], ALU.pow).then_inc(ln_rstd, 1)

        def ln_apply(dve, s, t):
            dve.wait_ge(ln_rstd, NT * s + t + 1)
            nc.vector.tensor_scalar(XN[:, t, :], X[:, t, :], mv[:, t, 0:1], rstd[:, t, :],
                                    ALU.subtract, ALU.mult).then_inc(xn_ready, 1)

        def layer_norm(dve, own, s):
            for t in range(NT):
                ln_stats(dve, own, s, t)
                if t >= 1:
                    ln_apply(dve, s, t - 1)
            ln_apply(dve, s, NT - 1)

        def transposes(pe, s, tiles):
            for t in tiles:
                pe.wait_ge(xn_ready, NT * s + t + 1)
                if t >= 2:
                    pe.wait_ge(xt_ready, NT * s + t - 1)
                for k in range(KC):
                    last = nc.tensor.transpose(PS[:, TR_BANK[s] + t % 2, k * P:k * P + P], XN[:, t, k * P:k * P + P], ident[:, :])
                last.then_inc(tr_done, 1)

        def xt_copies(act, s, tiles):
            for t in tiles:
                act.wait_ge(tr_done, NT * s + t + 1)
                nc.scalar.copy(XT[:, :, t * P:t * P + P],
                               PS[:, TR_BANK[s] + t % 2, :].rearrange("p (k n) -> p k n", k=KC)).then_inc(xt_ready, 1)

        def add_bias(pool, s, bias, loaded, n):
            pool.wait_ge(loaded, n)
            for t in range(NT):
                pool.wait_ge(xn_ready, NT * s + t + 1)
                nc.gpsimd.tensor_tensor(X[:, t, :], X[:, t, :], bias[:, :], ALU.add).then_inc(x_bias, 1)

        LAG = 2

        def transposes_behind(pe, nxt, t):
            if nxt is not None and t >= LAG:
                transposes(pe, nxt, (t - LAG,))

        KV = {ATTN_A: 8, ATTN_M: 1}
        DMA = 16
        att_names = ["prj_ps", "hi", "rest", "mid", "lo", "v_ps", "v_sb", "fill", "ring", "nm3", "st", "exp",
                     "pv", "o_sb", "rden", "norm"]
        am = {s: {n: sem(f"{n}{s}") for n in att_names} for s in KV}
        for s in KV:
            am[s].update(w=sem(f"at_w{s}"), ones=sem(f"ones{s}"), spl_out=[sem(f"spl_out{s}{i}") for i in range(2)],
                         back=[sem(f"back{s}{b}") for b in range(BATCH)], mt_in=[sem(f"mt_in{s}{i}") for i in range(2)],
                         o_in=[sem(f"o_in{s}{i}") for i in range(2)])
        split_q = {s: nc.dram_tensor(f"split_q{s}", [3, DIM, TOK], BF16, kind="Internal").ap() for s in KV}
        split_k = {s: nc.dram_tensor(f"split_k{s}", [3, KV[s] * HD, TOK], BF16, kind="Internal").ap() for s in KV}
        a_wo_sb = at(0, 2048).rearrange("p (k n) -> p k n", k=KC)
        a_wq_sb = at(2048, 2048).rearrange("p (k n) -> p k n", k=KC)
        a_wk_sb = at(4096, 512).rearrange("p (k n) -> p k n", k=KC)
        a_wv_sb = at(4608, 512).rearrange("p (k n) -> p k n", k=KC)
        o_raw = at(35840, 2048).rearrange("p (r n) -> p r n", r=4)
        den = at(2048, 1024).rearrange("p (r n) -> p r n", r=2)
        mt = at(4096, 512).bitcast(BF16).rearrange("p (r n) -> p r n", r=2)
        nmf = sb("nmf", [P, 4, 16])
        nmr = sb("nmr", [P, 4, 16])
        nm3 = sb("nm3", [P, 4, 3, 16], BF16)
        Q6 = at(5120, 16384).bitcast(BF16).rearrange("p (h n) -> p h n", h=HEADS)
        K6 = at(21504, 4096).bitcast(BF16).rearrange("p (g n) -> p g n", g=8)
        V = at(25600, 2048).rearrange("p (t g d) -> p t g d", t=NT, g=8)
        PT = at(27648, 4096).rearrange("p (r h n) -> p r h n", r=2, h=4)
        spl = at(33280, 1536).bitcast(BF16).rearrange("p (r k n) -> p r k n", r=2, k=3)
        rest = at(34816, 1024).rearrange("p (r n) -> p r n", r=2)
        OT = at(31744, 4096).rearrange("p (m n) -> p m n", m=KC)
        GH = 16
        GROUPS = BATCH * HEADS // GH
        FILLS = [(qt, h, n) for h4 in range(0, GH, 4) for qt, n in ((0, 4), (1, 2), (2, 1), (3, 1))
                 for h in range(h4, h4 + 4, n)]
        PROJ = [("k", 0, 0), ("k", 0, 1)] + [("q", m, b) for b in range(BATCH) for m in range(KC)]
        BACK = {ATTN_A: [6 + 6 * KC, 6 * KC], ATTN_M: [6 + 6 * KC, 6 * KC]}

        def attention_steps():
            steps = [("proj", i) for i in range(2 + KC)] + [("v", 0)]
            late = [("proj", 2 + KC + i) for i in range(KC)]
            steps += late[:2] + [("fill", 0, f) for f in range(len(FILLS))] + [("nmt", 0)] + late[2:]
            outs0 = [("out", t) for t in range(NTB)]
            per = GH // 4 * 8
            for g in range(GROUPS):
                f = 0
                for u in range(per):
                    steps.append(("st", g * per + u))
                    if u % 2 and g * per + u >= 3:
                        steps.append(("pv", (g * per + u - 3) // 2))
                        v = (g * per + u - 3) // 2
                        if v >= 8 and v % 8 in (3, 4, 5, 6):
                            steps.append(("rden", v // 8 - 1, v % 8 - 3))
                        if v >= 8 and v % 8 == 6:
                            steps.append(("norm", v // 8 - 1))
                    while g + 1 < GROUPS and f < len(FILLS) and f < 2 * (u + 1):
                        steps.append(("fill", g + 1, f))
                        f += 1
                    if g + 1 < GROUPS and u == 24:
                        steps.append(("nmt", g + 1))
                    if g == GROUPS - 1 and u % 6 == 0 and outs0:
                        steps.append(outs0.pop(0))
            last = GROUPS * per // 2 - 1
            steps += [("pv", last)] + [("early", NTB + t) for t in range(NTB)] + [("next", 0)]
            steps += [("rden", last // 8, j) for j in range(4)] + [("norm", last // 8)]
            steps += [("out", NTB + t) for t in range(NTB)]
            return steps

        STEPS = attention_steps()
        RING = [x for x in STEPS if x[0] in ("fill", "nmt", "out")]

        ABANKS = (0, 1, 6)
        NA = len(ABANKS)
        OB = 7

        def out_bank(t):
            return 2 + t - NTB if t >= NTB else ABANKS[ring_of(("out", t)) % NA]

        def ring_of(step):
            return RING.index(step)

        def attention_sp(sp, s):
            m, kv = am[s], KV[s]

            def send_back(i):
                kind, mm, b = PROJ[i]
                sp.wait_ge(m["spl_out"][i % 2], DMA * (i // 2 + 1))
                if kind == "k" and b == 0:
                    return
                if kind == "k":
                    src = split_k[s].rearrange("k (g d) n -> k d g n", d=HD)
                    for row, k in ((0, 0), (16, 1), (32, 2), (48, 0), (64, 1), (80, 0)):
                        sp.dma_start(K6[row:row + HD, 0:kv, :], src[k]).then_inc(m["back"][0], DMA)
                    return
                if i == 2:
                    sp.wait_ge(xt_ready, NT * s + NT)
                src = split_q[s][:, mm * P:mm * P + P, b * SEQ:b * SEQ + SEQ].rearrange("k (h d) n -> k d h n", d=HD)
                for row, k in ((0, 0), (16, 0), (32, 0), (48, 1), (64, 1), (80, 2)):
                    sp.dma_start(Q6[row:row + HD, HPC * mm:HPC * mm + HPC, b * SEQ:b * SEQ + SEQ],
                                 src[k]).then_inc(m["back"][b], DMA)

            for step in STEPS:
                if step[0] == "proj":
                    i = step[1]
                    kind, mm, b = PROJ[i]
                    rows = kv * HD if kind == "k" else P
                    dst = split_k[s] if kind == "k" else split_q[s][:, mm * P:mm * P + P, :]
                    sp.wait_ge(m["lo"], i + 1)
                    sp.dma_start(dst[:, :, b * SEQ:b * SEQ + SEQ].rearrange("k p n -> p k n"),
                                 spl[0:rows, i % 2, :, :]).then_inc(m["spl_out"][i % 2], DMA)
                    if i >= 1 and i != 2 + KC:
                        send_back(i - 1)
                    if i in (1 + KC, 1 + 2 * KC):
                        send_back(i)
                elif step[0] == "pv" and step[1] % 4 == 3:
                    i = step[1] // 4
                    b, hq = i // 8, i % 8
                    c = i // 2
                    sp.wait_ge(m["o_sb"], i + 1)
                    if c >= 2:
                        sp.wait_ge(m["norm"], c - 1)
                    for j in range(4):
                        r = hq % 2 * 64 + HD * j
                        sp.dma_start(OT[r:r + HD, hq // 2, b * SEQ:b * SEQ + SEQ],
                                     o_raw[32 * j:32 * j + HD, i % 4, :]).then_inc(m["o_in"][c % 2], DMA)
                        sp.dma_start(den[r:r + HD, c % 2, :],
                                     o_raw[32 * j + HD:32 * j + 2 * HD, i % 4, :]).then_inc(m["o_in"][c % 2], DMA)

        def attention_pe(pe, s, nxt):
            m, kv = am[s], KV[s]
            group = HEADS // kv
            pe.wait_ge(m["w"], 4 * DMA)
            for step in STEPS:
                if step[0] == "proj":
                    i = step[1]
                    kind, mm, b = PROJ[i]
                    if i < LAG:
                        transposes(pe, s, (NT - LAG + i,))
                    pe.wait_ge(xt_ready, NT * s + (NTB if i == 0 else NT))
                    w = a_wk_sb[:, :, 0:kv * HD] if kind == "k" else a_wq_sb[:, :, mm * P:mm * P + P]
                    if i >= 4:
                        pe.wait_ge(m["rest"], i - 3)
                    for k in range(KC):
                        last = nc.tensor.matmul(PS[0:w.shape[2], 2 + (i + 2) % 4, :], w[:, k, :], XT[:, k, b * SEQ:b * SEQ + SEQ],
                                                start=k == 0, stop=k == KC - 1)
                    last.then_inc(m["prj_ps"], 1)
                elif step[0] == "v":
                    for t in range(NT):
                        for k in range(KC):
                            last = nc.tensor.matmul(PS[:, 6 + t // 4, t % 4 * kv * HD:(t % 4 + 1) * kv * HD],
                                                    XT[:, k, t * P:t * P + P], a_wv_sb[:, k, 0:kv * HD],
                                                    start=k == 0, stop=k == KC - 1)
                        if t % 4 == 3:
                            last.then_inc(m["v_ps"], 1)
                elif step[0] == "fill":
                    g, f = step[1:]
                    b, h0 = g * GH // HEADS, g * GH % HEADS
                    a = ring_of(step)
                    if a == 0:
                        pe.wait_ge(m["v_sb"], 2)
                    if f == 0 and g in (0, GROUPS // 2):
                        pe.wait_ge(m["back"][b], DMA * BACK[s][b])
                    if a >= NA:
                        pe.wait_ge(m["ring"], a - NA + 1)
                    qt, h, n = FILLS[f]
                    w = (qt + 1) * P
                    for e in range(n):
                        hh = h0 + h + e
                        o = PS[:, ABANKS[a % NA], e * w:e * w + w]
                        q0 = b * SEQ + qt * P
                        nc.tensor.matmul(o, Q6[0:96, hh, q0:q0 + P], K6[0:96, hh // group, b * SEQ:b * SEQ + w],
                                         start=True, stop=False)
                        last = nc.tensor.matmul(o[:, qt * P:w], identb[:, :], mask_qk[:, :], start=False, stop=True)
                    last.then_inc(m["fill"], 1)
                elif step[0] == "nmt":
                    g = step[1]
                    a = ring_of(step)
                    pe.wait_ge(m["ring"], a - NA + 1)
                    pe.wait_ge(m["nm3"], g + 1)
                    o = PS[:, ABANKS[a % NA], :].bitcast(BF16)
                    for qt in range(4):
                        last = nc.tensor.transpose(o[0:48, qt * P:qt * P + P],
                                                   nm3[:, qt, :, :].rearrange("p k h -> p (k h)"), identb[:, :])
                    last.then_inc(m["fill"], 1)
                elif step[0] == "st":
                    u = step[1]
                    i, kt, pair = u // 8, u // 2 % 4, u % 2
                    b, hq = i // 8, i % 8
                    g = i // (GH // 4)
                    if u % (GH * 2) == 0:
                        pe.wait_ge(m["mt_in"][g % 2], DMA * 3 * (g // 2 + 1))
                    if u >= 2:
                        pe.wait_ge(m["exp"], u - 1)
                    else:
                        pe.wait_ge(m["rest"], len(PROJ) - 2 + 2 * u)
                    k0, w = b * SEQ + kt * P, SEQ - kt * P
                    for e in range(2):
                        hh = 4 * hq + 2 * pair + e
                        o = PS[:, 2 + u % 2 * 2 + e, 0:w]
                        nc.tensor.matmul(o, K6[0:99, hh // group, k0:k0 + P], Q6[0:99, hh, k0:(b + 1) * SEQ],
                                         start=True, stop=False)
                        last = nc.tensor.matmul(o[:, 0:P], identb[:, :], mask_kq[:, :], start=False, stop=True)
                    last.then_inc(m["st"], 1)
                elif step[0] == "pv":
                    v = step[1]
                    i, kt = v // 4, v % 4
                    b, hq = i // 8, i % 8
                    pe.wait_ge(m["exp"], 2 * v + 2)
                    if v == 0:
                        pe.wait_ge(m["v_sb"], 2)
                        pe.wait_ge(m["ones"], 2)
                    if kt == 0 and i >= 1:
                        pe.wait_ge(m["o_sb"], i)
                    w = SEQ - kt * P
                    for j in range(4):
                        hh = 4 * hq + j
                        last = nc.tensor.matmul(PS[32 * j:32 * j + 32, OB, kt * P:SEQ],
                                                V[:, b * NTB + kt, hh // group, :], PT[:, v % 2, j, 0:w],
                                                start=kt == 0, stop=kt == 3, tile_position=(0, 32 * j))
                    last.then_inc(m["pv"], 1)
                elif step[0] == "out":
                    t = step[1]
                    if t < NTB:
                        pe.wait_ge(m["ring"], ring_of(step) - NA + 1)
                    pe.wait_ge(m["norm"], KC * (t // NTB + 1))
                    for k in range(0 if t < NTB else KC - 1, KC):
                        last = nc.tensor.matmul(PS[:, out_bank(t), :], OT[:, k, t * P:t * P + P], a_wo_sb[:, k, :],
                                                start=k == 0, stop=k == KC - 1)
                    last.then_inc(m["fill"], 1)
                    if t >= NTB:
                        transposes_behind(pe, nxt, t)
                elif step[0] == "early":
                    t = step[1]
                    pe.wait_ge(m["exp"], GROUPS * GH * 2)
                    pe.wait_ge(m["norm"], 2 * KC - 1)
                    for k in range(KC - 1):
                        nc.tensor.matmul(PS[:, out_bank(t), :], OT[:, k, t * P:t * P + P], a_wo_sb[:, k, :],
                                         start=k == 0, stop=False)
                elif step[0] == "next" and nxt is not None:
                    pe.wait_ge(m["ring"], len(RING) - NTB)
                    pe.wait_ge(m["o_sb"], HEADS // 4 * BATCH)
                    transposes(pe, nxt, range(LAG))

        def attention_act(act, s, nxt):
            m, kv = am[s], KV[s]
            for step in STEPS:
                if step[0] == "proj":
                    i = step[1]
                    if i < LAG:
                        xt_copies(act, s, (NT - LAG + i,))
                    rows = kv * HD if PROJ[i][0] == "k" else P
                    act.wait_ge(m["prj_ps"], i + 1)
                    if i >= 2:
                        act.wait_ge(m["spl_out"][i % 2], DMA * (i // 2))
                    nc.scalar.copy(spl[0:rows, i % 2, 0, :], PS[0:rows, 2 + (i + 2) % 4, :]).then_inc(m["hi"], 1)
                elif step[0] == "next" and nxt is not None:
                    xt_copies(act, nxt, range(NT - LAG))
                elif step[0] == "v":
                    for n in range(2):
                        act.wait_ge(m["v_ps"], n + 1)
                        src = PS[:, 6 + n, 0:4 * kv * HD].rearrange("p (t g d) -> p t g d", t=4, g=kv)
                        for t in range(4):
                            last = nc.scalar.copy(V[:, 4 * n + t, 0:kv, 0:HD], src[:, t, :, :])
                        last.then_inc(m["v_sb"], 1)
                elif step[0] == "st":
                    u = step[1]
                    kt, pair, v = u // 2 % 4, u % 2, u // 2
                    w = SEQ - kt * P
                    act.wait_ge(m["st"], u + 1)
                    if v >= 2:
                        act.wait_ge(m["pv"], v - 1)
                    nc.scalar.activation(PT[:, v % 2, 2 * pair:2 * pair + 2, 0:w], PS[:, 2 + u % 2 * 2:4 + u % 2 * 2, 0:w],
                                         ACT.Exp, scale=SCALE).then_inc(m["exp"], 1)

        def attention_dve(dve, own, s, nxt):
            m, kv = am[s], KV[s]
            for step in STEPS:
                if step[0] == "proj":
                    i = step[1]
                    rows = kv * HD if PROJ[i][0] == "k" else P
                    dve.wait_ge(m["hi"], i + 1)
                    if i >= 2:
                        dve.wait_ge(m["lo"], i - 1)
                    nc.vector.tensor_tensor(rest[0:rows, i % 2, :], PS[0:rows, 2 + (i + 2) % 4, :], spl[0:rows, i % 2, 0, :],
                                            ALU.subtract).then_inc(m["rest"], 1)
                elif step[0] == "fill":
                    g, f = step[1:]
                    a = ring_of(step)
                    qt, h, n = FILLS[f]
                    dve.wait_ge(m["fill"], a + 1)
                    red = nc.vector.tensor_reduce(nmf[:, qt, h:h + n],
                                                  PS[:, ABANKS[a % NA], 0:n * (qt + 1) * P].rearrange("p (h n) -> p h n", h=n),
                                                  AX.X, ALU.max, negate=True)
                    red.then_inc(m["ring"], 1)
                    if f == len(FILLS) - 1:
                        dve.wait_ge(m["ring"], a + 1)
                        if g >= 1:
                            dve.wait_ge(m["fill"], ring_of(("nmt", g - 1)) + 1)
                        own.done(nc.vector.tensor_copy(nm3[:, :, 0, :], nmf[:, :, :]))
                        own.done(nc.vector.tensor_tensor(nmr[:, :, :], nmf[:, :, :], nm3[:, :, 0, :], ALU.subtract))
                        own.done(nc.vector.tensor_copy(nm3[:, :, 1, :], nmr[:, :, :]))
                        nc.vector.tensor_tensor(nm3[:, :, 2, :], nmr[:, :, :], nm3[:, :, 1, :],
                                                ALU.subtract).then_inc(m["nm3"], 1)
                        dve.wait_ge(m["nm3"], g + 1)
                elif step[0] == "nmt":
                    g = step[1]
                    a = ring_of(step)
                    dve.wait_ge(m["fill"], a + 1)
                    if g == 0:
                        dve.wait_ge(m["prj_ps"], 2)
                    if g >= 2:
                        dve.wait_ge(m["mt_in"][g % 2], DMA * 3 * (g // 2))
                    nc.vector.tensor_copy(mt[0:48, g % 2, :],
                                          PS[:, ABANKS[a % NA], :].bitcast(BF16)[0:48, 0:SEQ]).then_inc(m["ring"], 1)
                elif step[0] == "pv" and step[1] % 4 == 3:
                    i = step[1] // 4
                    dve.wait_ge(m["pv"], step[1] + 1)
                    if i >= 4:
                        dve.wait_ge(m["norm"], i // 2 - 1)
                    nc.vector.tensor_copy(o_raw[:, i % 4, :], PS[:, OB, :]).then_inc(m["o_sb"], 1)
                elif step[0] == "rden":
                    c, j = step[1:]
                    dve.wait_ge(m["o_in"][c % 2], DMA * 16 * (c // 2 + 1))
                    d = den[:, c % 2, j * P:j * P + P]
                    nc.vector.reciprocal(d, d).then_inc(m["rden"], 1)
                elif step[0] == "out":
                    t = step[1]
                    a = ring_of(step)
                    dve.wait_ge(m["fill"], a + 1)
                    nc.vector.tensor_tensor(X[:, t, :], X[:, t, :], PS[:, out_bank(t), :], ALU.add).then_inc(m["ring"], 1)
                    dve.wait_ge(m["ring"], a + 1)
                    if nxt is not None:
                        ln_stats(dve, own, nxt, t)
                        if t > NTB:
                            ln_apply(dve, nxt, t - 1)
                        if t == NT - 1:
                            ln_apply(dve, nxt, t)
                elif step[0] == "next" and nxt is not None:
                    dve.wait_ge(m["st"], GROUPS * GH * 2)
                    for t in range(NTB):
                        ln_apply(dve, nxt, t)

        def attention_pool(pool, own, s, nxt):
            m, kv = am[s], KV[s]
            if s != ATTN_A:
                pool.wait_ge(xn_ready, NT * s + NT)
            nc.gpsimd.memset(V[:, :, 0:kv, HD:2 * HD], 1.0).then_inc(m["ones"], 1)
            pool.wait_ge(m["ones"], 1)
            nc.gpsimd.memset(K6[96:99, 0:kv, :], 1.0).then_inc(m["ones"], 1)
            pool.wait_ge(m["ones"], 2)
            for step in STEPS:
                if step[0] == "proj":
                    i = step[1]
                    rows = kv * HD if PROJ[i][0] == "k" else P
                    pool.wait_ge(m["rest"], i + 1)
                    nc.gpsimd.tensor_copy(spl[0:rows, i % 2, 1, :], rest[0:rows, i % 2, :]).then_inc(m["mid"], 1)
                    pool.wait_ge(m["mid"], i + 1)
                    nc.gpsimd.tensor_tensor(spl[0:rows, i % 2, 2, :], rest[0:rows, i % 2, :], spl[0:rows, i % 2, 1, :],
                                            ALU.subtract).then_inc(m["lo"], 1)
                elif step[0] == "nmt":
                    g = step[1]
                    b, h0 = g * GH // HEADS, g * GH % HEADS
                    pool.wait_ge(m["ring"], ring_of(step) + 1)
                    for k in range(3):
                        pool.dma_start(Q6[96 + k:97 + k, h0:h0 + GH, b * SEQ:b * SEQ + SEQ],
                                     mt[GH * k:GH * k + GH, g % 2, :]).then_inc(m["mt_in"][g % 2], DMA)
                elif step[0] == "next" and nxt is not None:
                    ln_rstds(pool, own, nxt, range(NTB))
                elif step[0] == "norm":
                    c = step[1]
                    b, mm = c // KC, c % KC
                    pool.wait_ge(m["rden"], 4 * (c + 1))
                    o = OT[:, mm, b * SEQ:b * SEQ + SEQ]
                    nc.gpsimd.tensor_tensor(o, o, den[:, c % 2, :], ALU.mult).then_inc(m["norm"], 1)

        ffn_names = ["h_ps", "h_sb", "hw", "hwt_ps", "hwt_sb", "logit", "exp"]
        fm = {s: {n: sem(f"{n}{s}") for n in ffn_names} for s in (FFN_0, FFN_1)}
        Hcat = at(27648, NT * FCAT).rearrange("p (t n) -> p t n", t=NT)
        HW = at(28736, NT * ER).rearrange("p (t n) -> p t n", t=NT)
        HWT = at(29760, NT * P).rearrange("p (t n) -> p t n", t=NT)
        rt = [at(30784 + 64 * i, 64).rearrange("p (t e) -> p t e", t=NT) for i in range(8)]
        r1 = [at(31296 + 8 * i, 8) for i in range(6)]

        def last_tiles(t, ahead=LAG):
            return (t + ahead,) if t in range(NT - LAG - ahead, NT - ahead) else ()

        def ffn_pe(pe, s, nxt):
            m = fm[s]
            pe.wait_ge(w_ffn, 4 * DMA)
            for t in range(NT):
                transposes(pe, s, last_tiles(t))
                pe.wait_ge(xt_ready, NT * s + t + 1)
                if t >= 2:
                    pe.wait_ge(m["h_sb"], t - 1)
                for k in range(KC):
                    last = nc.tensor.matmul(PS[:, t % 2, 0:FCAT], XT[:, k, t * P:t * P + P], Wcat[:, k, :],
                                            start=k == 0, stop=k == KC - 1)
                last.then_inc(m["h_ps"], 1)

            def base(t):
                if t >= 4:
                    pe.wait_ge(x_done, NT * LINEAR[s] + t - 3)
                for k in range(KC):
                    nc.tensor.matmul(PS[:, 2 + t % 4, :], XT[:, k, t * P:t * P + P], Wf[:, k, :], start=k == 0, stop=False)

            base(0)
            base(1)
            for t in range(NT):
                pe.wait_ge(m["hw"], t + 1)
                if t == 0:
                    pe.wait_ge(m["h_sb"], NT)
                if t >= 2:
                    pe.wait_ge(m["hwt_sb"], t - 1)
                nc.tensor.transpose(PS[:, t % 2, 0:P], HW[:, t, :], ident[:, :]).then_inc(m["hwt_ps"], 1)
                if t + 2 < NT:
                    base(t + 2)
                pe.wait_ge(m["hwt_sb"], t + 1)
                nc.tensor.matmul(PS[:, 2 + t % 4, :], HWT[:, t, :], Wbt[:, :], start=False, stop=True).then_inc(out_ps, 1)
                transposes_behind(pe, nxt, t)

        def ffn_act(act, s, nxt):
            m = fm[s]
            for t in range(NT):
                xt_copies(act, s, last_tiles(t))
                act.wait_ge(m["h_ps"], t + 1)
                nc.scalar.copy(Hcat[:, t, :], PS[:, t % 2, 0:FCAT]).then_inc(m["h_sb"], 1)
            act.wait_ge(m["logit"], 1)
            nc.scalar.activation(rt[1], rt[0], ACT.Exp).then_inc(m["exp"], 1)
            for t in range(NT):
                act.wait_ge(m["hwt_ps"], t + 1)
                nc.scalar.copy(HWT[:, t, :], PS[:, t % 2, 0:P]).then_inc(m["hwt_sb"], 1)
                if nxt is not None and t >= LAG:
                    xt_copies(act, nxt, (t - LAG,))

        def ffn_dve(dve, own, s):
            m = fm[s]
            bc = lambda v: v.unsqueeze(2).broadcast_to([P, NT, EXPERTS])
            dve.wait_ge(m["h_sb"], NT)
            logit, e, p, c1, oh1, p2, c2, oh2 = rt
            mx, sm, m1, k1, m2, k2 = r1
            TT, TR, TS = nc.vector.tensor_tensor, nc.vector.tensor_reduce, nc.vector.tensor_scalar
            rank = rank8[:, :].unsqueeze(1).broadcast_to([P, NT, EXPERTS])
            own.done(TR(mx, Hcat[:, :, ER:FCAT], AX.X, ALU.max))
            TT(logit, Hcat[:, :, ER:FCAT], bc(mx), ALU.subtract).then_inc(m["logit"], 1)
            dve.wait_ge(m["exp"], 1)
            own.done(TR(sm, e, AX.X, ALU.add))
            own.done(nc.vector.reciprocal(sm, sm))
            own.done(TT(p, e, bc(sm), ALU.mult))
            own.done(TR(m1, p, AX.X, ALU.max))
            own.done(TT(c1, p, bc(m1), ALU.is_equal))
            own.done(TT(c1, c1, rank, ALU.mult))
            own.done(TR(k1, c1, AX.X, ALU.max))
            own.done(TT(oh1, c1, bc(k1), ALU.is_equal))
            own.done(nc.vector.scalar_tensor_tensor(p2, oh1, -2.0, p, ALU.mult, ALU.add))
            own.done(TR(m2, p2, AX.X, ALU.max))
            own.done(TT(c2, p2, bc(m2), ALU.is_equal))
            own.done(TT(c2, c2, rank, ALU.mult))
            own.done(TR(k2, c2, AX.X, ALU.max))
            own.done(TT(oh2, c2, bc(k2), ALU.is_equal))
            own.done(TT(sm, m1, m2, ALU.add))
            own.done(nc.vector.reciprocal(sm, sm))
            own.done(TT(m1, m1, sm, ALU.mult))
            own.done(TT(m2, m2, sm, ALU.mult))
            own.done(TT(oh1, oh1, bc(m1), ALU.mult))
            own.done(TT(oh2, oh2, bc(m2), ALU.mult))
            own.done(TT(oh1, oh1, oh2, ALU.add))
            for t in range(NT):
                nc.vector.tensor_tensor(HW[:, t, :].rearrange("p (e r) -> p e r", e=EXPERTS),
                                        Hcat[:, t, 0:ER].rearrange("p (e r) -> p e r", e=EXPERTS),
                                        oh1[:, t, :].unsqueeze(2).broadcast_to([P, EXPERTS, LORA]),
                                        ALU.mult).then_inc(m["hw"], 1)

        def add_outputs(dve, own, s, banks, nxt):
            for t in range(NT):
                dve.wait_ge(out_ps, NT * LINEAR[s] + t + 1)
                dve.wait_ge(x_bias, NT * LINEAR[s] + t + 1)
                nc.vector.tensor_tensor(X[:, t, :], X[:, t, :], PS[:, banks[t % len(banks)], :], ALU.add).then_inc(x_done, 1)
                dve.wait_ge(x_done, NT * LINEAR[s] + t + 1)
                if nxt is not None:
                    ln_stats(dve, own, nxt, t)
                    if t >= 1:
                        ln_apply(dve, nxt, t - 1)
            if nxt is not None:
                ln_apply(dve, nxt, NT - 1)

        qz_sb = at(17408, 256).bitcast(I32).rearrange("p (g c) -> p g c", g=4)
        zeros = at(17664, 2048).bitcast(I32).rearrange("p (g n) -> p g n", g=4)
        qw_sb = at(19712, 2048).bitcast(I32).rearrange("p (g n) -> p g n", g=4)
        sc_sb = at(21760, 2048).rearrange("p (g n) -> p g n", g=4)
        shift = sb("shift", [P, 1], I32)
        part = sb("part", [P, 1], I32)

        def quant_loads(sp):
            src = g_qw.rearrange("(g q) n -> q g n", g=4)
            for q in range(16):
                sp.dma_start(qw_sb[8 * q:8 * q + 8, :, :], src[q, :, :].partition_broadcast(8)).then_inc(w_quant, DMA)
            sp.dma_start(qz_sb, g_qz.partition_broadcast(P)).then_inc(w_quant, DMA)
            sp.dma_start(sc_sb, g_sc.partition_broadcast(P)).then_inc(w_quant, DMA)

        def dequantise(dve, own):
            dve.wait_ge(consts, CONSTS)
            own.done(nc.vector.tensor_scalar(shift[:, :], part[:, :], 7, 2, ALU.bitwise_and, ALU.logical_shift_left))
            dve.wait_ge(w_quant, 19 * DMA)
            own.done(nc.vector.tensor_scalar(qw_sb, qw_sb, shift[:, 0:1], 15, ALU.arith_shift_right, ALU.bitwise_and))
            z8 = zeros.rearrange("p g (c s) -> p g c s", s=8)
            for j in range(8):
                own.done(nc.vector.tensor_scalar(z8[:, :, :, j], qz_sb, 4 * j, 15, ALU.arith_shift_right, ALU.bitwise_and))
            own.done(nc.vector.tensor_tensor(Wg[:, :, :], qw_sb, zeros, ALU.subtract))
            nc.vector.tensor_tensor(Wg[:, :, :], Wg[:, :, :], sc_sb, ALU.mult).then_inc(wg_ready, 1)

        def quant_pe(pe, s, nxt):
            pe.wait_ge(wg_ready, 1)
            for t in range(NT):
                transposes(pe, s, last_tiles(t, NT - 1 - LAG))
                pe.wait_ge(xt_ready, NT * s + t + 1)
                if t >= 4:
                    pe.wait_ge(x_done, NT * LINEAR[s] + t - 3)
                for k in range(KC):
                    last = nc.tensor.matmul(PS[:, QUANT_BANKS[s][t % 4], :], XT[:, k, t * P:t * P + P], Wg[:, k, :],
                                            start=k == 0, stop=k == KC - 1)
                last.then_inc(out_ps, 1)
                transposes_behind(pe, nxt, t)

        QUANT_BANKS = {QUANT_0: (0, 1, 2, 3), QUANT_1: (2, 3, 4, 5)}

        def quant_act(act, s, nxt):
            for t in range(NT):
                xt_copies(act, s, last_tiles(t, NT - 1 - LAG))
                if nxt is not None and t >= LAG:
                    xt_copies(act, nxt, (t - LAG,))

        ms_names = ["par", "par2", "amin", "aexp",
                    "prj_ps", "prj_free", "th", "xs",
                    "ss_ps", "sq", "ms_ps", "rms", "sst", "bc_out",
                    "z_ps", "z_free", "ex", "w1", "r", "dtr", "ln", "dt",
                    "zero", "dA", "u", "scn", "hc", "diag", "y",
                    "tz", "yg"]
        mm_ = {n: sem(f"m_{n}") for n in ms_names}
        win_in = [sem(f"win_in{i}") for i in range(3)]
        bc_in = [sem(f"bc_in{i}") for i in range(4)]
        Wout = at(0, 4096).rearrange("p (k n) -> p k n", k=DTILES)
        Wx = at(4096, 512).rearrange("p (k n) -> p k n", k=DTILES)
        par = at(4608, 32 + 3 * 8 + 128)
        convw = par[:, 0:32].rearrange("p (i j) -> p i j", i=DTILES)
        convb, bdt, Dp = par[:, 32:40], par[:, 40:48], par[:, 48:56]
        Aneg = par[:, 56:184].rearrange("p (i n) -> p i n", i=DTILES)
        win = at(5120, 1536).rearrange("p (r k n) -> p r k n", r=3, k=KC)
        Wdt = at(6656, 1024)
        dtu = at(7680, 1024).rearrange("p (r n) -> p r n", r=2)
        tz = at(8704, 512)
        xs_, dts = [[at(9216 + 4096 * (k != b), 4096).rearrange("p (i n) -> p i n", i=DTILES) for b in range(BATCH)]
                    for k in range(2)]
        Bbc = at(17408, 8192).rearrange("p (n t) -> p n t", n=NSTATE)
        Cbc = at(25600, 8192).rearrange("p (n t) -> p n t", n=NSTATE)
        ub = [Wg[:, 2 * r:2 * r + 2, :] for r in range(2)] + \
             [at(33792 + 1024 * r, 1024).rearrange("p (n t) -> p n t", n=2) for r in range(4)]
        U = len(ub)

        def chunk_buffer(q):
            b = q // (NCH * DTILES)
            return ub[(q - b * NCH * DTILES) % U]

        TG = 4
        tmp = at(33792, 4096).rearrange("p (r k n) -> p r k n", r=TG, k=2)
        group_mean = at(4792, 64)[0:64, :]
        rms_eps = at(4856, 1)[0:64, :]
        diag = at(4860, 2 * P).rearrange("p (r n) -> p r n", r=2)
        sq, rms = at(7680, 512)[0:64, :], at(8192, 512)[0:64, :]
        ssT = at(8704, 512)[0:64, :]
        bc_dram = nc.dram_tensor("bc_dram", [BATCH, 2 * NSTATE, SEQ], F32, kind="Internal").ap()
        NCH = NSTATE // 2
        MRING = [("in", 0, i) for i in range(DTILES)]
        for b in range(BATCH):
            MRING += [("gate", b, i) for i in range(DTILES)]
            for t in range(NTB):
                MRING.append(("out", b, t))
                if b + 1 < BATCH:
                    MRING += [("in", b + 1, 2 * t), ("in", b + 1, 2 * t + 1)]

        def slot(kind, b, i):
            return MRING.index((kind, b, i))

        WIN = [x for x in MRING if x[0] in ("in", "gate")]

        def mamba_sp(sp):
            m = mm_
            sp.wait_ge(am[ATTN_A]["ring"], len(RING))
            sp.dma_start(convw, m_convw.rearrange("(i p) j -> p i j", p=P)).then_inc(m["par"], DMA)
            for dst, v in ((convb, m_convb), (bdt, m_bdt), (Dp, m_d)):
                sp.dma_start(dst, v.rearrange("(i p) -> p i", p=P), allow_slow_non_contiguous=True).then_inc(m["par"], DMA)
            sp.dma_start(Aneg, m_alog.rearrange("(i p) n -> p i n", p=P)).then_inc(m["par"], DMA)
            sp.dma_start(Wx, m_wx.rearrange("(k p) n -> p k n", p=P)).then_inc(m["par"], DMA)
            sp.dma_start(group_mean, m_group).then_inc(m["par"], DMA)
            sp.dma_start(Wout, m_wout.rearrange("(k p) n -> p k n", p=P)).then_inc(m["par"], DMA)

            def load_win(n):
                kind, b, i = WIN[n]
                j = i + (DTILES if kind == "gate" else 0)
                if n >= 3:
                    sp.wait_ge(m["prj_ps"], slot(*WIN[n - 3]) + 1)
                sp.dma_start(win[:, n % 3, :, :],
                             m_win[:, j * P:j * P + P].rearrange("(k p) n -> p k n", p=P)).then_inc(win_in[n % 3], DMA)

            for n in range(3):
                load_win(n)
            sp.dma_start(Wdt[0:DT_RANK, :], m_wdt).then_inc(m["par2"], DMA)
            for b in range(BATCH):
                for j in range(DTILES):
                    load_win(16 * b + j + 3)
                sp.wait_ge(m["sst"], b + 1)
                sp.dma_start(bc_dram[b, :, :], ssT[DT_RANK:64, :]).then_inc(m["bc_out"], DMA)
                sp.wait_ge(m["bc_out"], DMA * (b + 1))
                if b >= 1:
                    sp.wait_ge(m["hc"], NCH * DTILES * b)
                for q in range(4):
                    for k, dst in ((0, Bbc), (1, Cbc)):
                        sp.dma_start(dst[:, 4 * q:4 * q + 4, :],
                                     bc_dram[b, NSTATE * k + 4 * q:NSTATE * k + 4 * q + 4, :].partition_broadcast(P)
                                     ).then_inc(bc_in[q], DMA)
                for j in range(DTILES + 3, 2 * DTILES + 3):
                    if 16 * b + j < 32:
                        load_win(16 * b + j)

        def mamba_pe(pe, nxt):
            m = mm_
            transposes(pe, MAMBA, range(NT - LAG, NT))

            def free(R):
                if R >= 2:
                    pe.wait_ge(m["prj_free"], R - 1)
                return PS[:, 6 + R % 2, :]

            def project_step(kind, b, i, k):
                R, n = slot(kind, b, i), WIN.index((kind, b, i))
                if k == 0:
                    pe.wait_ge(win_in[n % 3], DMA * (n // 3 + 1))
                    if R < 2:
                        pe.wait_ge(xt_ready, NT * MAMBA + NT - LAG + R + 1)
                    free(R)
                last = nc.tensor.matmul(PS[:, 6 + R % 2, :], win[:, n % 3, k, :], XT[:, k, b * SEQ:b * SEQ + SEQ],
                                        start=k == 0, stop=k == KC - 1)
                if k == KC - 1:
                    last.then_inc(m["prj_ps"], 1)

            def project(kind, b, i):
                for k in range(KC):
                    project_step(kind, b, i, k)

            def state_inputs(b, i):
                if b == 0 and i == 0:
                    pe.wait_ge(m["par"], 8 * DMA)
                pe.wait_ge(m["xs"], DTILES * b + i + 1)
                last = nc.tensor.matmul(PS[0:64, 4, :], Wx[:, i, :], xs_[b][:, i, :], start=i == 0, stop=i == DTILES - 1)
                if i == DTILES - 1:
                    last.then_inc(m["ss_ps"], 1)

            def output(b, t):
                o = free(slot("out", b, t))
                for i in range(DTILES):
                    last = nc.tensor.matmul(o, xs_[b][:, i, t * P:t * P + P], Wout[:, i, :],
                                            start=i == 0, stop=i == DTILES - 1)
                last.then_inc(m["prj_ps"], 1)

            for i in range(DTILES):
                project("in", 0, i)
                if i >= 2:
                    state_inputs(0, i - 2)
            for b in range(BATCH):
                state_inputs(b, DTILES - 2)
                state_inputs(b, DTILES - 1)
                pe.wait_ge(m["sq"], b + 1)
                nc.tensor.matmul(PS[0:64, 5, :], group_mean, sq, start=True, stop=True).then_inc(m["ms_ps"], 1)
                pe.wait_ge(m["sst"], b + 1)
                pe.wait_ge(m["par2"], DMA)
                for i in range(DTILES):
                    if i >= 4:
                        pe.wait_ge(m["z_free"], b * DTILES + i - 3)
                    nc.tensor.matmul(PS[:, i % 4, :], Wdt[0:DT_RANK, i * P:i * P + P], ssT[0:DT_RANK, :],
                                     start=True, stop=True).then_inc(m["z_ps"], 1)
                for i in range(DTILES):
                    k = b * DTILES + i
                    if k >= 2:
                        pe.wait_ge(m["yg"], k - 1)
                    pe.wait_ge(m["diag"], k + 1)
                    nc.tensor.matmul(PS[:, 4 + k % 2, :], diag[:, k % 2, :], xs_[b][:, i, :], start=True, stop=False)
                    for c in range(NCH):
                        q = k * NCH + c
                        pe.wait_ge(m["hc"], q + 1)
                        for e in range(2):
                            last = nc.tensor.matmul(PS[:, 4 + k % 2, :], ident[:, :], chunk_buffer(q)[:, e, :],
                                                    start=False, stop=c == NCH - 1 and e == 1)
                        last.then_inc(m["y"], 1)
                        if c < KC:
                            project_step("gate", b, i, c)
                pe.wait_ge(m["yg"], DTILES * (b + 1))
                for t in range(NTB):
                    output(b, t)
                    if b + 1 < BATCH:
                        project("in", b + 1, 2 * t)
                        project("in", b + 1, 2 * t + 1)
                        if t:
                            state_inputs(b + 1, 2 * t - 2)
                            state_inputs(b + 1, 2 * t - 1)
                    elif nxt is not None:
                        transposes(pe, nxt, ((0, 1), (2, 3), (), (4, 5))[t])

        def mamba_act(act, own):
            m = mm_
            act.wait_ge(m["amin"], 1)
            nc.scalar.activation(Aneg, Aneg, ACT.Exp).then_inc(m["aexp"], 1)

            def skip_term(k):
                if k >= 2:
                    act.wait_ge(m["y"], NCH * (k - 1))
                i = k % DTILES
                nc.scalar.activation(diag[:, k % 2, :], ident[:, :], ACT.Identity, scale=Dp[:, i:i + 1]).then_inc(m["diag"], 1)

            act.wait_ge(m["par"], 8 * DMA)
            act.wait_ge(consts, CONSTS)
            skip_term(0)
            for b in range(BATCH):
                xs, dt_ = xs_[b], dts[b]
                for i in range(DTILES):
                    act.wait_ge(m["prj_free"], slot("in", b, i) + 1)
                    if i >= TG:
                        act.wait_ge(m["xs"], b * DTILES + i - TG + 1)
                    nc.scalar.activation(tmp[:, i % TG, 0, :], xs[:, i, :], ACT.Tanh).then_inc(m["th"], 1)
                act.wait_ge(m["ss_ps"], b + 1)
                nc.scalar.activation(sq, PS[0:64, 4, :], ACT.Square).then_inc(m["sq"], 1)
                act.wait_ge(m["ms_ps"], b + 1)
                nc.scalar.activation(rms, PS[0:64, 5, :], ACT.Sqrt, bias=rms_eps).then_inc(m["rms"], 1)
                for i0 in range(0, DTILES, TG):
                    for i in range(i0, i0 + TG):
                        act.wait_ge(m["z_ps"], b * DTILES + i + 1)
                        if i >= TG:
                            act.wait_ge(m["dt"], b * DTILES + i - TG + 1)
                        T = tmp[:, i % TG, 0, :]
                        own.done(nc.scalar.activation(T, PS[:, i % 4, :], ACT.Abs, bias=bdt[:, i:i + 1]))
                        nc.scalar.activation(T, T, ACT.Exp, scale=-1.0).then_inc(m["ex"], 1)
                    for i in range(i0, i0 + TG):
                        act.wait_ge(m["w1"], b * DTILES + i + 1)
                        act.wait_ge(m["r"], b * DTILES + i + 1)
                        nc.scalar.activation(tmp[:, i % TG, 1, :], tmp[:, i % TG, 1, :], ACT.Ln).then_inc(m["ln"], 1)
                act.wait_ge(m["dt"], b * DTILES + 1)
                act.wait_ge(m["zero"], b + 1)
                act.wait_ge(m["bc_out"], DMA * (b + 1))
                for i in range(DTILES):
                    k = b * DTILES + i
                    act.wait_ge(m["dt"], k + 1)
                    for c in range(NCH):
                        q = k * NCH + c
                        if q >= 2:
                            act.wait_ge(m["scn"], q - 1)
                        for e in range(2):
                            last = nc.scalar.activation(PS[:, q % 2 * 2 + e, 1:SEQ], dt_[:, i, 1:SEQ], ACT.Exp,
                                                        scale=Aneg[:, i, 2 * c + e:2 * c + e + 1])
                        last.then_inc(m["dA"], 1)
                        if c == 4 and k + 1 < BATCH * DTILES:
                            skip_term(k + 1)
                        if c == NCH - 1:
                            R = slot("gate", b, i)
                            act.wait_ge(m["prj_ps"], R + 1)
                            if k:
                                act.wait_ge(m["yg"], k)
                            nc.scalar.activation(tz, PS[:, 6 + R % 2, :], ACT.Tanh, scale=0.5).then_inc(m["tz"], 1)

        def mamba_pool(pool, own):
            m = mm_
            for b in range(BATCH):
                xs, dt_ = xs_[b], dts[b]
                for i in range(DTILES):
                    k = b * DTILES + i
                    if i == TG:
                        pool.wait_ge(m["dt"], b * DTILES + 1)
                        own.done(nc.gpsimd.tensor_tensor(dtu[:, 0, :], dt_[:, 0, :], xs[:, 0, :], ALU.mult))
                    pool.wait_ge(m["r"], k + 1)
                    pool.wait_ge(m["z_free"], k + 1)
                    nc.gpsimd.tensor_tensor(dt_[:, i, :], dt_[:, i, :], tmp[:, i % TG, 0, :], ALU.subtract).then_inc(m["dtr"], 1)
                for i in range(DTILES):
                    k = b * DTILES + i
                    pool.wait_ge(m["dt"], k + 1)
                    if i:
                        own.done(nc.gpsimd.tensor_tensor(dtu[:, k % 2, :], dt_[:, i, :], xs[:, i, :], ALU.mult))
                    for c in range(NCH):
                        q = k * NCH + c
                        if i == 0 and c % 2 == 0:
                            pool.wait_ge(bc_in[c // 2], 2 * DMA * (b + 1))
                        if i == 0 and c == 2:
                            pool.wait_ge(m["dt"], DTILES * (b + 1))
                        if q % (NCH * DTILES) >= U:
                            pool.wait_ge(m["y"], q - U + 1)
                        elif b and c == 0 and i == 0:
                            pool.wait_ge(m["y"], q)
                        nc.gpsimd.tensor_tensor(chunk_buffer(q), dtu[:, k % 2, :].unsqueeze(1).broadcast_to([P, 2, SEQ]),
                                                Bbc[:, 2 * c:2 * c + 2, :], ALU.mult).then_inc(m["u"], 1)

        def mamba_dve(dve, own, nxt):
            m = mm_
            TT, TS, STT = nc.vector.tensor_tensor, nc.vector.tensor_scalar, nc.vector.scalar_tensor_tensor
            dve.wait_ge(m["par"], 8 * DMA)
            own.done(nc.vector.memset(rms_eps, RMS_EPS))
            TS(Aneg, Aneg, 86.0, None, ALU.min).then_inc(m["amin"], 1)
            dve.wait_ge(m["aexp"], 1)
            own.done(TS(Aneg, Aneg, -1.0, None, ALU.mult))
            own.done(TS(par[:, 0:40], par[:, 0:40], 0.5, None, ALU.mult))
            def silu(b, i):
                dve.wait_ge(m["th"], b * DTILES + i + 1)
                STT(xs_[b][:, i, :], tmp[:, i % TG, 0, :], 1.0, xs_[b][:, i, :], ALU.add, ALU.mult).then_inc(m["xs"], 1)

            def convolution(b, i):
                xs, R = xs_[b], slot("in", b, i)
                dve.wait_ge(m["prj_ps"], R + 1)
                ps = PS[:, 6 + R % 2, :]
                own.done(TS(xs[:, i, :], ps, convw[:, i, 3:4], convb[:, i:i + 1], ALU.mult, ALU.add))
                for j in (2, 1):
                    own.done(STT(xs[:, i, 3 - j:SEQ], ps[:, 0:SEQ - 3 + j], convw[:, i, j:j + 1], xs[:, i, 3 - j:SEQ],
                                 ALU.mult, ALU.add))
                STT(xs[:, i, 3:SEQ], ps[:, 0:SEQ - 3], convw[:, i, 0:1], xs[:, i, 3:SEQ],
                    ALU.mult, ALU.add).then_inc(m["prj_free"], 1)
                if i:
                    silu(b, i - 1)

            def gated(k):
                b, i = k // DTILES, k % DTILES
                xs, R = xs_[b], slot("gate", b, i)
                dve.wait_ge(m["tz"], k + 1)
                STT(tz, tz, 1.0, PS[:, 6 + R % 2, :], ALU.add, ALU.mult).then_inc(m["prj_free"], 1)
                dve.wait_ge(m["y"], NCH * (k + 1))
                dve.wait_ge(m["prj_free"], R + 1)
                STT(xs[:, i, :], PS[:, 4 + k % 2, :], 0.5, tz, ALU.mult, ALU.mult).then_inc(m["yg"], 1)

            for i in range(DTILES):
                convolution(0, i)
            for b in range(BATCH):
                xs, dt_ = xs_[b], dts[b]
                silu(b, DTILES - 1)
                dve.wait_ge(m["rms"], b + 1)
                own.done(nc.vector.reciprocal(rms, rms))
                TT(ssT, rms, PS[0:64, 4, :], ALU.mult).then_inc(m["sst"], 1)
                for i0 in range(0, DTILES, TG):
                    for i in range(i0, i0 + TG):
                        k = b * DTILES + i
                        dve.wait_ge(m["ex"], k + 1)
                        e, w = tmp[:, i % TG, 0, :], tmp[:, i % TG, 1, :]
                        TS(w, e, 1.0, None, ALU.add).then_inc(m["w1"], 1)
                        TS(dt_[:, i, :], PS[:, i % 4, :], bdt[:, i:i + 1], 0.0, ALU.add, ALU.max).then_inc(m["z_free"], 1)
                        dve.wait_ge(m["w1"], k + 1)
                        STT(e, w, 1.0, e, ALU.subtract, ALU.subtract).then_inc(m["r"], 1)
                    if i0 + TG == DTILES:
                        dve.wait_ge(m["z_free"], DTILES * (b + 1))
                        nc.vector.memset(PS[:, 0:4, 0:1], 0.0).then_inc(m["zero"], 1)
                    for i in range(i0, i0 + TG):
                        k = b * DTILES + i
                        dve.wait_ge(m["ln"], k + 1)
                        dve.wait_ge(m["dtr"], k + 1)
                        TT(dt_[:, i, :], dt_[:, i, :], tmp[:, i % TG, 1, :], ALU.add).then_inc(m["dt"], 1)
                for i in range(DTILES):
                    k = b * DTILES + i
                    for c in range(NCH + 1):
                        q = k * NCH + c
                        if c < NCH:
                            v = chunk_buffer(q).rearrange("p n t -> p (n t)")
                            dve.wait_ge(m["dA"], q + 1)
                            dve.wait_ge(m["u"], q + 1)
                            nc.vector.tensor_tensor_scan(v, PS[:, q % 2 * 2:q % 2 * 2 + 2, :].rearrange("p n t -> p (n t)"), v,
                                                         0.0, ALU.mult, ALU.add).then_inc(m["scn"], 1)
                        if c >= 1:
                            dve.wait_ge(m["scn"], q)
                            TT(chunk_buffer(q - 1), chunk_buffer(q - 1), Cbc[:, 2 * c - 2:2 * c, :],
                               ALU.mult).then_inc(m["hc"], 1)
                        if c == 3 and i:
                            gated(k - 1)
                gated(b * DTILES + DTILES - 1)
                if b + 1 == BATCH and nxt is not None:
                    for t in range(NTB):
                        ln_apply(dve, nxt, t)
                for t in range(NTB):
                    tt = b * NTB + t
                    R = slot("out", b, t)
                    dve.wait_ge(m["prj_ps"], R + 1)
                    TT(X[:, tt, :], X[:, tt, :], PS[:, 6 + R % 2, :], ALU.add).then_inc(m["prj_free"], 1)
                    dve.wait_ge(m["prj_free"], R + 1)
                    if nxt is not None:
                        ln_stats(dve, own, nxt, tt)
                    if b + 1 < BATCH:
                        convolution(b + 1, 2 * t)
                        convolution(b + 1, 2 * t + 1)
                    elif t and nxt is not None:
                        ln_apply(dve, nxt, tt - 1)
            if nxt is not None:
                ln_apply(dve, nxt, NT - 1)

        hs_names = ["w", "zero", "prj_ps", "stg", "q_in", "k_in", "v_in", "vt", "s_ps", "sub", "ex", "rs", "p", "pt",
                    "o_ps", "ct", "ct_ps", "res"]
        hm = {n: sem(f"h_{n}") for n in hs_names}
        h_out = [sem(f"h_out{i}") for i in range(2)]
        HALF = P
        HM = 4096
        split_h = nc.dram_tensor("heads_qkv", [3, DIM, TOK], F32, kind="Internal").ap()
        QKV = [at(2 * HM * i, 2 * HM).rearrange("p (h t) -> p h t", h=HEADS) for i in range(3)]
        token_head = lambda off: at(off, HM).rearrange("p (t g) -> p t g", t=HALF)
        VG = [token_head(6 * HM), token_head(2 * HM)]
        PRT = [token_head(8 * HM), XT[:, :, :].rearrange("p k n -> p (k n)").rearrange("p (t g) -> p t g", t=HALF)]
        PR = token_head(7 * HM)
        CT = token_head(0)
        hwv, stg = at(6 * HM, 2048), at(6 * HM + 2048, 1024).rearrange("p (r n) -> p r n", r=2)
        hw = [w.rearrange("p (k n) -> p k n", k=KC) for w in (at(8 * HM, 2048), at(8 * HM + 2048, 2048), hwv)]
        hmax = at(9 * HM, HALF)
        hsum = at(9 * HM + HALF, HALF)
        hb = at(9 * HM + 2 * HALF, 3 * KC)
        BT = 512 // HEADS
        NB = HALF // BT
        HPROJ = [(i, b, mm) for i in range(3) for b in range(BATCH) for mm in range(KC)]
        NP = len(HPROJ)

        def heads_order(nxt):
            order = [("proj", i) for i in range(2 * NP // 3 + 3)]
            rest_ = [("proj", i) for i in range(2 * NP // 3 + 3, NP)]
            for e in range(NB):
                order.append(("s", e))
                if rest_:
                    order.append(rest_.pop(0))
            order += [(kind, e) for kind, n0 in (("s", NB), ("pv", 0), ("ct", 0)) for e in range(n0, n0 + NB)]
            return order + ([("next", t) for t in range(NT - LAG)] if nxt is not None else [])

        def heads_sp(sp):
            m = hm
            sp.wait_ge(am[ATTN_M]["ring"], len(RING))
            for i, w in enumerate((h_wq, h_wk, h_wv)):
                sp.dma_start(hw[i], w.rearrange("(k p) n -> p k n", p=P)).then_inc(m["w"], DMA)
            sp.dma_start(hb, h_bias).then_inc(m["w"], DMA)
            for u, (i, b, mm) in enumerate(HPROJ):
                sp.wait_ge(m["stg"], u + 1)
                sp.dma_start(split_h[i, mm * P:mm * P + P, b * SEQ:b * SEQ + SEQ], stg[:, u % 2, :]).then_inc(h_out[u % 2], DMA)
                if mm < KC - 1:
                    continue
                for par in range(2):
                    sp.wait_ge(h_out[par], DMA * (u // 2 + 1))
                if i == 2:
                    sp.wait_ge(m["zero"], 1)
                elif i == 0:
                    sp.wait_ge(xt_ready, NT * ATTN_H + NT)
                for r in (2 * b, 2 * b + 1):
                    row = 32 * r + (HD * (r % 2) if i == 2 else 0)
                    sp.dma_start(QKV[i][row:row + HD, :, :],
                                 split_h[i, :, r * 2 * HALF:(r + 1) * 2 * HALF].rearrange("(h d) t -> d h t", d=HD)
                                 ).then_inc(m[("q_in", "k_in", "v_in")[i]], DMA)

        def heads_pool(pool, own):
            m = hm
            pool.wait_ge(am[ATTN_M]["ring"], len(RING))
            nc.gpsimd.memset(QKV[2][:, :, :], 0.0).then_inc(m["zero"], 1)
            for e in range(2 * NB):
                pool.wait_ge(m["rs"], e + 1)
                sl = slice(e % NB * BT, e % NB * BT + BT)
                nc.gpsimd.tensor_tensor(PR[:, sl, :], PR[:, sl, :], hsum[:, sl].unsqueeze(2).broadcast_to([P, BT, HEADS]),
                                        ALU.mult).then_inc(m["p"], 1)

        def heads_pe(pe, nxt):
            m = hm
            pe.wait_ge(m["w"], 4 * DMA)
            for kind, u in heads_order(nxt):
                if kind == "next":
                    transposes(pe, nxt, (u,))
                elif kind == "proj":
                    i, b, mm = HPROJ[u]
                    if u < LAG:
                        transposes(pe, ATTN_H, (NT - LAG + u,))
                    pe.wait_ge(xt_ready, NT * ATTN_H + NTB * (b + 1))
                    if u >= 4:
                        pe.wait_ge(m["stg"], u - 3)
                    for k in range(KC):
                        last = nc.tensor.matmul(PS[:, u % 4, :], hw[i][:, k, mm * P:mm * P + P],
                                                XT[:, k, b * SEQ:b * SEQ + SEQ], start=k == 0, stop=k == KC - 1)
                    last.then_inc(m["prj_ps"], 1)
                elif kind == "s":
                    if u == 0:
                        pe.wait_ge(m["q_in"], 4 * DMA)
                        pe.wait_ge(m["k_in"], 4 * DMA)
                        pe.wait_ge(xt_ready, NT * ATTN_H + NT)
                    if u >= 4:
                        pe.wait_ge(m["sub"], u - 3)
                    for j in range(BT):
                        t = BT * u + j
                        for r in range(4):
                            last = nc.tensor.matmul(PS[32 * r:32 * r + 32, 4 + u % 4, j * HEADS:j * HEADS + HEADS],
                                                    QKV[0][32 * r:32 * r + HD, :, t], QKV[1][32 * r:32 * r + HD, :, t],
                                                    start=True, stop=True, tile_position=(32 * r, 32 * r))
                    last.then_inc(m["s_ps"], 1)
                elif kind == "pv":
                    if u == 0:
                        pe.wait_ge(m["stg"], NP)
                    pe.wait_ge(m["pt"], NB + u + 1)
                    pe.wait_ge(m["vt"], 4 + u * BT // 32 + 1)
                    if u >= 4:
                        pe.wait_ge(m["ct"], u - 3)
                    for j in range(BT):
                        for hf in range(2):
                            for h2 in range(2):
                                rows = slice(64 * h2, 64 * h2 + 64)
                                col = 32 * (2 * hf + h2)
                                last = nc.tensor.matmul(PS[col:col + 32, u % 4, j * HEADS:j * HEADS + HEADS],
                                                        VG[hf][rows, BT * u + j, :], PRT[hf][rows, BT * u + j, :],
                                                        start=True, stop=True, tile_position=(64 * h2, col))
                    last.then_inc(m["o_ps"], 1)
                else:
                    if u == 0:
                        pe.wait_ge(m["ct"], NB)
                        pe.wait_ge(m["sub"], 2 * NB)
                    if u >= 4:
                        pe.wait_ge(m["res"], u - 3)
                    for h in range(4 * u, 4 * u + 4):
                        last = nc.tensor.transpose(PS[:, 4 + u % 4, h % 4 * P:h % 4 * P + P], CT[:, :, h], ident[:, :])
                    last.then_inc(m["ct_ps"], 1)

        def heads_act(act, nxt):
            m = hm
            act.wait_ge(m["w"], 4 * DMA)
            for kind, u in heads_order(nxt):
                if kind == "next":
                    xt_copies(act, nxt, (u,))
                elif kind == "proj":
                    i, b, mm = HPROJ[u]
                    if u < LAG:
                        xt_copies(act, ATTN_H, (NT - LAG + u,))
                    act.wait_ge(m["prj_ps"], u + 1)
                    if u >= 2:
                        act.wait_ge(h_out[u % 2], DMA * (u // 2))
                    nc.scalar.activation(stg[:, u % 2, :], PS[:, u % 4, :], ACT.Identity,
                                         bias=hb[:, KC * i + mm:KC * i + mm + 1]).then_inc(m["stg"], 1)
                elif kind == "s":
                    act.wait_ge(m["sub"], u + 1)
                    sl = slice(u % NB * BT, u % NB * BT + BT)
                    nc.scalar.activation(PR[:, sl, :], PR[:, sl, :], ACT.Exp, scale=SCALE).then_inc(m["ex"], 1)
                elif kind == "pv":
                    act.wait_ge(m["o_ps"], u + 1)
                    if u == 0:
                        act.wait_ge(m["s_ps"], 2 * NB)
                    nc.scalar.copy(CT[:, u * BT:u * BT + BT, :], PS[:, u % 4, :].rearrange("p (t h) -> p t h", t=BT)
                                   ).then_inc(m["ct"], 1)

        def heads_dve(dve, own, nxt):
            m = hm
            TT, TR = nc.vector.tensor_tensor, nc.vector.tensor_reduce
            part_of = lambda ee: slice(ee % NB * BT, ee % NB * BT + BT)

            def v_transposed(hf, c):
                sl, t0 = slice(32 * c, 32 * c + 32), hf * HALF + 32 * c
                nc.vector.transpose(VG[hf][:, sl, :],
                                    QKV[2][:, :, t0:t0 + 32].rearrange("p h t -> p t h")).then_inc(m["vt"], 1)

            for e in range(2 * NB + 3):
                if e < 2 * NB:
                    sl = part_of(e)
                    ps = PS[:, 4 + e % 4, :].rearrange("p (t g) -> p t g", t=BT)
                    dve.wait_ge(m["s_ps"], e + 1)
                    own.done(TR(hmax[:, sl], ps, AX.X, ALU.max, negate=True))
                    if e >= NB:
                        dve.wait_ge(m["pt"], e - NB + 1)
                    TT(PR[:, sl, :], ps, hmax[:, sl].unsqueeze(2).broadcast_to([P, BT, HEADS]), ALU.add).then_inc(m["sub"], 1)
                if 1 <= e <= 2 * NB:
                    sl = part_of(e - 1)
                    dve.wait_ge(m["ex"], e)
                    own.done(TR(hsum[:, sl], PR[:, sl, :], AX.X, ALU.add))
                    nc.vector.reciprocal(hsum[:, sl], hsum[:, sl]).then_inc(m["rs"], 1)
                if e >= 3:
                    hf, sl = (e - 3) // NB, part_of(e - 3)
                    if e - 3 == 0:
                        dve.wait_ge(m["prj_ps"], 2 * NP // 3)
                    if e - 3 == NB:
                        dve.wait_ge(m["prj_ps"], NP)
                    dve.wait_ge(m["p"], e - 2)
                    nc.vector.transpose(PRT[hf][:, sl, :], PR[:, sl, :]).then_inc(m["pt"], 1)
                if e == NB + 2:
                    dve.wait_ge(m["prj_ps"], NP)
                    dve.wait_ge(h_out[0], DMA * NP // 2)
                    dve.wait_ge(h_out[1], DMA * NP // 2)
                    dve.wait_ge(m["v_in"], 4 * DMA)
                if NB + 2 <= e < NB + 6:
                    v_transposed(0, e - NB - 2)
                if e == 2 * NB - 1:
                    dve.wait_ge(m["s_ps"], 2 * NB)
                    v_transposed(1, 0)
            for c in range(1, 4):
                v_transposed(1, c)
            for u in range(NB):
                dve.wait_ge(m["ct_ps"], u + 1)
                src = PS[:, 4 + u % 4, :].rearrange("p (h f r d) -> p f r h d", h=4, f=2, r=4)
                dst = X[:, :, 64 * u:64 * u + 64].rearrange("p (r f) (h d) -> p f r h d", f=2, h=4)
                for hf in range(2):
                    last = TT(dst[:, hf], dst[:, hf], src[:, hf], ALU.add)
                last.then_inc(m["res"], 1)
            dve.wait_ge(m["res"], NB)
            if nxt is not None:
                dve.wait_ge(m["o_ps"], NB)
                for t in range(NT):
                    ln_stats(dve, own, nxt, t)
                    if t:
                        ln_apply(dve, nxt, t - 1)
                ln_apply(dve, nxt, NT - 1)

        CONSTS = 6
        block = ctx.enter_context(nc.Block())

        def attention_weights(sp, s, wq, wk, wv, wo):
            kw = wk.shape[1]
            for dst, w in ((a_wk_sb[:, :, 0:kw], wk), (a_wq_sb, wq), (a_wv_sb[:, :, 0:kw], wv), (a_wo_sb, wo)):
                sp.dma_start(dst, w.rearrange("(k p) n -> p k n", p=P)).then_inc(am[s]["w"], DMA)

        @block.sync
        def _(sp):
            x_tiles = x.rearrange("b (t p) c -> p (b t) c", p=P)
            for i in range(NT // 2):
                sp.dma_start(X[:, 2 * i:2 * i + 2, :], x_tiles[:, 2 * i:2 * i + 2, :]).then_inc(x_loaded[i], DMA)
            attention_weights(sp, ATTN_A, a_wq, a_wk, a_wv, a_wo)
            for dst, w in ((Wf[:, :, :], f_wbase), (Wcat[:, :, :], f_cat)):
                sp.dma_start(dst, w.rearrange("(k p) n -> p k n", p=P)).then_inc(w_ffn, DMA)
            sp.dma_start(Wbt[:, :], f_bt).then_inc(w_ffn, DMA)
            sp.dma_start(bias_f[:, :], f_bias.partition_broadcast(P)).then_inc(w_ffn, DMA)
            sp.dma_start(bias_g[:, :], g_bias.partition_broadcast(P)).then_inc(w_quant, DMA)
            attention_sp(sp, ATTN_A)
            mamba_sp(sp)
            sp.wait_ge(mm_["hc"], NCH * DTILES * BATCH)
            quant_loads(sp)
            sp.wait_ge(mm_["prj_free"], len(MRING))
            attention_weights(sp, ATTN_M, q_wq, q_wk, q_wv, q_wo)
            attention_sp(sp, ATTN_M)
            heads_sp(sp)
            out_tiles = out.rearrange("b (t p) c -> p (b t) c", p=P)
            for i in range(NT // 2):
                sp.wait_ge(x_done, NT * LINEAR[QUANT_1] + 2 * i + 2)
                sp.dma_start(out_tiles[:, 2 * i:2 * i + 2, :], X[:, 2 * i:2 * i + 2, :]).then_inc(stored, DMA)
            sp.wait_ge(stored, NT // 2 * DMA)

        @block.gpsimd
        def _(pool):
            own = Own(pool, pool_own)
            own.done(nc.gpsimd.memset(ident[:, :], 0.0))
            nc.gpsimd.affine_select(out=ident[:, :], in_=ident[:, :], compare_op=ALU.not_equal, fill=1.0, base=0,
                                    pattern=[[-1, P]], channel_multiplier=1).then_inc(consts, 1)
            own.done(nc.gpsimd.memset(identb[:, :], 0.0))
            nc.gpsimd.affine_select(out=identb[:, :], in_=identb[:, :], compare_op=ALU.not_equal, fill=1.0, base=0,
                                    pattern=[[-1, P]], channel_multiplier=1).then_inc(consts, 1)
            own.done(nc.gpsimd.memset(mask_qk[:, :], 0.0))
            nc.gpsimd.affine_select(out=mask_qk[:, :], in_=mask_qk[:, :], compare_op=ALU.is_ge, fill=NEG, base=0,
                                    pattern=[[-1, P]], channel_multiplier=1).then_inc(consts, 1)
            own.done(nc.gpsimd.memset(mask_kq[:, :], 0.0))
            nc.gpsimd.affine_select(out=mask_kq[:, :], in_=mask_kq[:, :], compare_op=ALU.is_ge, fill=NEG, base=0,
                                    pattern=[[1, P]], channel_multiplier=-1).then_inc(consts, 1)
            own.done(nc.gpsimd.memset(minus_half[:, :], -0.5))
            nc.gpsimd.iota(part[:, :], [[0, 1]], base=0, channel_multiplier=1).then_inc(consts, 1)
            for e in range(EXPERTS):
                own.done(nc.gpsimd.memset(rank8[:, e:e + 1], float(EXPERTS - e)))
            nc.gpsimd.memset(rank8[:, 0:1], float(EXPERTS)).then_inc(consts, 1)
            pool.wait_ge(consts, CONSTS)
            ln_rstds(pool, own, ATTN_A)
            attention_pool(pool, own, ATTN_A, FFN_0)
            ln_rstds(pool, own, FFN_0, range(NTB, NT))
            add_bias(pool, FFN_0, bias_f, w_ffn, 4 * DMA)
            ln_rstds(pool, own, MAMBA)
            mamba_pool(pool, own)
            ln_rstds(pool, own, FFN_1)
            add_bias(pool, FFN_1, bias_f, w_ffn, 4 * DMA)
            ln_rstds(pool, own, ATTN_M)
            attention_pool(pool, own, ATTN_M, QUANT_0)
            ln_rstds(pool, own, QUANT_0, range(NTB, NT))
            add_bias(pool, QUANT_0, bias_g, w_quant, 19 * DMA)
            ln_rstds(pool, own, ATTN_H)
            heads_pool(pool, own)
            ln_rstds(pool, own, QUANT_1)
            add_bias(pool, QUANT_1, bias_g, w_quant, 19 * DMA)

        @block.scalar
        def _(act):
            own = Own(act, act_own)
            xt_copies(act, ATTN_A, range(NT - LAG))
            attention_act(act, ATTN_A, FFN_0)
            ffn_act(act, FFN_0, MAMBA)
            xt_copies(act, MAMBA, range(NT - LAG, NT))
            mamba_act(act, own)
            xt_copies(act, FFN_1, range(NT - LAG))
            ffn_act(act, FFN_1, ATTN_M)
            attention_act(act, ATTN_M, QUANT_0)
            quant_act(act, QUANT_0, ATTN_H)
            heads_act(act, QUANT_1)
            quant_act(act, QUANT_1, None)

        @block.vector
        def _(dve):
            own = Own(dve, dve_own)
            layer_norm(dve, own, ATTN_A)
            attention_dve(dve, own, ATTN_A, FFN_0)
            ffn_dve(dve, own, FFN_0)
            add_outputs(dve, own, FFN_0, (2, 3, 4, 5), MAMBA)
            mamba_dve(dve, own, FFN_1)
            dequantise(dve, own)
            ffn_dve(dve, own, FFN_1)
            add_outputs(dve, own, FFN_1, (2, 3, 4, 5), ATTN_M)
            attention_dve(dve, own, ATTN_M, QUANT_0)
            add_outputs(dve, own, QUANT_0, QUANT_BANKS[QUANT_0], ATTN_H)
            heads_dve(dve, own, QUANT_1)
            add_outputs(dve, own, QUANT_1, QUANT_BANKS[QUANT_1], None)

        @block.tensor
        def _(pe):
            pe.wait_ge(consts, CONSTS)
            transposes(pe, ATTN_A, range(NT - LAG))
            attention_pe(pe, ATTN_A, FFN_0)
            ffn_pe(pe, FFN_0, MAMBA)
            mamba_pe(pe, FFN_1)
            ffn_pe(pe, FFN_1, ATTN_M)
            attention_pe(pe, ATTN_M, QUANT_0)
            quant_pe(pe, QUANT_0, ATTN_H)
            heads_pe(pe, QUANT_1)
            quant_pe(pe, QUANT_1, None)


def _laid_out(i):
    import numpy as np
    c = np.ascontiguousarray
    w = {k: np.asarray(v) for k, v in i.items()}
    group = np.repeat([0, 0, 1, 2], 16)
    same = group[:, None] == group[None, :]
    head_cols = lambda b: b.reshape(KC, P).T
    return {
        "x": w["L0_attn_a_x"],
        "a_wq": w["L0_attn_a_wq"], "a_wk": w["L0_attn_a_wk"], "a_wv": w["L0_attn_a_wv"], "a_wo": w["L0_attn_a_wo"],
        "m_win": c(w["L0_attn_b_W_in"].T), "m_convw": w["L0_attn_b_conv_w"], "m_convb": w["L0_attn_b_conv_b"],
        "m_wx": c(w["L0_attn_b_W_x"].T), "m_wdt": c(w["L0_attn_b_W_dt"].T), "m_bdt": w["L0_attn_b_b_dt"],
        "m_alog": w["L0_attn_b_A_log"], "m_d": w["L0_attn_b_D"],
        "m_group": (same / same.sum(0)).astype(np.float32), "m_wout": c(w["L0_attn_b_W_out"].T),
        "f_wbase": c(w["L0_ffn_W_base"].T),
        "f_cat": c(np.concatenate([w["L0_ffn_A"].reshape(ER, DIM), w["L0_ffn_W_gate"]], 0).T),
        "f_bias": w["L0_ffn_b_base"], "f_bt": c(w["L0_ffn_B"].transpose(0, 2, 1).reshape(ER, DIM)),
        "q_wq": w["L1_attn_a_wq"], "q_wk": w["L1_attn_a_wk"], "q_wv": w["L1_attn_a_wv"], "q_wo": w["L1_attn_a_wo"],
        "h_wq": c(w["L1_attn_b_wq"].T), "h_wk": c(w["L1_attn_b_wk"].T), "h_wv": c(w["L1_attn_b_wv"].T),
        "h_bias": c(np.stack([head_cols(w["L1_attn_b_bq"]), head_cols(w["L1_attn_b_bk"]), head_cols(w["L1_attn_b_bv"])], 1).reshape(P, 3 * KC)),
        "g_qw": w["L1_ffn_qweight"], "g_qz": w["L1_ffn_qzeros"], "g_sc": w["L1_ffn_scales"], "g_bias": w["L1_ffn_bias"],
    }


def kernel(**inputs):
    import numpy as _np
    import concourse.bacc as _bacc
    from concourse import mybir as _mybir
    from concourse.bass_utils import run_bass_kernel_spmd as _run

    nc = _bacc.Bacc("TRN2", target_bir_lowering=False, num_devices=1)
    arrays = {f"in_{k}": _np.ascontiguousarray(v) for k, v in _laid_out(inputs).items()}
    args = [nc.dram_tensor(k, a.shape, _mybir.dt.from_np(a.dtype), kind="ExternalInput").ap() for k, a in arrays.items()]
    args.append(nc.dram_tensor("out_x", (BATCH, SEQ, DIM), _mybir.dt.float32, kind="ExternalOutput").ap())
    hybrid_kernel(nc, *args)
    r = _run(nc, [arrays], core_ids=[0])
    return r.results[0]["out_x"]
```
